# Optimizing a Trainium2 kernel written in Bass

```python
import numpy as np
import jax
import jax.numpy as jnp

def _softmax(x, axis=-1):
    return jax.nn.softmax(x, axis=axis)

def _gelu(x):
    return jax.nn.gelu(x, approximate=True)

def _silu(x):
    return jax.nn.silu(x)

def _sigmoid(x):
    return jax.nn.sigmoid(x)

def _layernorm(x, axis=-1, eps=1e-05):
    m = jnp.mean(x, axis=axis, keepdims=True)
    v = jnp.var(x, axis=axis, keepdims=True)
    return (x - m) / jnp.sqrt(v + eps)

def _scatter_add(tgt, idx, src, axis=0):
    return tgt.at[idx].add(src)

def _segment_sum(src, seg, n):
    return jax.ops.segment_sum(src, seg, n)
kernel_name = 'mk_gps_d1_gnn_r32_90b7ad'

def setup_inputs(seed: int=0):
    np.random.seed(seed)
    _w = jnp.asarray

    def _rec_inputs():
        import jax
        import jax.numpy as jnp
        _gk = jax.random.key(seed)
        x = -0.0002117 + 1 * jax.random.normal(jax.random.fold_in(_gk, 1), (3125, 256), jnp.float32)
        src = jax.random.randint(jax.random.fold_in(_gk, 2), (50000,), 0, 3125, jnp.int32)
        dst = jax.random.randint(jax.random.fold_in(_gk, 3), (50000,), 0, 3125, jnp.int32)
        _o = jnp.argsort(dst, stable=True)
        src = src[_o]
        dst = dst[_o]
        return (x, src, dst)
    x, src, dst = _rec_inputs()

    def _L0_gnn_setup():
        import jax, jax.numpy as jnp
        import numpy as np
        N = 3125
        D = 256
        E = 9375
        BN_EPS = 1e-05

        def _batchnorm(x, gamma, beta):
            mean = jnp.mean(x, axis=0)
            var = jnp.var(x, axis=0)
            return (x - mean) * jax.lax.rsqrt(var + BN_EPS) * gamma + beta
        key = jax.random.key(seed)
        ks = jax.random.split(key, 8)
        h = jax.random.normal(ks[0], (N, D), dtype=jnp.float32)
        edge_index = jax.random.randint(ks[1], (2, E), 0, N, dtype=jnp.int64)
        W1 = jax.random.normal(ks[2], (D, 2 * D), dtype=jnp.float32) / np.sqrt(D)
        b1 = jnp.zeros((2 * D,), dtype=jnp.float32)
        g1 = jnp.ones((2 * D,), dtype=jnp.float32)
        bt1 = jnp.zeros((2 * D,), dtype=jnp.float32)
        W2 = jax.random.normal(ks[3], (2 * D, D), dtype=jnp.float32) / np.sqrt(2 * D)
        b2 = jnp.zeros((D,), dtype=jnp.float32)
        g2 = jnp.ones((D,), dtype=jnp.float32)
        bt2 = jnp.zeros((D,), dtype=jnp.float32)
        eps_gin = jnp.zeros((), dtype=jnp.float32)
        return {'h': h, 'edge_index': edge_index, 'W1': W1, 'b1': b1, 'g1': g1, 'bt1': bt1, 'W2': W2, 'b2': b2, 'g2': g2, 'bt2': bt2, 'eps_gin': eps_gin}
    _L0_gnn_all = _L0_gnn_setup()
    _L0_gnn_in = {k: v for k, v in _L0_gnn_all.items() if k in ('W1', 'b1', 'g1', 'bt1', 'W2', 'b2', 'g2', 'bt2', 'eps_gin')}
    del _L0_gnn_all

    def _L0_mix_setup():
        import jax, jax.numpy as jnp
        import numpy as np
        EMB, HEADS, DEPTH, SEQ, BATCH = (256, 8, 4, 256, 4)
        DH = EMB // HEADS
        FF = 4 * EMB
        EPS = 1e-05

        def _layernorm(x, g, b):
            mu = x.mean(-1, keepdims=True)
            var = ((x - mu) ** 2).mean(-1, keepdims=True)
            return (x - mu) * jax.lax.rsqrt(var + EPS) * g + b

        def _linear_attn(x, Wq, Wk, Wv, Wo, bo):
            b, n, dm = x.shape
            split = lambda t: t.reshape(b, n, HEADS, DH).transpose(0, 2, 1, 3)
            scale = DH ** (-0.25)
            q = jax.nn.softmax(split(x @ Wq) * scale, axis=-1)
            k = jax.nn.softmax(split(x @ Wk) * scale, axis=-2)
            v = split(x @ Wv)
            context = jnp.einsum('bhnd,bhne->bhde', k, v)
            out = jnp.einsum('bhnd,bhde->bhne', q, context)
            out = out.transpose(0, 2, 1, 3).reshape(b, n, dm)
            return out @ Wo + bo

        def _forward(x, Wq, Wk, Wv, Wo, bo, ln1_g, ln1_b, W1, b1, W2, b2, ln2_g, ln2_b):
            for i in range(DEPTH):
                h = _layernorm(x, ln1_g[i], ln1_b[i])
                x = x + _linear_attn(h, Wq[i], Wk[i], Wv[i], Wo[i], bo[i])
                h = _layernorm(x, ln2_g[i], ln2_b[i])
                x = x + (jax.nn.gelu(h @ W1[i] + b1[i], approximate=False) @ W2[i] + b2[i])
            return x
        key = jax.random.key(seed)
        ks = jax.random.split(key, 8)
        w = lambda k, shape: jax.random.normal(k, shape, dtype=jnp.float32) * 0.02
        D = DEPTH
        return {'x': jax.random.normal(ks[0], (BATCH, SEQ, EMB), dtype=jnp.float32), 'Wq': w(ks[1], (D, EMB, EMB)), 'Wk': w(ks[2], (D, EMB, EMB)), 'Wv': w(ks[3], (D, EMB, EMB)), 'Wo': w(ks[4], (D, EMB, EMB)), 'bo': jnp.zeros((D, EMB), jnp.float32), 'ln1_g': jnp.ones((D, EMB), jnp.float32), 'ln1_b': jnp.zeros((D, EMB), jnp.float32), 'W1': w(ks[5], (D, EMB, FF)), 'b1': jnp.zeros((D, FF), jnp.float32), 'W2': w(ks[6], (D, FF, EMB)), 'b2': jnp.zeros((D, EMB), jnp.float32), 'ln2_g': jnp.ones((D, EMB), jnp.float32), 'ln2_b': jnp.zeros((D, EMB), jnp.float32)}
    _L0_mix_all = _L0_mix_setup()
    _L0_mix_in = {k: v for k, v in _L0_mix_all.items() if k in ('Wq', 'Wk', 'Wv', 'Wo', 'bo', 'ln1_g', 'ln1_b', 'W1', 'b1', 'W2', 'b2', 'ln2_g', 'ln2_b')}
    del _L0_mix_all

    def _L0_ffn_setup():
        import jax, jax.numpy as jnp
        import numpy as np
        NUM_EXPERTS = 8
        TOP_K = 2
        B, S, D = (8, 256, 256)

        def _moe(tokens, router_w, w1, b1, w2, b2):
            N = tokens.shape[0]
            E = router_w.shape[0]
            logits = tokens.astype(jnp.float32) @ router_w.astype(jnp.float32).T
            probs = jax.nn.softmax(logits, axis=-1)
            rw, re = jax.lax.top_k(probs, TOP_K)
            if TOP_K > 1:
                rw = rw / jnp.maximum(rw.sum(-1, keepdims=True), 1e-12)
            rw = rw.astype(tokens.dtype)
            combine = jnp.zeros((N, E), tokens.dtype).at[jnp.arange(N)[:, None], re].set(rw)
            out = tokens
            for e in range(E):
                h = jax.nn.gelu(tokens @ w1[e] + b1[e], approximate=False)
                y = h @ w2[e] + b2[e]
                out = out + combine[:, e:e + 1] * y
            return out
        key = jax.random.key(seed)
        ks = jax.random.split(key, 4)
        scale = 1.0 / np.sqrt(D).astype(np.float32)
        return {'input_embeddings': jax.random.normal(ks[0], (B, S, D), jnp.float32), 'router_w': jax.random.normal(ks[1], (NUM_EXPERTS, D), jnp.float32) * scale, 'w1': jax.random.normal(ks[2], (NUM_EXPERTS, D, D), jnp.float32) * scale, 'b1': jnp.zeros((NUM_EXPERTS, D), jnp.float32), 'w2': jax.random.normal(ks[3], (NUM_EXPERTS, D, D), jnp.float32) * scale, 'b2': jnp.zeros((NUM_EXPERTS, D), jnp.float32)}
    _L0_ffn_all = _L0_ffn_setup()
    _L0_ffn_in = {k: v for k, v in _L0_ffn_all.items() if k in ('router_w', 'w1', 'b1', 'w2', 'b2')}
    del _L0_ffn_all
    return {'x': x, 'src': src, 'dst': dst, 'L0_gnn_W1': _L0_gnn_in['W1'], 'L0_gnn_b1': _L0_gnn_in['b1'], 'L0_gnn_g1': _L0_gnn_in['g1'], 'L0_gnn_bt1': _L0_gnn_in['bt1'], 'L0_gnn_W2': _L0_gnn_in['W2'], 'L0_gnn_b2': _L0_gnn_in['b2'], 'L0_gnn_g2': _L0_gnn_in['g2'], 'L0_gnn_bt2': _L0_gnn_in['bt2'], 'L0_gnn_eps_gin': _L0_gnn_in['eps_gin'], 'L0_mix_Wq': _L0_mix_in['Wq'], 'L0_mix_Wk': _L0_mix_in['Wk'], 'L0_mix_Wv': _L0_mix_in['Wv'], 'L0_mix_Wo': _L0_mix_in['Wo'], 'L0_mix_bo': _L0_mix_in['bo'], 'L0_mix_ln1_g': _L0_mix_in['ln1_g'], 'L0_mix_ln1_b': _L0_mix_in['ln1_b'], 'L0_mix_W1': _L0_mix_in['W1'], 'L0_mix_b1': _L0_mix_in['b1'], 'L0_mix_W2': _L0_mix_in['W2'], 'L0_mix_b2': _L0_mix_in['b2'], 'L0_mix_ln2_g': _L0_mix_in['ln2_g'], 'L0_mix_ln2_b': _L0_mix_in['ln2_b'], 'L0_ffn_router_w': _L0_ffn_in['router_w'], 'L0_ffn_w1': _L0_ffn_in['w1'], 'L0_ffn_b1': _L0_ffn_in['b1'], 'L0_ffn_w2': _L0_ffn_in['w2'], 'L0_ffn_b2': _L0_ffn_in['b2']}

def reference(x, src, dst, L0_gnn_W1, L0_gnn_b1, L0_gnn_g1, L0_gnn_bt1, L0_gnn_W2, L0_gnn_b2, L0_gnn_g2, L0_gnn_bt2, L0_gnn_eps_gin, L0_mix_Wq, L0_mix_Wk, L0_mix_Wv, L0_mix_Wo, L0_mix_bo, L0_mix_ln1_g, L0_mix_ln1_b, L0_mix_W1, L0_mix_b1, L0_mix_W2, L0_mix_b2, L0_mix_ln2_g, L0_mix_ln2_b, L0_ffn_router_w, L0_ffn_w1, L0_ffn_b1, L0_ffn_w2, L0_ffn_b2):
    import jax
    import jax.numpy as jnp

    def _L0_gnn_ref(h, edge_index, W1, b1, g1, bt1, W2, b2, g2, bt2, eps_gin):
        import jax, jax.numpy as jnp
        import numpy as np
        N = 3125
        D = 256
        E = 9375
        BN_EPS = 1e-05

        def _batchnorm(x, gamma, beta):
            mean = jnp.mean(x, axis=0)
            var = jnp.var(x, axis=0)
            return (x - mean) * jax.lax.rsqrt(var + BN_EPS) * gamma + beta
        src, dst = (edge_index[0], edge_index[1])
        agg = jax.ops.segment_sum(h[src], dst, num_segments=N)
        z = (1.0 + eps_gin) * h + agg
        t = jnp.dot(z, W1) + b1
        t = jax.nn.relu(_batchnorm(t, g1, bt1))
        conv_out = jnp.dot(t, W2) + b2
        out = jax.nn.relu(_batchnorm(conv_out + h, g2, bt2))
        return out

    def _L0_mix_ref(x, Wq, Wk, Wv, Wo, bo, ln1_g, ln1_b, W1, b1, W2, b2, ln2_g, ln2_b):
        import jax, jax.numpy as jnp
        import numpy as np
        EMB, HEADS, DEPTH, SEQ, BATCH = (256, 8, 4, 256, 4)
        DH = EMB // HEADS
        FF = 4 * EMB
        EPS = 1e-05

        def _layernorm(x, g, b):
            mu = x.mean(-1, keepdims=True)
            var = ((x - mu) ** 2).mean(-1, keepdims=True)
            return (x - mu) * jax.lax.rsqrt(var + EPS) * g + b

        def _linear_attn(x, Wq, Wk, Wv, Wo, bo):
            b, n, dm = x.shape
            split = lambda t: t.reshape(b, n, HEADS, DH).transpose(0, 2, 1, 3)
            scale = DH ** (-0.25)
            q = jax.nn.softmax(split(x @ Wq) * scale, axis=-1)
            k = jax.nn.softmax(split(x @ Wk) * scale, axis=-2)
            v = split(x @ Wv)
            context = jnp.einsum('bhnd,bhne->bhde', k, v)
            out = jnp.einsum('bhnd,bhde->bhne', q, context)
            out = out.transpose(0, 2, 1, 3).reshape(b, n, dm)
            return out @ Wo + bo

        def _forward(x, Wq, Wk, Wv, Wo, bo, ln1_g, ln1_b, W1, b1, W2, b2, ln2_g, ln2_b):
            for i in range(DEPTH):
                h = _layernorm(x, ln1_g[i], ln1_b[i])
                x = x + _linear_attn(h, Wq[i], Wk[i], Wv[i], Wo[i], bo[i])
                h = _layernorm(x, ln2_g[i], ln2_b[i])
                x = x + (jax.nn.gelu(h @ W1[i] + b1[i], approximate=False) @ W2[i] + b2[i])
            return x
        return _forward(x, Wq, Wk, Wv, Wo, bo, ln1_g, ln1_b, W1, b1, W2, b2, ln2_g, ln2_b)

    def _L0_ffn_ref(input_embeddings, router_w, w1, b1, w2, b2):
        import jax, jax.numpy as jnp
        import numpy as np
        NUM_EXPERTS = 8
        TOP_K = 2
        B, S, D = (8, 256, 256)

        def _moe(tokens, router_w, w1, b1, w2, b2):
            N = tokens.shape[0]
            E = router_w.shape[0]
            logits = tokens.astype(jnp.float32) @ router_w.astype(jnp.float32).T
            probs = jax.nn.softmax(logits, axis=-1)
            rw, re = jax.lax.top_k(probs, TOP_K)
            if TOP_K > 1:
                rw = rw / jnp.maximum(rw.sum(-1, keepdims=True), 1e-12)
            rw = rw.astype(tokens.dtype)
            combine = jnp.zeros((N, E), tokens.dtype).at[jnp.arange(N)[:, None], re].set(rw)
            out = tokens
            for e in range(E):
                h = jax.nn.gelu(tokens @ w1[e] + b1[e], approximate=False)
                y = h @ w2[e] + b2[e]
                out = out + combine[:, e:e + 1] * y
            return out
        b, s, d = input_embeddings.shape
        tokens = input_embeddings.reshape(b * s, d)
        return _moe(tokens, router_w, w1, b1, w2, b2).reshape(b, s, d)
    edge_index = jnp.stack([src, dst])
    xn = _layernorm(x, axis=-1)
    x = x + _L0_gnn_ref(xn, edge_index, L0_gnn_W1, L0_gnn_b1, L0_gnn_g1, L0_gnn_bt1, L0_gnn_W2, L0_gnn_b2, L0_gnn_g2, L0_gnn_bt2, L0_gnn_eps_gin) + _L0_mix_ref(xn[None], L0_mix_Wq, L0_mix_Wk, L0_mix_Wv, L0_mix_Wo, L0_mix_bo, L0_mix_ln1_g, L0_mix_ln1_b, L0_mix_W1, L0_mix_b1, L0_mix_W2, L0_mix_b2, L0_mix_ln2_g, L0_mix_ln2_b)[0]
    x = x + _L0_ffn_ref(_layernorm(x, axis=-1)[None], L0_ffn_router_w, L0_ffn_w1, L0_ffn_b1, L0_ffn_w2, L0_ffn_b2)[0]
    return x

_drawn_inputs = setup_inputs


def setup_inputs(seed=0):
    import zlib

    import numpy as np

    out = dict(_drawn_inputs(seed))
    spreads = {'L0_gnn_b1': (0.0, 2.0),
     'L0_gnn_g1': (1.0, 0.545),
     'L0_gnn_bt1': (0.0, 0.469),
     'L0_gnn_b2': (0.0, 2.0),
     'L0_gnn_g2': (1.0, 0.2),
     'L0_gnn_bt2': (0.0, 0.284),
     'L0_mix_bo': (0.0, 0.1),
     'L0_mix_ln1_g': (1.0, 0.6),
     'L0_mix_ln1_b': (0.0, 0.589),
     'L0_mix_b1': (0.0, 0.1),
     'L0_mix_b2': (0.0, 0.1),
     'L0_mix_ln2_g': (1.0, 0.6),
     'L0_mix_ln2_b': (0.0, 0.583),
     'L0_ffn_b1': (0.0, 0.559),
     'L0_ffn_b2': (0.0, 0.376)}
    factors = {'L0_mix_Wq': 8.0, 'L0_mix_Wk': 8.0, 'L0_mix_Wv': 2.934, 'L0_mix_Wo': 2.705}
    for name, (base, spread) in spreads.items():
        noise = np.random.default_rng([zlib.crc32(name.encode()), seed]).standard_normal(out[name].shape)
        drawn = base * np.exp(spread * noise) if base else spread * noise
        out[name] = jnp.asarray(drawn.astype(out[name].dtype))
    for name, factor in factors.items():
        out[name] = (out[name] * factor).astype(out[name].dtype)
    return out
```

```python
from contextlib import ExitStack

import concourse.bass as bass
from concourse import mybir

F32 = mybir.dt.float32
F16 = mybir.dt.float16
I32 = mybir.dt.int32
U32 = mybir.dt.uint32
ALU = mybir.AluOpType
ACT = mybir.ActivationFunctionType
AX = mybir.AxisListType.X
ds = bass.ds

N, D, L, E = 3125, 256, 4, 8
P = 128
TT = 125
TG = 5
GT = TT * TG
NG = N // GT
NT = N // TT
KC = D // P
FF = 4 * D
FC = FF // P
HEADS, DH = 8, 32
SCALE = DH ** -0.25
EPS = 1e-5
EDGES = 50000
ER = EDGES // TT
EG = 256
NEG_ = -(-EDGES // EG) + NT
RING = 8
NGRP = -(-NEG_ // RING) * RING
GF = 2 * D
GC = GF // P

W_UP = 64.0
K_UP = 256.0
C_DOWN = 1.0 / (W_UP * K_UP)
PARTS = ((0, 375), (375, 250))
PAIRS = ((0, 250), (250, 250), (500, 125))
PASSES = ((0, 0), (0, 1), (1, 0))

QV0, K0, WO0, WA = 0, KC * 2 * D, KC * 3 * D, 2050
W10, W20, WB = 0, KC * FF, 4100
WAS, WBS = WA // NG, WB // NG
NPRM = 16


def build(nc, a, stop=""):
    ctx = ExitStack()
    with ctx:
        def sb(name, shape, dt):
            return ctx.enter_context(nc.sbuf_tensor(name, shape, dt))

        def sem(name):
            return ctx.enter_context(nc.semaphore(name))

        X = sb("X", [TT, NT * D], F32)
        Z = sb("Z", [TT, (NT + 1) * D], F32)
        ft32 = sb("FT", [P, KC * N], F32)[:, :]
        FT = ft32.bitcast(F16).rearrange("p (s c n) -> p s c n", s=2, c=KC)
        KV = sb("KV", [P, 12800], F32)
        WAs = sb("WAs", [P, 2, WA], F16)
        wb32 = sb("WBs", [P, WB], F32)[:, :]
        hid32 = sb("HID", [P, FC * GT], F32)[:, :]
        WBs = wb32.bitcast(F16).rearrange("p (s n) -> p s n", s=2)
        HID = hid32.bitcast(F16).rearrange("p (s c n) -> p s c n", s=2, c=FC)
        H1 = sb("H1", [TT, TG, D], F32)
        QS = sb("QS", [TT, TG, D], F32)
        H2 = QS
        QN = sb("QN", [TT, TG, D], F32)
        STA = sb("STA", [P, WAS], F32)
        STB = sb("STB", [P, WBS], F32)
        BO = sb("BO", [TT, D], F32)
        B2 = sb("B2", [TT, D], F32)
        PRM = sb("PRM", [P, NPRM], F32)
        PR0 = sb("PR0", [P, 2 * KC], F32)
        IDF = sb("IDF", [P, P], F32)
        IDH = sb("IDH", [P, P], F16)
        MASK = sb("MASK", [P, P], F32)
        EPSB = sb("EPSB", [TT, 2], F32)
        EXPO = sb("EXPO", [P, 8], F32)
        QMX = sb("QMX", [TT, TG, HEADS], F32)
        QSUM = sb("QSUM", [TT, TG, HEADS], F32)
        RINV = sb("RINV", [TT, TG, HEADS], F32)
        KMX = sb("KMX", [P, KC, NG], F32)
        KM = sb("KM", [P, KC], F32)
        NKB = sb("NKB", [P, KC], F32)
        KSUM = sb("KSUM", [P, KC, NG], F32)
        RKS = sb("RKS", [P, 2, KC], F32)
        CTXA = hid32[:, 3500:3500 + KC * P].rearrange("p (c n) -> p c n", c=KC)
        CTXM = hid32[:, 3200:3200 + KC * P].rearrange("p (c n) -> p c n", c=KC)
        CTX = sb("CTX", [P, 2, KC, P], F16)
        MF = hid32[:, 2600:2600 + KC * D].rearrange("p (c n) -> p c n", c=KC)
        M = sb("M", [P, 2, KC, D], F16)

        KR = KV[:, 0:KC * N].rearrange("p (c n) -> p c n", c=KC)
        V = KV[:TT, KC * N:KC * N + NT * D].bitcast(F16).rearrange("p (s n) -> p s n", s=2)
        KE = hid32[:, 0:KC * GT].rearrange("p (c n) -> p c n", c=KC)
        KT = hid32[:TT, KC * GT:KC * GT + 2 * TG * P].bitcast(F16).rearrange(
            "p (s m j c) -> p s m j c", s=2, m=KC, j=TG)
        XIN = QS
        DSTI, DSTF = KV[:TT, 0:ER].bitcast(I32), KV[:TT, ER:2 * ER]
        JUNK = KV[:TT, 2 * ER:2 * ER + NT * ER].rearrange("p (t n) -> p t n", t=NT)
        ONES = sb("ONES", [TT, P], F32)
        CNT = sb("CNT", [TT, NT + 1], F32)
        SEG = sb("SEG", [P, NT + 1], F32)
        GRI = sb("GRI", [P, NT], I32)
        GRF = sb("GRF", [P, 5, NT + 1], F32)
        KIDI = sb("KIDI", [P, 2], I32)
        KIDX = sb("KIDX", [P, 2, 2], F32)
        GMK = sb("GMK", [P, 2, 2, NT], F32)
        LSF = sb("LSF", [P, 2, 2], F32)
        LST = sb("LST", [P, 2, 2], I32)
        LROW = sb("LROW", [1, 512], I32)
        TBI = STB[:, 0:512].bitcast(I32)
        TBF = sb("TBF", [P, 256], F32)
        IOTI = hid32[:, 0:TT].bitcast(I32)
        IOTA = sb("IOTA", [P, TT], F32)
        IDXR = sb("IDXR", [P, RING, 4], I32)
        LOC = sb("LOC", [P, RING, 2], F32)
        OH = sb("OH", [P, RING, 2, TT], F16)
        GAT = KV[:, 0:RING * 2 * D].bitcast(F16).rearrange("p (r c n) -> p r c n", r=RING, c=2)
        GPR = sb("GPR", [P, 3 * GC + 3 * KC], F32)
        GW1 = wb32[:, 0:KC * GF]
        TH = KV[:, 0:GC * N].rearrange("p (c n) -> p c n", c=GC)
        ZT = hid32[:, 0:KC * GT].rearrange("p (c n) -> p c n", c=KC)
        Y = ft32.rearrange("p (c n) -> p c n", c=KC)
        BST = wb32[:, 3640:3640 + GC * 12 * NG].rearrange("p (c n) -> p c n", c=GC)
        BMV = sb("BMV", [P, GC, 2], F32)
        BVE = sb("BVE", [P, 4, GC], F32)
        ID64 = sb("ID64", [TT, TT], F16)
        MWC = 8195
        MWS = MWC // NG
        MW = KV[:, 0:MWC].bitcast(F16).rearrange("p (s n) -> p s n", s=2)
        STM = wb32[:, KC * GF:KC * GF + MWS]
        RW = sb("RW", [P, 2, KC * E], F16)
        RWF = wb32[:, 3600:3600 + 2 * KC * E].rearrange("p (s n) -> p s n", s=2)
        EB1 = sb("EB1", [P, E * KC], F32)
        EB2 = wb32[:E, 3300:3300 + D]
        LG = Z[:, 0:NT * E].rearrange("p (t e) -> p t e", e=E)
        RT = Z[:, NT * E:9 * NT * E].rearrange("p (k t e) -> p k t e", k=8, e=E)
        RM = Z[:, 2000:2000 + 6 * NT].rearrange("p (k t) -> p k t", k=6)
        R8 = sb("R8", [TT, E], F32)
        R8I = sb("R8I", [TT, E], I32)
        CB = Z[:, 9 * NT * E:10 * NT * E].rearrange("p (t e) -> p t e", e=E)
        CBG = wb32[:TT, 3560:3560 + TG * E]
        CT = wb32[:E, 2670:2670 + GT]
        XHL = QN[:, :, :].bitcast(F16)

        FFP = ctx.enter_context(nc.psum_tensor("FFP", [P, 4, 512], F32))
        PT = ctx.enter_context(nc.psum_tensor("PT", [P, 2, 512], F32))
        TM = ctx.enter_context(nc.psum_tensor("TM", [P, 2, 512], F32))

        class Unit:
            def __init__(self, k):
                self.ST = sb(f"ST{k}", [TT, TG, 6], F32)
                self.MV = sb(f"MV{k}", [TT, TG, 2], F32)
                self.VE = sb(f"VE{k}", [TT, TG], F32)
                self.RS = sb(f"RS{k}", [TT, TG], F32)
                self.MR = sb(f"MR{k}", [TT, TG], F32)
                self.stats = sem(f"ln{k}_stats")
                self.moments = sem(f"ln{k}_moments")
                self.scales = sem(f"ln{k}_scales")
                self.h = sem(f"ln{k}_h")
                self.turned = sem(f"ln{k}_turned")
                self.hi = sem(f"ln{k}_hi")
                self.lo = sem(f"ln{k}_lo")

        UX, U1, U2, U3 = Unit("x"), Unit("1"), Unit("2"), Unit("3")

        names = """list_step bn_step x_loaded x_used xn_hl_hi xn_hl_lo xn_stored z_init consts consts0 prm0_loaded prm_loaded wa_loaded wa_used wa_split wb_loaded wb_used wb_split k_mm k_evac k_max v_hi q_max qv_mm qv_evac q_exp q_sum q_rinv q_norm q_turned q_hi q_lo kmax_all k_bias ke ke_turned kt_hi kt_lo ctx_zero ctx_mm ctx_acc ctx_lo m_mm m_lo x_bo ao_mm ao_evac x_b2 f1_mm g_hi g_lo f2_mm f2_evac eps_ready out_stored xhl_free held dst_loaded cnt cnt_mm g_list list_stored list_loaded tile_off oh_loc oh_done agg_mm agg_add gw_loaded zs z_turned zt t_mm t_evac t_stat bn_mv bn_b xhl_loaded xhl_used th_relu th_hi th_lo y_mm y_evac y_stat r_relu r_turned x1 x_in_loaded x_in_used x_plus mw_loaded mw_used mw_split rw_lo x_tok log_mm log rt comb cbg cb_turned ct cb_mm cb_add e1_mm eg_hi eg_lo e2_mm e_out""".split()
        S = {n: sem(n) for n in names}
        idx_loaded = [sem(f"idx_loaded{r}") for r in range(RING)]
        gathered = [sem(f"gathered{r}") for r in range(RING)]

        block = ctx.enter_context(nc.Block())

        def hold(engine, semaphore, value):
            engine.wait_ge(semaphore, value)
            engine.sem_inc(S["held"], 1)

        def xt(t):
            return X[:, ds(t * D, D)]

        def ft(part, k, off, w):
            return FT[:, part, k, ds(off, w)]

        @block.sync
        def _(sp):
            sp.dma_start(DSTI, a["dst"]).then_inc(S["dst_loaded"], 16)
            sp.dma_start(PR0[:, :], a["prm0"]).then_inc(S["prm0_loaded"], 16)
            sp.dma_start(EPSB[:, 0:1], a["eps"].broadcast_to([TT, 1])).then_inc(S["prm0_loaded"], 16)
            sp.sem_inc(S["xhl_free"], 1)
            with sp.Fori(0, NG) as g:
                sp.wait_ge(S["x_used"], g + 1)
                sp.dma_start(XIN[:, :, :], a["x"].rearrange("(g j p) d -> g p j d", g=NG, j=TG)[ds(g, 1)]
                             .rearrange("a p j d -> p (a j) d")).then_inc(S["x_loaded"], 16)
                sp.wait_ge(S["wa_used"], g + 1)
                sp.dma_start(STA[:, :], a["wa"][0, :, ds(g, 1), :].rearrange("p a c -> p (a c)"))\
                    .then_inc(S["wa_loaded"], 16)
                sp.wait_ge(S["xn_hl_lo"], g + 1)
                sp.dma_start(a["xn_hl"].rearrange("(g j p) d -> g p j d", g=NG, j=TG)[ds(g, 1)]
                             .rearrange("a p j d -> p (a j) d"), XHL).then_inc(S["xn_stored"], 16)
                sp.wait_ge(S["xn_stored"], 16 * g + 16)
                sp.sem_inc(S["xhl_free"], 1)
            with sp.Fori(0, L) as l:
                sp.wait_ge(U1.lo, 15 * l + 16)
                sp.dma_start(PRM[:, :], a["prm"][ds(l, 1)].rearrange("a p c -> p (a c)"))\
                    .then_inc(S["prm_loaded"], 16)
                sp.dma_start(BO[:, :], a["bo"][ds(l, 1), :].broadcast_to([TT, D])).then_inc(S["prm_loaded"], 16)
                sp.dma_start(B2[:, :], a["b2"][ds(l, 1), :].broadcast_to([TT, D])).then_inc(S["prm_loaded"], 16)
                with sp.Fori(0, NG) as g:
                    sp.wait_ge(S["wb_used"], l * NG + g + 1)
                    sp.dma_start(STB[:, :], a["wb"][ds(l, 1), :, ds(g, 1), :].rearrange("b p a c -> p (b a c)"))\
                        .then_inc(S["wb_loaded"], 16)
                with sp.Fori(0, NG) as g:
                    sp.wait_ge(S["wa_used"], l * NG + g + NG + 1)
                    sp.dma_start(STA[:, :], a["wa"][ds(l + 1, 1), :, ds(g, 1), :].rearrange("b p a c -> p (b a c)"))\
                        .then_inc(S["wa_loaded"], 16)
            sp.wait_ge(S["g_list"], 2)
            sp.dma_start(a["lists"].rearrange("(h p) w -> p h w", p=P), LST[:, :, :]).then_inc(S["list_stored"], 16)
            sp.wait_ge(S["list_stored"], 16)
            sp.dma_start(LROW[:, :], a["lists"].rearrange("(o n) w -> o (n w)", o=1)).then_inc(S["list_loaded"], 16)
            sp.dma_start(TBI, a["lists"].rearrange("(o n) w -> o (n w)", o=1).broadcast_to([P, 512])).then_inc(S["list_loaded"], 16)
            sp.wait_ge(S["list_loaded"], 32)
            with sp.Fori(0, NGRP // RING) as i:
                for r in range(RING):
                    start = sp.value_load(LROW[0:1, ds((i * RING + r) * 2, 1)], min_val=0, max_val=EDGES)
                    sp.wait_ge(S["agg_mm"], i * RING + r + 1)
                    sp.wait_ge(S["oh_done"], i * RING + r + 1)
                    sp.dma_start(IDXR[:, r, :], a["edges"][ds(start, EG), :].rearrange("(p c) w -> p (c w)", c=2))\
                        .then_inc(idx_loaded[r], 16)
            sp.wait_ge(S["f2_evac"], L * NG * TG + 1)
            sp.dma_start(GW1, a["gw1"]).then_inc(S["gw_loaded"], 16)
            sp.dma_start(GPR[:, :], a["gprm"]).then_inc(S["gw_loaded"], 16)
            sp.dma_start(RWF[:, 0, :], a["rw"]).then_inc(S["gw_loaded"], 16)
            sp.dma_start(EB1[:, :], a["eb1"]).then_inc(S["gw_loaded"], 16)
            sp.dma_start(EB2, a["eb2"]).then_inc(S["gw_loaded"], 16)
            with sp.Fori(0, NG) as g:
                sp.wait_ge(S["xhl_used"], g + 1)
                sp.dma_start(XHL, a["xn_hl"].rearrange("(g j p) d -> g p j d", g=NG, j=TG)[ds(g, 1)]
                             .rearrange("a p j d -> p (a j) d")).then_inc(S["xhl_loaded"], 16)
            with sp.Fori(0, NG) as g:
                sp.wait_ge(S["x_in_used"], g + 1)
                sp.dma_start(XIN[:, :, :], a["x"].rearrange("(g j p) d -> g p j d", g=NG, j=TG)[ds(g, 1)]
                             .rearrange("a p j d -> p (a j) d")).then_inc(S["x_in_loaded"], 16)
                sp.wait_ge(S["mw_used"], g + 1)
                sp.dma_start(STM, a["mw"][:, ds(g, 1), :].rearrange("p a c -> p (a c)")).then_inc(S["mw_loaded"], 16)
            with sp.Fori(0, NG) as g:
                sp.wait_ge(S["e_out"], g * (E * TG) + E * TG + 1)
                sp.dma_start(a["out"].rearrange("(g j p) d -> g p j d", g=NG, j=TG)[ds(g, 1)].rearrange("a p j d -> p (a j) d"),
                             X[:, ds(g * (TG * D), TG * D)].rearrange("p (j d) -> p j d", j=TG))\
                    .then_inc(S["out_stored"], 16)
            sp.wait_ge(S["out_stored"], 16 * NG)
            if stop == "mix":
                sp.wait_ge(S["f2_evac"], L * NG * TG + 1)
                sp.wait_ge(S["xn_stored"], 16 * NG)
                sp.dma_start(a["out"].rearrange("(t p) d -> p t d", t=NT), X[:, :].rearrange("p (t d) -> p t d", t=NT))\
                    .then_inc(S["out_stored"], 16)
                sp.wait_ge(S["out_stored"], 16)

        @block.gpsimd
        def _(pool):
            pool.sem_inc(S["wa_used"], 1)
            pool.sem_inc(S["wb_used"], 1)
            pool.sem_inc(S["q_norm"], 1)
            pool.sem_inc(S["x_tok"], 1)
            pool.memset(EXPO[:, :], -0.5).then_inc(S["consts0"], 1)
            pool.memset(IDF[:, :], 0.0).then_inc(S["consts0"], 1)
            pool.memset(MASK[:, :], 1.0).then_inc(S["consts0"], 1)
            pool.iota(KIDI[:, :], pattern=[[P, 2]], base=0, channel_multiplier=1).then_inc(S["consts0"], 1)
            pool.iota(IOTI, pattern=[[1, TT]], base=0, channel_multiplier=0).then_inc(S["consts0"], 1)
            pool.iota(R8I[:, :], pattern=[[-1, E]], base=E, channel_multiplier=0).then_inc(S["consts0"], 1)
            pool.wait_ge(S["consts0"], 6)
            pool.affine_select(out=IDF[:, :], in_=IDF[:, :], compare_op=ALU.not_equal, fill=1.0, base=0,
                               pattern=[[-1, P]], channel_multiplier=1).then_inc(S["consts0"], 1)
            heads = MASK[:, :].rearrange("p (b c) -> p b c", c=DH)
            pool.affine_select(out=heads, in_=heads, compare_op=ALU.is_ge, fill=0.0, base=0,
                               pattern=[[-DH, P // DH], [0, DH]], channel_multiplier=1).then_inc(S["consts0"], 1)
            pool.wait_ge(S["consts0"], 8)
            pool.affine_select(out=heads, in_=heads, compare_op=ALU.is_ge, fill=0.0, base=DH - 1,
                               pattern=[[DH, P // DH], [0, DH]], channel_multiplier=-1).then_inc(S["consts"], 1)
            pool.tensor_copy(IDH[:, :], IDF[:, :]).then_inc(S["consts"], 1)
            pool.tensor_copy(KIDX[:, 0, :], KIDI[:, :]).then_inc(S["consts"], 1)
            pool.tensor_copy(IOTA[:, :], IOTI).then_inc(S["consts"], 1)
            pool.tensor_copy(R8[:, :], R8I[:, :]).then_inc(S["consts"], 1)
            pool.memset(Z[:, NT * D:(NT + 1) * D], 0.0).then_inc(S["consts"], 1)
            pool.memset(ONES[:, :], 1.0).then_inc(S["consts"], 1)
            pool.memset(CNT[:, 0:1], 0.0).then_inc(S["consts"], 1)
            pool.memset(CNT[:, NT:NT + 1], float(ER)).then_inc(S["consts"], 1)
            pool.tensor_scalar(ID64[:, :], IDF[:TT, :TT], W_UP, 0.0, ALU.mult, ALU.add).then_inc(S["consts"], 1)

            def rstd(U, u):
                hold(pool, U.moments, (u + 1) * TG)
                pool.tensor_scalar(U.VE[:, :], U.MV[:, :, 1], 1.0, EPS, ALU.mult, ALU.add).then_inc(U.scales, 1)
                pool.wait_ge(U.scales, 3 * u + 1)
                pool.tensor_tensor(U.RS[:, :], U.VE[:, :], EXPO[:TT, 0:TG], ALU.pow).then_inc(U.scales, 1)
                pool.wait_ge(U.scales, 3 * u + 2)
                pool.tensor_tensor(U.MR[:, :], U.MV[:, :, 0], U.RS[:, :], ALU.mult).then_inc(U.scales, 1)

            def split_a(i, g):
                hold(pool, S["wa_loaded"], 16 * (i + 1))
                pool.tensor_scalar(STA[:, :], STA[:, :], W_UP, 0.0, ALU.mult, ALU.add).then_inc(S["wa_split"], 1)
                hold(pool, S["wa_split"], 3 * i + 1)
                pool.tensor_copy(WAs[:, 0, ds(g * WAS, WAS)], STA[:, :]).then_inc(S["wa_split"], 1)
                pool.wait_ge(S["wa_split"], 3 * i + 2)
                pool.tensor_tensor(WAs[:, 1, ds(g * WAS, WAS)], STA[:, :], WAs[:, 0, ds(g * WAS, WAS)],
                                   ALU.subtract).then_inc(S["wa_split"], 1)
                hold(pool, S["wa_split"], 3 * i + 3)
                pool.sem_inc(S["wa_used"], 1)

            def split_b(i, g):
                hold(pool, S["wb_loaded"], 16 * (i + 1))
                pool.tensor_scalar(STB[:, :], STB[:, :], W_UP, 0.0, ALU.mult, ALU.add).then_inc(S["wb_split"], 1)
                hold(pool, S["wb_split"], 3 * i + 1)
                pool.tensor_copy(WBs[:, 0, ds(g * WBS, WBS)], STB[:, :]).then_inc(S["wb_split"], 1)
                pool.wait_ge(S["wb_split"], 3 * i + 2)
                pool.tensor_tensor(WBs[:, 1, ds(g * WBS, WBS)], STB[:, :], WBs[:, 0, ds(g * WBS, WBS)],
                                   ALU.subtract).then_inc(S["wb_split"], 1)
                hold(pool, S["wb_split"], 3 * i + 3)
                pool.sem_inc(S["wb_used"], 1)

            with pool.Fori(0, NG) as g:
                rstd(UX, g)
                rstd(U1, g)
                split_a(g, g)

            with pool.Fori(0, L) as l:
                hold(pool, S["prm_loaded"], 48 * l + 48)
                with pool.Fori(0, NG) as g:
                    n = l * NG + g
                    pool.wait_ge(U1.h, (n + 1) * TG)
                    pool.tensor_tensor(X[:, ds(g * TG * D, TG * D)].rearrange("p (j d) -> p j d", j=TG),
                                       X[:, ds(g * TG * D, TG * D)].rearrange("p (j d) -> p j d", j=TG),
                                       BO[:, :].unsqueeze(1).to_broadcast([TT, TG, D]), ALU.add)\
                        .then_inc(S["x_bo"], 1)
                    pool.wait_ge(S["q_turned"], n * 3 + 1)
                    for j in range(TG):
                        pool.wait_ge(S["q_rinv"], n * TG + j + 1)
                        pool.tensor_tensor(QN[:, j, :].rearrange("p (h c) -> p h c", h=HEADS),
                                           QS[:, j, :].rearrange("p (h c) -> p h c", h=HEADS),
                                           RINV[:, j, :].unsqueeze(2).to_broadcast([TT, HEADS, DH]), ALU.mult)\
                            .then_inc(S["q_norm"], 1)
                    pool.wait_ge(S["f2_evac"], l * NG * TG + 1)
                    split_b(n, g)
                rstd(U2, l * NG)
                hold(pool, S["m_mm"], l + 1)
                def x_plus_b2(n, g):
                    pool.wait_ge(U2.h, (n + 1) * TG)
                    pool.tensor_tensor(X[:, ds(g * TG * D, TG * D)].rearrange("p (j d) -> p j d", j=TG),
                                       X[:, ds(g * TG * D, TG * D)].rearrange("p (j d) -> p j d", j=TG),
                                       B2[:, :].unsqueeze(1).to_broadcast([TT, TG, D]), ALU.add)\
                        .then_inc(S["x_b2"], 1)

                with pool.Fori(0, NG - 1) as g:
                    n = l * NG + g
                    x_plus_b2(n, g)
                    split_a(n + NG, g)
                    rstd(U2, n + 1)
                    rstd(U1, n + NG)
                x_plus_b2(l * NG + NG - 1, NG - 1)
                split_a(l * NG + 2 * NG - 1, NG - 1)
                rstd(U1, l * NG + 2 * NG - 1)

            hold(pool, S["xn_stored"], 16 * NG)
            with pool.Fori(0, NGRP // RING) as i:
                for r in range(RING):
                    pool.wait_ge(idx_loaded[r], 16 * i + 16)
                    hold(pool, S["agg_mm"], i * RING + r + 1)
                    for c in range(2):
                        pool.indirect_dma_start(
                            out=GAT[:, r, c, :], out_offset=None, in_=a["xn_hl"],
                            in_offset=bass.IndirectOffsetOnAxis(ap=IDXR[:, r, 2 * c:2 * c + 1].bitcast(U32), axis=0))\
                            .then_inc(gathered[r], 16)

            def bn_scales(i, chunks, g0, b0):
                pool.wait_ge(S["bn_mv"], (GC, GC + KC)[i])
                pool.tensor_scalar(BVE[:, 0, :chunks], BMV[:, :chunks, 1], 1.0, EPS, ALU.mult, ALU.add).then_inc(S["bn_step"], 1)
                pool.wait_ge(S["bn_step"], 4 * i + 1)
                pool.tensor_tensor(BVE[:, 1, :chunks], BVE[:, 0, :chunks], EXPO[:, :chunks], ALU.pow).then_inc(S["bn_step"], 1)
                pool.wait_ge(S["bn_step"], 4 * i + 2)
                pool.tensor_tensor(BVE[:, 2, :chunks], BVE[:, 1, :chunks], GPR[:, g0:g0 + chunks], ALU.mult).then_inc(S["bn_step"], 1)
                pool.wait_ge(S["bn_step"], 4 * i + 3)
                pool.tensor_tensor(BVE[:, 0, :chunks], BVE[:, 2, :chunks], BMV[:, :chunks, 0], ALU.mult).then_inc(S["bn_step"], 1)
                pool.wait_ge(S["bn_step"], 4 * i + 4)
                pool.tensor_tensor(BVE[:, 3, :chunks], GPR[:, b0:b0 + chunks], BVE[:, 0, :chunks], ALU.subtract).then_inc(S["bn_b"], 1)

            pool.wait_ge(S["gw_loaded"], 80)
            pool.tensor_scalar(RWF[:, 1, :], RWF[:, 0, :], W_UP, 0.0, ALU.mult, ALU.add).then_inc(S["rw_lo"], 1)
            pool.wait_ge(S["rw_lo"], 1)
            pool.tensor_copy(RW[:, 0, :], RWF[:, 1, :]).then_inc(S["rw_lo"], 1)
            pool.wait_ge(S["rw_lo"], 2)
            pool.tensor_tensor(RW[:, 1, :], RWF[:, 1, :], RW[:, 0, :], ALU.subtract).then_inc(S["rw_lo"], 1)
            bn_scales(0, GC, GC, 2 * GC)
            bn_scales(1, KC, 3 * GC + KC, 3 * GC + 2 * KC)
            pool.sem_inc(S["x_in_used"], 1)
            pool.sem_inc(S["mw_used"], 1)
            with pool.Fori(0, NG) as g:
                xg = X[:, ds(g * TG * D, TG * D)].rearrange("p (j d) -> p j d", j=TG)
                pool.wait_ge(S["x_in_loaded"], 16 * g + 16)
                pool.tensor_tensor(xg, xg, XIN[:, :, :], ALU.add).then_inc(S["x_plus"], 1)
                hold(pool, S["x_plus"], g + 1)
                pool.sem_inc(S["x_in_used"], 1)
                hold(pool, S["mw_loaded"], 16 * g + 16)
                pool.tensor_scalar(STM, STM, W_UP, 0.0, ALU.mult, ALU.add).then_inc(S["mw_split"], 1)
                hold(pool, S["mw_split"], 3 * g + 1)
                pool.tensor_copy(MW[:, 0, ds(g * MWS, MWS)], STM).then_inc(S["mw_split"], 1)
                pool.wait_ge(S["mw_split"], 3 * g + 2)
                pool.tensor_tensor(MW[:, 1, ds(g * MWS, MWS)], STM, MW[:, 0, ds(g * MWS, MWS)],
                                   ALU.subtract).then_inc(S["mw_split"], 1)
                hold(pool, S["mw_split"], 3 * g + 3)
                pool.sem_inc(S["mw_used"], 1)
            with pool.Fori(0, NG) as g:
                rstd(U3, g)
                xg = X[:, ds(g * TG * D, TG * D)].rearrange("p (j d) -> p j d", j=TG)
                pool.wait_ge(U3.h, (g + 1) * TG)
                pool.tensor_tensor(xg, xg, H1[:, :, :], ALU.add).then_inc(S["x_tok"], 1)

        @block.tensor
        def _(pe):
            pe.sem_inc(S["q_turned"], 1)
            pe.sem_inc(S["ke_turned"], 2)
            pe.sem_inc(S["ctx_mm"], 2)
            for c in ("y_mm", "cb_mm"):
                pe.sem_inc(S[c], 1)
            pe.sem_inc(S["r_turned"], 1)
            pe.sem_inc(S["z_turned"], 1)
            pe.sem_inc(S["agg_mm"], RING)
            for U in (U1, U2, U3):
                pe.sem_inc(U.turned, 1)

            def turn(U, u, H, free):
                for i, (off, w) in enumerate(PAIRS):
                    pe.wait_ge(U.h, u * TG + (2 * i + 2 if i < 2 else TG))
                    if i in free:
                        pe.wait_ge(*free[i])
                    for t in range(w // TT):
                        for c in range(KC):
                            last = pe.transpose(PT[:, i % 2, c * 250 + t * TT:c * 250 + (t + 1) * TT],
                                                H[:, 2 * i + t, c * P:(c + 1) * P], IDF[:TT, :TT])
                    last.then_inc(U.turned, 1)

            def mm3(out, lhs, rhs, chunks):
                for k in range(chunks):
                    for s, (x, y) in enumerate(PASSES):
                        last = pe.matmul(out, lhs(x, k), rhs(y, k), start=(k == 0 and s == 0),
                                         stop=(k == chunks - 1 and s == len(PASSES) - 1))
                return last

            pe.wait_ge(S["consts"], 10)
            with pe.Fori(0, NG) as g:
                turn(U1, g, H1, {0: (U1.lo, g * 3 + 1), 2: (U1.lo, g * 3 + 2)})

            pe.wait_ge(S["cnt"], NT - 1)
            pe.matmul(TM[:, 0, 0:NT + 1], ONES[:, :], CNT[:, :], start=True, stop=True).then_inc(S["cnt_mm"], 1)
            pe.wait_ge(S["list_step"], 2)

            def k_product(l, g, n):
                pe.wait_ge(U1.lo, 3 * n + 4)
                pe.wait_ge(S["k_evac"], 4 * n + 1)
                for m in range(KC):
                    for p, (off, w) in enumerate(PARTS):
                        mm3(FFP[:, 2 * m + p, :w],
                            lambda x, k: WAs[:, x, K0 + k * D + m * P:K0 + k * D + (m + 1) * P],
                            lambda y, k: ft(y, k, g * GT + off, w), KC).then_inc(S["k_mm"], 1)

            def qv_product(l, g, n):
                for j in range(TG):
                    if j != 1:
                        pe.wait_ge(S["qv_evac"], n * TG + 1 + (j - 1 if j else 0))
                    mm3(TM[:TT, j % 2, :], lambda x, k: ft(x, k, g * GT + j * TT, TT),
                        lambda y, k: WAs[:, y, QV0 + k * 2 * D:QV0 + (k + 1) * 2 * D], KC).then_inc(S["qv_mm"], 1)

            def turn_q(n):
                for i, (off, w) in enumerate(PAIRS):
                    pe.wait_ge(S["q_norm"], n * TG + (2 * i + 2 if i < 2 else TG) + 1)
                    if i != 1:
                        pe.wait_ge(S["q_lo"], n * 3 + 1 + (1 if i else 0))
                    for t in range(w // TT):
                        for c in range(KC):
                            last = pe.transpose(PT[:, i % 2, c * 250 + t * TT:c * 250 + (t + 1) * TT],
                                                QN[:, 2 * i + t, c * P:(c + 1) * P], IDF[:TT, :TT])
                    last.then_inc(S["q_turned"], 1)

            def attention_out(g0, g, n):
                for j in range(TG):
                    if j == 0:
                        if g is not None:
                            pe.wait_ge(S["f2_evac"], (n - 1) * TG + 1)
                        pe.wait_ge(S["q_lo"], 3 * n + 4)
                    if j > 1:
                        pe.wait_ge(S["ao_evac"], n * TG + j)
                    mm3(TM[:TT, j % 2, :D], lambda x, k: ft(x, k, g0 * GT + j * TT, TT),
                        lambda y, k: M[:, y, k, :], KC).then_inc(S["ao_mm"], 1)

            def ff1(l, g, n):
                pe.wait_ge(U2.lo, 3 * n + 4)
                for m in range(FC):
                    if m >= 2:
                        pe.wait_ge(S["g_lo"], 16 * n + 2 * m - 2 + 1)
                    for p, (off, w) in enumerate(PARTS):
                        mm3(FFP[:, 2 * (m % 2) + p, :w],
                            lambda x, k: WBs[:, x, W10 + k * FF + m * P:W10 + k * FF + (m + 1) * P],
                            lambda y, k: ft(y, k, g * GT + off, w), KC).then_inc(S["f1_mm"], 1)

            def ff2(n, tiles, other):
                for j in tiles:
                    if j == 0:
                        pe.wait_ge(S["g_lo"], 16 * n + 17)
                        pe.wait_ge(*other)
                    elif j > 1:
                        pe.wait_ge(S["f2_evac"], n * TG + j)
                    mm3(TM[:TT, j % 2, :D], lambda x, k: HID[:, x, k, j * TT:(j + 1) * TT],
                        lambda y, k: WBs[:, y, W20 + k * D:W20 + (k + 1) * D], FC).then_inc(S["f2_mm"], 1)

            with pe.Fori(0, L) as l:
                pe.wait_ge(S["wa_split"], 3 * (l * NG + NG))
                pe.wait_ge(S["f2_evac"], l * NG * TG + 1)
                k_product(l, 0, l * NG)
                qv_product(l, 0, l * NG)
                with pe.Fori(1, NG) as g:
                    n = l * NG + g
                    k_product(l, g, n)
                    turn_q(n - 1)
                    qv_product(l, g, n)
                turn_q(l * NG + NG - 1)
                with pe.Fori(0, NG) as g:
                    b = (l * NG + g) * KC
                    for m in range(KC):
                        pe.wait_ge(S["ke"], b + m + 1)
                        pe.wait_ge(S["kt_lo"], b + m + 1)
                        bank = (PT, FFP)[m]
                        for j in range(TG):
                            last = pe.transpose(bank[:TT, j // 4, (j % 4) * P:(j % 4 + 1) * P],
                                                KE[:, m, j * TT:(j + 1) * TT], IDF[:, :])
                        last.then_inc(S["ke_turned"], 1)
                    for m in range(KC):
                        pe.wait_ge(S["kt_lo"], b + m + 3)
                        pe.wait_ge(S["ctx_acc"], b + m + 1)
                        for j in range(TG):
                            for s, (x, y) in enumerate(PASSES):
                                last = pe.matmul(TM[:, m, :P], V[:, x, ds(g * (TG * D) + (j * D + m * P), P)],
                                                 KT[:, y, m, j, :], start=(j == 0 and s == 0),
                                                 stop=(j == TG - 1 and s == 2))
                        last.then_inc(S["ctx_mm"], 1)
                pe.wait_ge(S["ctx_lo"], 3 * l + 3)
                for m in range(KC):
                    for s, (x, y) in enumerate(PASSES):
                        last = pe.matmul(FFP[:, 0, m * D:(m + 1) * D], CTX[:, x, m, :],
                                         WAs[:, y, WO0 + m * D:WO0 + (m + 1) * D], start=(s == 0), stop=(s == 2))
                last.then_inc(S["m_mm"], 1)
                pe.wait_ge(S["m_lo"], 6 * l + 6)
                pe.wait_ge(S["wb_split"], 3 * (l * NG + NG))
                n0 = l * NG
                attention_out(0, None, n0)
                turn(U2, n0, H2, {0: (U1.lo, 3 * (n0 + NG) + 1), 2: (U2.lo, 3 * n0 + 2)})
                ff1(l, 0, n0)
                attention_out(1, 1, n0 + 1)
                ff2(n0, (0, 1), (S["ao_evac"], (n0 + 2) * TG + 1))
                turn(U2, n0 + 1, H2, {0: (U2.lo, 3 * (n0 + 1) + 1), 2: (U2.lo, 3 * (n0 + 1) + 2)})
                ff2(n0, (2, 3, 4), None)
                with pe.Fori(1, NG - 1) as g:
                    n = l * NG + g
                    ff1(l, g, n)
                    attention_out(g + 1, g + 1, n + 1)
                    turn(U1, n + NG - 1, H1, {0: (U2.lo, 3 * (n + 1) + 1), 2: (U1.lo, 3 * (n + NG - 1) + 2)})
                    ff2(n, (0, 1), (S["ao_evac"], (n + 2) * TG + 1))
                    turn(U2, n + 1, H2, {0: (U1.lo, 3 * (n + NG) + 1), 2: (U2.lo, 3 * (n + 1) + 2)})
                    ff2(n, (2, 3, 4), None)
                n4 = n0 + NG - 1
                ff1(l, NG - 1, n4)
                turn(U1, n4 + NG - 1, H1, {0: (U2.lo, 3 * (n4 + 1) + 1), 2: (U1.lo, 3 * (n4 + NG - 1) + 2)})
                ff2(n4, (0, 1, 2, 3, 4), (S["f2_evac"], n4 * TG + 1))
                turn(U1, n4 + NG, H1, {0: (U1.lo, 3 * (n4 + NG) + 1), 2: (U1.lo, 3 * (n4 + NG) + 2)})

            with pe.Fori(0, NGRP // RING) as i:
                for r in range(RING):
                    pe.wait_ge(S["oh_done"], i * RING + r + RING + 1)
                    pe.wait_ge(gathered[r], 32 * i + 32)
                    pe.wait_ge(S["agg_add"], i * RING + r + 1)
                    for c in range(2):
                        for s in range(2):
                            last = pe.matmul(TM[:TT, r % 2, :D], OH[:, r, c, :], GAT[:, r, c, s * D:(s + 1) * D],
                                             start=(c == 0 and s == 0), stop=(c == 1 and s == 1))
                    last.then_inc(S["agg_mm"], 1)
            pe.wait_ge(S["gw_loaded"], 80)
            with pe.Fori(0, NG) as g:
                for i, (off, w) in enumerate(PAIRS):
                    pe.wait_ge(S["zs"], g + 1)
                    pe.wait_ge(S["zt"], 3 * g + 1 + (1 if i == 2 else 0))
                    for t in range(w // TT):
                        for c in range(KC):
                            last = pe.transpose(PT[:, i % 2, c * 250 + t * TT:c * 250 + (t + 1) * TT],
                                                H1[:, 2 * i + t, c * P:(c + 1) * P], IDF[:TT, :TT])
                    last.then_inc(S["z_turned"], 1)
                pe.wait_ge(S["zt"], 3 * g + 4)
                for m in range(GC):
                    for p, (off, w) in enumerate(PARTS):
                        pe.wait_ge(S["t_evac"], 8 * g + 2 * m + p + 1)
                        for k in range(KC):
                            last = pe.matmul(FFP[:, 2 * (m % 2) + p, :w], GW1[:, k * GF + m * P:k * GF + (m + 1) * P],
                                             ZT[:, k, off:off + w], start=(k == 0), stop=(k == KC - 1))
                        last.then_inc(S["t_mm"], 1)
            pe.wait_ge(S["wa_split"], 3 * (L + 1) * NG)
            with pe.Fori(0, NG) as g:
                pe.wait_ge(S["th_lo"], g * GC + GC)
                pe.wait_ge(S["xhl_loaded"], 16 * g + 16)
                for m in range(KC):
                    for p, (off, w) in enumerate(PARTS):
                        pe.wait_ge(S["y_evac"], 4 * g + 2 * m + p + 1)
                        out = FFP[:, 2 * m + p, :w]
                        for k in range(GC):
                            for s, (x, y) in enumerate(PASSES):
                                pe.matmul(out, WAs[:, x, k * D + m * P:k * D + (m + 1) * P], HID[:, y, k, off:off + w],
                                          start=(k == 0 and s == 0), stop=False, skip_group_check=True)
                        tiles = range(off // TT, (off + w) // TT)
                        for j in tiles:
                            for s in range(2):
                                last = pe.matmul(FFP[:, 2 * m + p, j * TT - off:(j + 1) * TT - off],
                                                 XHL[:, j, s * D + m * P:s * D + (m + 1) * P], ID64[:, :],
                                                 start=False, stop=(j == tiles[-1] and s == 1), skip_group_check=True)
                        last.then_inc(S["y_mm"], 1)
            with pe.Fori(0, NG) as g:
                pe.wait_ge(S["r_relu"], KC * (g + 1))
                for j in range(TG):
                    if j != 1:
                        pe.wait_ge(S["x1"], g * TG + (j if j else 1))
                    for c in range(KC):
                        last = pe.transpose(TM[:TT, j % 2, c * P:(c + 1) * P], ZT[:, c, j * TT:(j + 1) * TT], IDF[:, :])
                    last.then_inc(S["r_turned"], 1)
            pe.wait_ge(S["rw_lo"], 3)
            with pe.Fori(0, NG) as g:
                turn(U3, g, H1, {0: (U3.lo, 3 * g + 1), 2: (U3.lo, 3 * g + 2)})
                pe.wait_ge(U3.lo, 3 * g + 4)
                pe.wait_ge(S["log"], g + 1)
                for j in range(TG):
                    last = mm3(TM[:TT, 0, j * E:(j + 1) * E], lambda x, k: ft(x, k, g * GT + j * TT, TT),
                               lambda y, k: RW[:, y, k * E:(k + 1) * E], KC)
                last.then_inc(S["log_mm"], 1)
            with pe.Fori(0, NG) as g:
                pe.wait_ge(S["cbg"], g + 1)
                pe.wait_ge(S["ct"], 2 * g + 1)
                for j in range(TG):
                    last = pe.transpose(PT[:E, j // 4, (j % 4) * TT:(j % 4 + 1) * TT], CBG[:, j * E:(j + 1) * E], IDF[:TT, :TT])
                last.then_inc(S["cb_turned"], 1)
                pe.wait_ge(S["ct"], 2 * g + 3)
                for j in range(TG):
                    if j != 1:
                        pe.wait_ge(S["cb_add"], g * TG + (j if j else 1))
                    pe.matmul(TM[:TT, j % 2, :D], CT[:, j * TT:(j + 1) * TT], EB2, start=True, stop=True)\
                        .then_inc(S["cb_mm"], 1)
            pe.wait_ge(S["mw_split"], 3 * NG)
            pe.wait_ge(S["cb_add"], NT + 1)
            with pe.Fori(0, NG) as g:
                with pe.Fori(0, E // 2) as h:
                    for q in range(2):
                        e, x = h * 2 + q, g * E + h * 2 + q
                        for m in range(KC):
                            pe.wait_ge(S["eg_lo"], 4 * x + 2 * m + 2)
                            for p, (off, w) in enumerate(PARTS):
                                mm3(FFP[:, 2 * m + p, :w],
                                    lambda s, k: MW[:, s, ds(e * (4 * D) + (k * D + m * P), P)],
                                    lambda s, k: ft(s, k, g * GT + off, w), KC).then_inc(S["e1_mm"], 1)
                    for q in range(2):
                        e, x = h * 2 + q, g * E + h * 2 + q
                        pe.wait_ge(S["eg_lo"], 4 * x + 4 + 4)
                        for j in range(TG):
                            if j != 1:
                                pe.wait_ge(S["e_out"], x * TG + (j if j else 1))
                            mm3(TM[:TT, j % 2, :D], lambda s, k: HID[:, s, 2 * q + k, j * TT:(j + 1) * TT],
                                lambda s, k: MW[:, s, ds(e * (4 * D) + (2 * D + k * D), D)], KC).then_inc(S["e2_mm"], 1)

        @block.scalar
        def _(act):
            act.sem_inc(S["k_evac"], 1)

            def ln_hi(U, u, g, scale, bias):
                for i, (off, w) in enumerate(PAIRS):
                    act.wait_ge(U.turned, 3 * u + i + 2)
                    for c in range(KC):
                        ps = PT[:, i % 2, c * 250:c * 250 + w]
                        act.activation(ft(0, c, g * GT + off, w), ps, ACT.Identity,
                                       bias=bias[:, c:c + 1], scale=scale[:, c:c + 1]).then_inc(U.hi, 1)
                        act.activation(ps, ps, ACT.Identity,
                                       bias=bias[:, c:c + 1], scale=scale[:, c:c + 1]).then_inc(U.hi, 1)

            act.wait_ge(S["prm0_loaded"], 32)
            act.activation(EPSB[:, 1:2], EPSB[:, 0:1], ACT.Identity, bias=1.0, scale=1.0).then_inc(S["eps_ready"], 1)
            act.wait_ge(S["eps_ready"], 1)
            with act.Fori(0, NG) as g:
                for j in range(TG):
                    act.wait_ge(UX.h, g * TG + j + 1)
                    if j == 0:
                        act.wait_ge(S["xhl_free"], g + 1)
                    act.activation(XHL[:, j, 0:D], xt(g * TG + j), ACT.Copy).then_inc(S["xn_hl_hi"], 1)
                    act.activation(Z[:, ds(g * (TG * D) + j * D, D)], xt(g * TG + j), ACT.Copy,
                                   scale=EPSB[:, 1:2]).then_inc(S["z_init"], 1)
                ln_hi(U1, g, g, PR0[:, 0:KC], PR0[:, KC:2 * KC])

            def q_hi(g, n):
                for i, (off, w) in enumerate(PAIRS):
                    act.wait_ge(S["q_turned"], 3 * n + i + 2)
                    act.activation(FT[:, 0, :, ds(g * GT + off, w)],
                                   PT[:, i % 2, 0:500].rearrange("p (c w) -> p c w", c=KC)[:, :, :w],
                                   ACT.Copy, scale=W_UP).then_inc(S["q_hi"], 1)

            def phase_a(g, n, with_q):
                for m in range(KC):
                    for p, (off, w) in enumerate(PARTS):
                        act.wait_ge(S["k_mm"], 4 * n + 2 * m + p + 1)
                        act.activation(KR[:, m, ds(g * GT + off, w)], FFP[:, 2 * m + p, :w], ACT.Copy)\
                            .then_inc(S["k_evac"], 1)
                if with_q:
                    q_hi(g - 1, n - 1)
                for j in range(TG + 1):
                    if j < TG:
                        act.wait_ge(S["qv_mm"], n * TG + j + 1)
                        act.activation(V[:, 0, ds(g * (TG * D) + j * D, D)], TM[:TT, j % 2, D:2 * D], ACT.Copy)\
                            .then_inc(S["v_hi"], 1)
                    if j >= 1:
                        act.wait_ge(S["qv_evac"], n * TG + j + 1)
                        act.activation(QS[:, j - 1, :], QS[:, j - 1, :], ACT.Exp, scale=SCALE / W_UP)\
                            .then_inc(S["q_exp"], 1)

            def gelu(n):
                for m in range(FC):
                    for p, (off, w) in enumerate(PARTS):
                        ps = FFP[:, 2 * (m % 2) + p, :w]
                        act.wait_ge(S["f1_mm"], 16 * n + 2 * m + p + 1)
                        act.activation(HID[:, 0, m, off:off + w], ps, ACT.Gelu, bias=PRM[:, 8 + m:9 + m],
                                       scale=1 / W_UP).then_inc(S["g_hi"], 1)
                        act.activation(ps, ps, ACT.Gelu, bias=PRM[:, 8 + m:9 + m],
                                       scale=1 / W_UP).then_inc(S["g_hi"], 1)

            with act.Fori(0, L) as l:
                n0 = l * NG
                phase_a(0, n0, False)
                with act.Fori(1, NG) as g:
                    phase_a(g, l * NG + g, True)
                q_hi(NG - 1, n0 + NG - 1)
                act.wait_ge(S["k_bias"], l + 1)
                with act.Fori(0, NG) as g:
                    b = (l * NG + g) * KC
                    for m in range(KC):
                        act.wait_ge(S["ke_turned"], b + m + 1)
                        act.activation(KE[:, m, :], KR[:, m, ds(g * GT, GT)], ACT.Exp, bias=NKB[:, m:m + 1],
                                       scale=SCALE / W_UP, accum_out=KSUM[:, m, ds(g, 1)]).then_inc(S["ke"], 1)
                    for m in range(KC):
                        bank = (PT, FFP)[m]
                        act.wait_ge(S["ke_turned"], b + m + 3)
                        act.wait_ge(S["ctx_mm"], b + m + 1)
                        act.activation(KT[:, 0, m, 0:4, :], bank[:TT, 0, :].rearrange("p (j c) -> p j c", j=4), ACT.Copy,
                                       scale=K_UP).then_inc(S["kt_hi"], 1)
                        act.activation(KT[:, 0, m, 4, :], bank[:TT, 1, :P], ACT.Copy,
                                       scale=K_UP).then_inc(S["kt_hi"], 1)
                ln_hi(U2, n0, 0, PRM[:, 4:6], PRM[:, 6:8])
                gelu(n0)
                ln_hi(U2, n0 + 1, 1, PRM[:, 4:6], PRM[:, 6:8])
                with act.Fori(1, NG - 1) as g:
                    n = l * NG + g
                    gelu(n)
                    ln_hi(U1, n + NG - 1, g - 1, PRM[:, 0:2], PRM[:, 2:4])
                    ln_hi(U2, n + 1, g + 1, PRM[:, 4:6], PRM[:, 6:8])
                gelu(n0 + NG - 1)
                ln_hi(U1, n0 + 2 * NG - 2, NG - 2, PRM[:, 0:2], PRM[:, 2:4])
                ln_hi(U1, n0 + 2 * NG - 1, NG - 1, PRM[:, 0:2], PRM[:, 2:4])

            act.sem_inc(S["zt"], 1)
            act.sem_inc(S["t_evac"], 4)
            act.sem_inc(S["y_evac"], 4)
            act.sem_inc(S["ct"], 1)
            act.wait_ge(S["gw_loaded"], 80)
            with act.Fori(0, NG) as g:
                for i, (off, w) in enumerate(PAIRS):
                    act.wait_ge(S["z_turned"], 3 * g + i + 2)
                    act.activation(ZT[:, :, off:off + w],
                                   PT[:, i % 2, 0:500].rearrange("p (c w) -> p c w", c=KC)[:, :, :w],
                                   ACT.Copy).then_inc(S["zt"], 1)
                for m in range(GC):
                    for p, (off, w) in enumerate(PARTS):
                        act.wait_ge(S["t_mm"], 8 * g + 2 * m + p + 1)
                        act.activation(TH[:, m, ds(g * GT + off, w)], FFP[:, 2 * (m % 2) + p, :w], ACT.Identity,
                                       bias=GPR[:, m:m + 1]).then_inc(S["t_evac"], 1)
            act.wait_ge(S["bn_b"], 1)
            with act.Fori(0, NG) as g:
                for m in range(GC):
                    act.activation(TH[:, m, ds(g * GT, GT)], TH[:, m, ds(g * GT, GT)], ACT.Relu,
                                   bias=BVE[:, 3, m:m + 1], scale=BVE[:, 2, m:m + 1]).then_inc(S["th_relu"], 1)
                hold(act, S["y_mm"], 4 * g + 1)
                for m in range(GC):
                    hold(act, S["th_relu"], g * GC + m + 1)
                    act.activation(HID[:, 0, m, :], TH[:, m, ds(g * GT, GT)], ACT.Copy).then_inc(S["th_hi"], 1)
                for m in range(KC):
                    for p, (off, w) in enumerate(PARTS):
                        act.wait_ge(S["y_mm"], 4 * g + 2 * m + p + 2)
                        act.activation(Y[:, m, ds(g * GT + off, w)], FFP[:, 2 * m + p, :w], ACT.Identity,
                                       bias=GPR[:, 3 * GC + m:3 * GC + m + 1], scale=1 / W_UP).then_inc(S["y_evac"], 1)
            act.wait_ge(S["bn_b"], 2)
            with act.Fori(0, NG) as g:
                act.wait_ge(S["r_turned"], g * TG + 1)
                for c in range(KC):
                    act.activation(ZT[:, c, :], Y[:, c, ds(g * GT, GT)], ACT.Relu, bias=BVE[:, 3, c:c + 1],
                                   scale=BVE[:, 2, c:c + 1]).then_inc(S["r_relu"], 1)
            with act.Fori(0, NG) as g:
                for i, (off, w) in enumerate(PAIRS):
                    act.wait_ge(U3.turned, 3 * g + i + 2)
                    act.activation(FT[:, 0, :, ds(g * GT + off, w)],
                                   PT[:, i % 2, 0:500].rearrange("p (c w) -> p c w", c=KC)[:, :, :w],
                                   ACT.Copy).then_inc(U3.hi, 1)
            act.wait_ge(S["rt"], 2)
            act.activation(RT[:, 1, :, :], RT[:, 0, :, :], ACT.Exp).then_inc(S["rt"], 1)
            with act.Fori(0, NG) as g:
                act.wait_ge(S["cb_turned"], g + 1)
                act.wait_ge(S["cb_mm"], g * TG + 1)
                act.activation(CT[:, 0:4 * TT], PT[:E, 0, 0:4 * TT], ACT.Copy).then_inc(S["ct"], 1)
                act.activation(CT[:, 4 * TT:GT], PT[:E, 1, 0:TT], ACT.Copy).then_inc(S["ct"], 1)
            with act.Fori(0, NG) as g:
                with act.Fori(0, E // 2) as h:
                    for q in range(2):
                        e, x = h * 2 + q, g * E + h * 2 + q
                        for m in range(KC):
                            for p, (off, w) in enumerate(PARTS):
                                ps = FFP[:, 2 * m + p, :w]
                                hold(act, S["e1_mm"], 4 * x + 2 * m + p + 1)
                                act.activation(HID[:, 0, 2 * q + m, off:off + w], ps, ACT.Gelu,
                                               bias=EB1[:, ds(e * KC + m, 1)], scale=1 / W_UP).then_inc(S["eg_hi"], 1)
                                act.activation(ps, ps, ACT.Gelu, bias=EB1[:, ds(e * KC + m, 1)],
                                               scale=1 / W_UP).then_inc(S["eg_hi"], 1)

        @block.vector
        def _(v):
            for s, c in (("x_used", 1), ("qv_evac", 1), ("q_lo", 1), ("kt_lo", 2), ("ctx_acc", 2), ("ao_evac", 1),
                         ("f2_evac", 1), ("g_lo", 1)):
                v.sem_inc(S[s], c)
            v.sem_inc(U1.lo, 1)
            v.sem_inc(U2.lo, 1)
            v.sem_inc(U3.lo, 1)
            v.sem_inc(S["oh_done"], RING)
            v.sem_inc(S["agg_add"], 2)
            for c in ("x1", "log", "cb_add", "e_out"):
                v.sem_inc(S[c], 1)
            v.sem_inc(S["eg_lo"], 4)

            def stats(U, u, src):
                for j in range(TG):
                    v.bn_stats(U.ST[:, j, :], src(j)).then_inc(U.stats, 1)
                hold(v, U.stats, u * TG + TG)
                for j in range(TG):
                    v.bn_aggr(U.MV[:, j, :], U.ST[:, j, :]).then_inc(U.moments, 1)

            def norm(U, u, src, dst):
                v.wait_ge(U.scales, 3 * u + 3)
                for j in range(TG):
                    v.tensor_scalar(dst(j), src(j), U.RS[:, j:j + 1], U.MR[:, j:j + 1], ALU.mult,
                                    ALU.subtract).then_inc(U.h, 1)

            def ln_lo(U, u, g):
                for i, (off, w) in enumerate(PAIRS):
                    v.wait_ge(U.hi, 12 * u + 4 * (i + 1))
                    v.tensor_tensor(FT[:, 1, :, ds(g * GT + off, w)],
                                    PT[:, i % 2, 0:500].rearrange("p (c w) -> p c w", c=KC)[:, :, :w],
                                    FT[:, 0, :, ds(g * GT + off, w)], ALU.subtract).then_inc(U.lo, 1)

            with v.Fori(0, NG) as g:
                tile = lambda j: X[:, ds(g * (TG * D) + j * D, D)]
                hold(v, S["x_loaded"], 16 * g + 16)
                stats(UX, g, lambda j: XIN[:, j, :])
                norm(UX, g, lambda j: XIN[:, j, :], tile)
                v.wait_ge(UX.h, (g + 1) * TG)
                v.sem_inc(S["x_used"], 1)
                for j in range(TG):
                    v.wait_ge(S["xn_hl_hi"], g * TG + j + 1)
                    last = v.tensor_tensor(XHL[:, j, D:2 * D], tile(j), XHL[:, j, 0:D], ALU.subtract)
                last.then_inc(S["xn_hl_lo"], 1)
                stats(U1, g, tile)
                v.wait_ge(U1.turned, 3 * g + 1)
                norm(U1, g, tile, lambda j: H1[:, j, :])
                ln_lo(U1, g, g)

            v.wait_ge(S["dst_loaded"], 16)
            v.tensor_copy(DSTF, DSTI).then_inc(S["list_step"], 1)
            v.wait_ge(S["list_step"], 1)
            for t in range(1, NT):
                v.tensor_scalar(JUNK[:, t, :], DSTF, float(t * TT), 0.0, ALU.is_lt, ALU.add,
                                accum_out=CNT[:, t:t + 1]).then_inc(S["cnt"], 1)
            v.wait_ge(S["cnt_mm"], 1)
            v.tensor_copy(SEG[:, :], TM[:, 0, 0:NT + 1]).then_inc(S["list_step"], 1)
            v.wait_ge(S["list_step"], 2)
            v.tensor_tensor(GRF[:, 0, 0:NT], SEG[:, 1:NT + 1], SEG[:, 0:NT], ALU.subtract).then_inc(S["list_step"], 1)
            v.wait_ge(S["list_step"], 3)
            v.tensor_scalar(GRI[:, :], GRF[:, 0, 0:NT], 1 / EG, 255 / 512, ALU.mult, ALU.add).then_inc(S["list_step"], 1)
            v.wait_ge(S["list_step"], 4)
            v.tensor_copy(GRF[:, 1, 0:NT], GRI[:, :]).then_inc(S["list_step"], 1)
            v.memset(GRF[:, 4, :], 1.0).then_inc(S["list_step"], 1)
            v.memset(GRF[:, 3, 0:1], 0.0).then_inc(S["list_step"], 1)
            v.wait_ge(S["list_step"], 7)
            v.tensor_tensor_scan(GRF[:, 2, 0:NT], GRF[:, 4, 0:NT], GRF[:, 1, 0:NT], 0.0, ALU.mult, ALU.add)\
                .then_inc(S["list_step"], 1)
            v.wait_ge(S["list_step"], 8)
            v.scalar_tensor_tensor(GRF[:, 3, 1:NT + 1], GRF[:, 2, 0:NT], -float(EG), SEG[:, 1:NT + 1], ALU.mult, ALU.add)\
                .then_inc(S["list_step"], 1)
            v.wait_ge(S["list_step"], 9)
            v.tensor_tensor(GRF[:, 0, 0:NT], GRF[:, 3, 1:NT + 1], GRF[:, 3, 0:NT], ALU.subtract).then_inc(S["list_step"], 1)
            v.wait_ge(S["consts"], 10)
            v.tensor_scalar(KIDX[:, 1, :], KIDX[:, 0, :], float(EG), None, ALU.mult).then_inc(S["list_step"], 1)
            v.wait_ge(S["list_step"], 10)
            for h in range(2):
                v.tensor_scalar(GMK[:, h, 0, :], GRF[:, 2, 0:NT], KIDX[:, 0, h:h + 1], None, ALU.is_le).then_inc(S["list_step"], 1)
                v.wait_ge(S["list_step"], 11 + 2 * h + 1)
                v.tensor_tensor(GMK[:, h, 1, :], GMK[:, h, 0, :], GRF[:, 0, 0:NT], ALU.mult).then_inc(S["list_step"], 1)
            v.wait_ge(S["list_step"], 15)
            for h in range(2):
                v.tensor_reduce(LSF[:, h, 1:2], GMK[:, h, 0, :], AX, ALU.add).then_inc(S["list_step"], 1)
                v.tensor_reduce(LSF[:, h, 0:1], GMK[:, h, 1, :], AX, ALU.add).then_inc(S["list_step"], 1)
            v.wait_ge(S["list_step"], 19)
            v.tensor_tensor(KIDX[:, 0, :], LSF[:, :, 0], KIDX[:, 1, :], ALU.add).then_inc(S["list_step"], 1)
            v.wait_ge(S["list_step"], 20)
            v.tensor_scalar(LST[:, :, 0], KIDX[:, 0, :], float(EDGES), None, ALU.min).then_inc(S["g_list"], 1)
            v.tensor_copy(LST[:, :, 1], LSF[:, :, 1]).then_inc(S["g_list"], 1)

            def q_lo(g, n):
                for i, (off, w) in enumerate(PAIRS):
                    v.wait_ge(S["q_hi"], 3 * n + i + 1)
                    v.scalar_tensor_tensor(FT[:, 1, :, ds(g * GT + off, w)],
                                           PT[:, i % 2, 0:500].rearrange("p (c w) -> p c w", c=KC)[:, :, :w], W_UP,
                                           FT[:, 0, :, ds(g * GT + off, w)], ALU.mult, ALU.subtract)\
                        .then_inc(S["q_lo"], 1)

            def phase_a(g, n, with_q):
                if with_q:
                    q_lo(g - 1, n - 1)
                v.wait_ge(S["k_evac"], 4 * n + 5)
                v.tensor_reduce(KMX[:, :, ds(g, 1)].rearrange("p c a -> p (c a)"), KR[:, :, ds(g * GT, GT)], AX, ALU.max)\
                    .then_inc(S["k_max"], 1)
                v.wait_ge(S["q_norm"], n * TG + 1)
                for j in range(TG + 1):
                    if j < TG:
                        q = TM[:TT, j % 2, 0:D].rearrange("p (h c) -> p h c", h=HEADS)
                        v.wait_ge(S["v_hi"], n * TG + j + 1)
                        v.tensor_reduce(QMX[:, j, :], q, AX, ALU.max).then_inc(S["q_max"], 1)
                        v.tensor_tensor(V[:, 1, ds(g * (TG * D) + j * D, D)], TM[:TT, j % 2, D:2 * D],
                                        V[:, 0, ds(g * (TG * D) + j * D, D)], ALU.subtract)
                        v.wait_ge(S["q_max"], n * TG + j + 1)
                        v.tensor_tensor(QS[:, j, :].rearrange("p (h c) -> p h c", h=HEADS), q,
                                        QMX[:, j, :].unsqueeze(2).to_broadcast([TT, HEADS, DH]), ALU.subtract)\
                            .then_inc(S["qv_evac"], 1)
                    if j >= 1:
                        v.wait_ge(S["q_exp"], n * TG + j)
                        v.tensor_reduce(QSUM[:, j - 1, :], QS[:, j - 1, :].rearrange("p (h c) -> p h c", h=HEADS),
                                        AX, ALU.add).then_inc(S["q_sum"], 1)
                        v.wait_ge(S["q_sum"], n * TG + j)
                        v.reciprocal(RINV[:, j - 1, :], QSUM[:, j - 1, :]).then_inc(S["q_rinv"], 1)

            def residual(n, g, done, scale, evac, first):
                for j in range(TG):
                    x = X[:, ds(g * (TG * D) + j * D, D)]
                    v.wait_ge(done, n * TG + j + 1)
                    if j == 0:
                        v.wait_ge(first, n + 1)
                    v.scalar_tensor_tensor(x, TM[:TT, j % 2, :D], scale, x, ALU.mult, ALU.add).then_inc(evac, 1)
                hold(v, evac, n * TG + TG + 1)

            def gelu_lo(n):
                for m in range(FC):
                    for p, (off, w) in enumerate(PARTS):
                        v.wait_ge(S["g_hi"], 32 * n + 2 * (2 * m + p) + 2)
                        v.tensor_tensor(HID[:, 1, m, off:off + w], FFP[:, 2 * (m % 2) + p, :w],
                                        HID[:, 0, m, off:off + w], ALU.subtract).then_inc(S["g_lo"], 1)

            def ln_group(U, u, g, H):
                tile = lambda j: X[:, ds(g * (TG * D) + j * D, D)]
                stats(U, u, tile)
                v.wait_ge(U.turned, 3 * u + 1)
                norm(U, u, tile, lambda j: H[:, j, :])

            with v.Fori(0, L) as l:
                n0 = l * NG
                phase_a(0, n0, False)
                with v.Fori(1, NG) as g:
                    phase_a(g, l * NG + g, True)
                q_lo(NG - 1, n0 + NG - 1)
                v.wait_ge(S["k_max"], n0 + NG)
                v.tensor_reduce(KM[:, :], KMX[:, :, :], AX, ALU.max).then_inc(S["kmax_all"], 1)
                v.memset(CTXA[:, :, :], 0.0).then_inc(S["ctx_zero"], 1)
                v.wait_ge(S["kmax_all"], l + 1)
                v.tensor_scalar(NKB[:, :], KM[:, :], -SCALE / W_UP, None, ALU.mult).then_inc(S["k_bias"], 1)
                hold(v, S["ctx_zero"], l + 1)
                with v.Fori(0, NG) as g:
                    b = (l * NG + g) * KC
                    for m in range(KC):
                        bank = (PT, FFP)[m]
                        v.wait_ge(S["kt_hi"], 2 * b + 2 * m + 2)
                        v.scalar_tensor_tensor(KT[:, 1, m, 0:4, :], bank[:TT, 0, :].rearrange("p (j c) -> p j c", j=4),
                                               K_UP, KT[:, 0, m, 0:4, :], ALU.mult, ALU.subtract)
                        v.scalar_tensor_tensor(KT[:, 1, m, 4, :], bank[:TT, 1, :P], K_UP,
                                               KT[:, 0, m, 4, :], ALU.mult, ALU.subtract).then_inc(S["kt_lo"], 1)
                    for m in range(KC):
                        v.wait_ge(S["ctx_mm"], b + m + 3)
                        v.wait_ge(S["ctx_acc"], b + m + 1)
                        v.tensor_tensor(CTXA[:, m, :], TM[:, m, :P], CTXA[:, m, :], ALU.add).then_inc(S["ctx_acc"], 1)
                v.wait_ge(S["ctx_acc"], (n0 + NG) * KC + 2)
                v.scalar_tensor_tensor(CTXM[:, :, :], CTXA[:, :, :], C_DOWN, MASK[:, :].unsqueeze(1).to_broadcast([P, KC, P]),
                                       ALU.mult, ALU.mult).then_inc(S["ctx_lo"], 1)
                v.wait_ge(S["ctx_lo"], 3 * l + 1)
                v.tensor_copy(CTX[:, 0, :, :], CTXM[:, :, :]).then_inc(S["ctx_lo"], 1)
                v.wait_ge(S["ctx_lo"], 3 * l + 2)
                v.tensor_tensor(CTX[:, 1, :, :], CTXM[:, :, :], CTX[:, 0, :, :], ALU.subtract).then_inc(S["ctx_lo"], 1)
                v.wait_ge(S["ke"], (n0 + NG) * KC)
                v.tensor_reduce(RKS[:, 0, :], KSUM[:, :, :], AX, ALU.add).then_inc(S["m_lo"], 1)
                v.wait_ge(S["m_lo"], 6 * l + 1)
                v.reciprocal(RKS[:, 1, :], RKS[:, 0, :]).then_inc(S["m_lo"], 1)
                v.wait_ge(S["m_lo"], 6 * l + 2)
                v.wait_ge(S["m_mm"], l + 1)
                for m in range(KC):
                    v.tensor_scalar(MF[:, m, :], FFP[:, 0, m * D:(m + 1) * D], RKS[:, 1, m:m + 1], None, ALU.mult)\
                        .then_inc(S["m_lo"], 1)
                v.wait_ge(S["m_lo"], 6 * l + 4)
                v.tensor_copy(M[:, 0, :, :], MF[:, :, :]).then_inc(S["m_lo"], 1)
                v.wait_ge(S["m_lo"], 6 * l + 5)
                v.tensor_tensor(M[:, 1, :, :], MF[:, :, :], M[:, 0, :, :], ALU.subtract).then_inc(S["m_lo"], 1)
                A_S, F_S = 1 / (W_UP * W_UP), 1 / W_UP
                residual(n0, 0, S["ao_mm"], A_S, S["ao_evac"], S["x_bo"])
                ln_group(U2, n0, 0, H2)
                ln_lo(U2, n0, 0)
                gelu_lo(n0)
                residual(n0 + 1, 1, S["ao_mm"], A_S, S["ao_evac"], S["x_bo"])
                ln_group(U2, n0 + 1, 1, H2)
                ln_lo_and_f2 = None
                ff_out = lambda n, g, js: [
                    (v.wait_ge(S["f2_mm"], n * TG + j + 1), v.wait_ge(S["x_b2"], n + 1) if j == 0 else None,
                     v.scalar_tensor_tensor(X[:, ds(g * (TG * D) + j * D, D)], TM[:TT, j % 2, :D], F_S,
                                            X[:, ds(g * (TG * D) + j * D, D)], ALU.mult, ALU.add)
                     .then_inc(S["f2_evac"], 1)) for j in js]
                ff_out(n0, 0, (0, 1))
                ln_lo(U2, n0 + 1, 1)
                ff_out(n0, 0, (2, 3, 4))
                hold(v, S["f2_evac"], n0 * TG + TG + 1)
                ln_group(U1, n0 + NG, 0, H1)
                with v.Fori(1, NG - 1) as g:
                    n = l * NG + g
                    gelu_lo(n)
                    residual(n + 1, g + 1, S["ao_mm"], A_S, S["ao_evac"], S["x_bo"])
                    ln_group(U2, n + 1, g + 1, H2)
                    ln_lo(U1, n + NG - 1, g - 1)
                    ff_out(n, g, (0, 1))
                    ln_lo(U2, n + 1, g + 1)
                    ff_out(n, g, (2, 3, 4))
                    hold(v, S["f2_evac"], n * TG + TG + 1)
                    ln_group(U1, n + NG, g, H1)
                n4 = n0 + NG - 1
                gelu_lo(n4)
                ln_lo(U1, n4 + NG - 1, NG - 2)
                ff_out(n4, NG - 1, range(TG))
                hold(v, S["f2_evac"], n4 * TG + TG + 1)
                ln_group(U1, n4 + NG, NG - 1, H1)
                ln_lo(U1, n4 + NG, NG - 1)

            hold(v, S["list_loaded"], 32)
            v.tensor_scalar(TBF[:, :], TBI.rearrange("p (n w) -> p w n", w=2)[:, 1, :], float(TT), None, ALU.mult).then_inc(S["tile_off"], 1)
            hold(v, S["tile_off"], 1)
            with v.Fori(0, NGRP // RING) as i:
                for r in range(RING):
                    hold(v, idx_loaded[r], 16 * i + 16)
                    v.tensor_scalar(LOC[:, r, :], IDXR[:, r, :].rearrange("p (c w) -> p w c", w=2)[:, 1, :],
                                    TBF[:, ds(i * RING + r, 1)], None, ALU.subtract).then_inc(S["oh_loc"], 1)
                for r in range(RING):
                    v.wait_ge(S["oh_loc"], i * RING + r + 1)
                    v.wait_ge(S["agg_mm"], i * RING + r + 1)
                    for c in range(2):
                        last = v.tensor_scalar(OH[:, r, c, :], IOTA[:, :], LOC[:, r, c:c + 1], None, ALU.is_equal)
                    last.then_inc(S["oh_done"], 1)
                for r in range(RING):
                    tile = v.value_load(LROW[0:1, ds((i * RING + r) * 2 + 1, 1)], min_val=0, max_val=NT)
                    z = Z[:, ds(tile * D, D)]
                    v.wait_ge(S["agg_mm"], i * RING + r + RING + 1)
                    v.wait_ge(S["agg_add"], i * RING + r + 2)
                    v.tensor_tensor(z, TM[:TT, r % 2, :D], z, ALU.add).then_inc(S["agg_add"], 1)
            v.wait_ge(S["agg_add"], NGRP + 2)
            hold(v, S["z_init"], NT)
            with v.Fori(0, NG) as g:
                v.wait_ge(S["z_turned"], 3 * g + 1)
                v.tensor_copy(H1[:, :, :], Z[:, ds(g * (TG * D), TG * D)].rearrange("p (j d) -> p j d", j=TG)).then_inc(S["zs"], 1)
                for m in range(GC):
                    for p, (off, w) in enumerate(PARTS):
                        hold(v, S["t_evac"], 8 * g + 2 * m + p + 5)
                        v.bn_stats(BST[:, m, ds(g * 12 + p * 6, 6)], TH[:, m, ds(g * GT + off, w)]).then_inc(S["t_stat"], 1)
            v.wait_ge(S["t_stat"], NG * GC * 2)
            for m in range(GC):
                v.bn_aggr(BMV[:, m, :], BST[:, m, :]).then_inc(S["bn_mv"], 1)
            hold(v, S["bn_b"], 1)
            v.sem_inc(S["xhl_used"], 1)
            with v.Fori(0, NG) as g:
                for m in range(GC):
                    v.wait_ge(S["th_hi"], g * GC + m + 1)
                    v.tensor_tensor(HID[:, 1, m, :], TH[:, m, ds(g * GT, GT)], HID[:, 0, m, :], ALU.subtract)\
                        .then_inc(S["th_lo"], 1)
                for m in range(KC):
                    for p, (off, w) in enumerate(PARTS):
                        hold(v, S["y_evac"], 4 * g + 2 * m + p + 5)
                        v.bn_stats(BST[:, m, ds(g * 12 + p * 6, 6)], Y[:, m, ds(g * GT + off, w)]).then_inc(S["y_stat"], 1)
                v.sem_inc(S["xhl_used"], 1)
            v.wait_ge(S["y_stat"], NG * KC * 2)
            for m in range(KC):
                v.bn_aggr(BMV[:, m, :], BST[:, m, :]).then_inc(S["bn_mv"], 1)
            hold(v, S["bn_mv"], GC + KC)
            with v.Fori(0, NG) as g:
                for j in range(TG):
                    x = X[:, ds(g * (TG * D) + j * D, D)]
                    if j == 0:
                        v.wait_ge(S["x_plus"], g + 1)
                    v.wait_ge(S["r_turned"], g * TG + j + 2)
                    v.tensor_tensor(x, TM[:TT, j % 2, :D], x, ALU.add).then_inc(S["x1"], 1)
            hold(v, S["x1"], NT + 1)
            with v.Fori(0, NG) as g:
                tile = lambda j: X[:, ds(g * (TG * D) + j * D, D)]
                stats(U3, g, tile)
                v.wait_ge(U3.turned, 3 * g + 1)
                v.wait_ge(S["x_tok"], g + 1)
                norm(U3, g, tile, lambda j: H1[:, j, :])
                for i, (off, w) in enumerate(PAIRS):
                    v.wait_ge(U3.hi, 3 * g + i + 1)
                    v.tensor_tensor(FT[:, 1, :, ds(g * GT + off, w)],
                                    PT[:, i % 2, 0:500].rearrange("p (c w) -> p c w", c=KC)[:, :, :w],
                                    FT[:, 0, :, ds(g * GT + off, w)], ALU.subtract).then_inc(U3.lo, 1)
                v.wait_ge(S["log_mm"], g + 1)
                v.tensor_scalar(LG[:, ds(g * TG, TG), :].rearrange("p t e -> p (t e)"), TM[:TT, 0, 0:TG * E], 1 / W_UP, None,
                                ALU.mult).then_inc(S["log"], 1)
            wide = lambda k: RT[:, k, :, :]
            per = lambda k: RM[:, k, :].unsqueeze(2).to_broadcast([TT, NT, E])
            r8 = R8[:, :].unsqueeze(1).to_broadcast([TT, NT, E])
            v.wait_ge(S["log"], NG + 1)
            v.tensor_reduce(RM[:, 0, :], LG[:, :, :], AX, ALU.max).then_inc(S["rt"], 1)
            v.wait_ge(S["rt"], 1)
            v.tensor_tensor(wide(0), LG[:, :, :], per(0), ALU.subtract).then_inc(S["rt"], 1)
            v.wait_ge(S["rt"], 3)
            v.tensor_reduce(RM[:, 1, :], wide(1), AX, ALU.add).then_inc(S["rt"], 1)
            v.wait_ge(S["rt"], 4)
            v.reciprocal(RM[:, 2, :], RM[:, 1, :]).then_inc(S["rt"], 1)
            v.wait_ge(S["rt"], 5)
            v.tensor_tensor(wide(2), wide(1), per(2), ALU.mult).then_inc(S["rt"], 1)
            n = 6
            src = 2
            for k in range(2):
                v.wait_ge(S["rt"], n)
                v.tensor_reduce(RM[:, 3 + k, :], wide(src), AX, ALU.max).then_inc(S["rt"], 1)
                v.wait_ge(S["rt"], n + 1)
                v.tensor_tensor(wide(3), wide(src), per(3 + k), ALU.is_equal).then_inc(S["rt"], 1)
                v.wait_ge(S["rt"], n + 2)
                v.tensor_tensor(wide(4), wide(3), r8, ALU.mult).then_inc(S["rt"], 1)
                v.wait_ge(S["rt"], n + 3)
                v.tensor_reduce(RM[:, 5, :], wide(4), AX, ALU.max).then_inc(S["rt"], 1)
                v.wait_ge(S["rt"], n + 4)
                v.tensor_tensor(wide(5 + k), wide(4), per(5), ALU.is_equal).then_inc(S["rt"], 1)
                n += 5
                if k == 0:
                    v.wait_ge(S["rt"], n)
                    v.scalar_tensor_tensor(wide(7), wide(5), -2.0, wide(2), ALU.mult, ALU.add).then_inc(S["rt"], 1)
                    n += 1
                    src = 7
            v.wait_ge(S["rt"], n)
            v.tensor_tensor(RM[:, 0, :], RM[:, 3, :], RM[:, 4, :], ALU.add).then_inc(S["rt"], 1)
            v.tensor_tensor(wide(0), wide(5), wide(6), ALU.add).then_inc(S["rt"], 1)
            v.wait_ge(S["rt"], n + 2)
            v.tensor_scalar(RM[:, 1, :], RM[:, 0, :], 1e-12, None, ALU.max).then_inc(S["rt"], 1)
            v.tensor_tensor(wide(1), wide(0), wide(2), ALU.mult).then_inc(S["rt"], 1)
            v.wait_ge(S["rt"], n + 4)
            v.reciprocal(RM[:, 2, :], RM[:, 1, :]).then_inc(S["rt"], 1)
            v.wait_ge(S["rt"], n + 5)
            v.tensor_tensor(wide(3), wide(1), per(2), ALU.mult).then_inc(S["rt"], 1)
            v.wait_ge(S["rt"], n + 6)
            v.tensor_scalar(CB[:, :, :], wide(3), 1 / W_UP, None, ALU.mult).then_inc(S["comb"], 1)
            hold(v, S["comb"], 1)
            with v.Fori(0, NG) as g:
                v.wait_ge(S["ct"], 2 * g + 1)
                v.tensor_copy(CBG, RT[:, 3, ds(g * TG, TG), :].rearrange("p t e -> p (t e)")).then_inc(S["cbg"], 1)
                for j in range(TG):
                    x = X[:, ds(g * (TG * D) + j * D, D)]
                    if j == 0:
                        v.wait_ge(S["x_tok"], g + 2)
                    v.wait_ge(S["cb_mm"], g * TG + j + 2)
                    v.tensor_tensor(x, TM[:TT, j % 2, :D], x, ALU.add).then_inc(S["cb_add"], 1)
            hold(v, S["cb_add"], NT + 1)
            with v.Fori(0, NG) as g:
                with v.Fori(0, E // 2) as h:
                    for q in range(2):
                        x = g * E + h * 2 + q
                        for m in range(KC):
                            for p, (off, w) in enumerate(PARTS):
                                v.wait_ge(S["eg_hi"], 8 * x + 4 * m + 2 * p + 2)
                                v.tensor_tensor(HID[:, 1, 2 * q + m, off:off + w], FFP[:, 2 * m + p, :w],
                                                HID[:, 0, 2 * q + m, off:off + w], ALU.subtract).then_inc(S["eg_lo"], 1)
                    for q in range(2):
                        e, x = h * 2 + q, g * E + h * 2 + q
                        for j in range(TG):
                            xt_ = X[:, ds(g * (TG * D) + j * D, D)]
                            v.wait_ge(S["e2_mm"], x * TG + j + 1)
                            v.wait_ge(S["e_out"], x * TG + 1)
                            v.scalar_tensor_tensor(xt_, TM[:TT, j % 2, :D],
                                                   CB[:, :, :].rearrange("p t e -> p (t e)")[:, ds(g * (TG * E) + e + j * E, 1)],
                                                   xt_, ALU.mult, ALU.add).then_inc(S["e_out"], 1)


_SHAPES = {}


def kernel(**inputs):
    import numpy as np
    import concourse.bacc as bacc
    from concourse.bass_utils import run_bass_kernel_spmd

    i = {k: np.asarray(v) for k, v in inputs.items()}

    def cols(w):
        w = w.reshape(*w.shape[:-2], w.shape[-2] // P, P, w.shape[-1])
        w = np.moveaxis(w, -3, -2)
        return w.reshape(*w.shape[:-2], -1)

    def pad(w, n):
        return np.concatenate([w, np.zeros((*w.shape[:-1], n - w.shape[-1]), w.dtype)], -1)

    wa = pad(np.concatenate([cols(np.concatenate([i["L0_mix_Wq"], i["L0_mix_Wv"]], -1)), cols(i["L0_mix_Wk"]),
                             cols(i["L0_mix_Wo"])], -1), WA)
    wa = np.concatenate([wa, pad(cols(i["L0_gnn_W2"]), WA)[None]], 0)
    wb = pad(np.concatenate([cols(i["L0_mix_W1"]), cols(i["L0_mix_W2"])], -1), WB)

    def vec(b):
        return np.swapaxes(b.reshape(*b.shape[:-1], -1, P), -1, -2)

    g1, b1 = vec(i["L0_mix_ln1_g"]), vec(i["L0_mix_ln1_b"])
    nxt = lambda t: np.concatenate([t[1:], np.zeros_like(t[:1])], 0)
    prm = np.concatenate([nxt(g1), nxt(b1), vec(i["L0_mix_ln2_g"]), vec(i["L0_mix_ln2_b"]), vec(i["L0_mix_b1"])], -1)
    data = {
        "x": i["x"],
        "prm0": np.concatenate([g1[0], b1[0]], -1),
        "prm": prm,
        "bo": i["L0_mix_bo"], "b2": i["L0_mix_b2"],
        "eps": i["L0_gnn_eps_gin"].reshape(1, 1),
        "wa": wa.reshape(L + 1, P, NG, WAS),
        "wb": wb.reshape(L, P, NG, WBS),
        "dst": i["dst"].reshape(TT, ER),
        "edges": np.concatenate([np.stack([i["src"], i["dst"]], -1), np.zeros((EG, 2), i["src"].dtype)], 0),
        "gw1": cols(i["L0_gnn_W1"]),
        "gprm": np.concatenate([vec(i["L0_gnn_" + k]) for k in ("b1", "g1", "bt1", "b2", "g2", "bt2")], -1),
        "rw": cols(i["L0_ffn_router_w"].T),
        "eb1": np.moveaxis(vec(i["L0_ffn_b1"]), 1, 0).reshape(P, -1), "eb2": i["L0_ffn_b2"],
        "mw": pad(np.moveaxis(np.concatenate([cols(i["L0_ffn_w1"]), cols(i["L0_ffn_w2"])], -1), 1, 0).reshape(P, -1), 8195)
        .reshape(P, NG, -1),
    }
    data = {k: np.ascontiguousarray(w) for k, w in data.items()}
    nc = bacc.Bacc("TRN2", target_bir_lowering=False, num_devices=1)
    aps = {k: nc.dram_tensor(f"in_{k}", w.shape, mybir.dt.from_np(w.dtype), kind="ExternalInput").ap()
           for k, w in data.items()}
    aps["xn_hl"] = nc.dram_tensor("xn_hl", [N, 2 * D], F16).ap()
    aps["lists"] = nc.dram_tensor("lists", [256, 2], I32).ap()
    aps["out"] = nc.dram_tensor("out_0", [N, D], F32, kind="ExternalOutput").ap()
    build(nc, aps, stop=STOP)
    r = run_bass_kernel_spmd(nc, [{f"in_{k}": w for k, w in data.items()}], core_ids=[0])
    return r.results[0]["out_0"]


STOP = ""
```

```python
from contextlib import ExitStack

import concourse.bass as bass
from concourse import mybir

F32 = mybir.dt.float32
F16 = mybir.dt.float16
I32 = mybir.dt.int32
U32 = mybir.dt.uint32
ALU = mybir.AluOpType
ACT = mybir.ActivationFunctionType
AX = mybir.AxisListType.X
ds = bass.ds

N, D, L, E = 3125, 256, 4, 8
P = 128
TT = 125
TG = 5
GT = TT * TG
NG = N // GT
NT = N // TT
KC = D // P
FF = 4 * D
FC = FF // P
HEADS, DH = 8, 32
SCALE = DH ** -0.25
EPS = 1e-5
EDGES = 50000
ER = EDGES // TT
EG = 256
NEG_ = -(-EDGES // EG) + NT
RING = 12
NPAIR = RING // 2
assert L * NG * RING >= NEG_
GF = 2 * D
GC = GF // P

W_UP = 64.0
K_UP = 256.0
C_DOWN = 1.0 / (W_UP * K_UP)
PARTS = ((0, 375), (375, 250))
PAIRS = ((0, 250), (250, 250), (500, 125))
PASSES = ((0, 0), (0, 1), (1, 0))

QV0, K0, WO0, WA = 0, KC * 2 * D, KC * 3 * D, 2050
W10, W20, WB = 0, KC * FF, 4100
WAS, WBS = WA // NG, WB // NG
NPRM = 20


def build(nc, a, stop=""):
    ctx = ExitStack()
    with ctx:
        def sb(name, shape, dt):
            return ctx.enter_context(nc.sbuf_tensor(name, shape, dt))

        def sem(name):
            return ctx.enter_context(nc.semaphore(name))

        X = sb("X", [TT, NT * D], F32)
        Z = sb("Z", [TT, (NT + 1) * D], F32)
        ft32 = sb("FT", [P, KC * N], F32)[:, :]
        FT = ft32.bitcast(F16).rearrange("p (s c n) -> p s c n", s=2, c=KC)
        KV = sb("KV", [P, 12800], F32)
        WAs = sb("WAs", [P, 2, WA], F16)
        wb32 = sb("WBs", [P, WB], F32)[:, :]
        hid32 = sb("HID", [P, FC * GT], F32)[:, :]
        WBs = wb32.bitcast(F16).rearrange("p (s n) -> p s n", s=2)
        HID = hid32.bitcast(F16).rearrange("p (s c n) -> p s c n", s=2, c=FC)
        H1 = sb("H1", [TT, TG, D], F32)
        QS = sb("QS", [TT, TG, D], F32)
        H2 = QS
        QN = sb("QN", [TT, TG, D], F32)
        STA = sb("STA", [P, WAS], F32)
        STB = sb("STB", [P, WBS], F32)
        BIAS = sb("BIAS", [2 * L, 2 * D], F16)
        SEL = sb("SEL", [2 * L, L, TT], F16)
        PRM = sb("PRM", [P, NPRM], F32)
        PR0 = sb("PR0", [P, 2 * KC], F32)
        IDF = sb("IDF", [P, P], F32)
        MASK = sb("MASK", [P, P], F32)
        EPSB = sb("EPSB", [TT, 2], F32)
        EXPO = sb("EXPO", [P, 8], F32)
        QMX = sb("QMX", [TT, TG, HEADS], F32)
        QSUM = sb("QSUM", [TT, TG, HEADS], F32)
        RINV = sb("RINV", [TT, TG, HEADS], F32)
        KMX = sb("KMX", [P, KC, NG], F32)
        KM = sb("KM", [P, KC], F32)
        NKB = sb("NKB", [P, KC], F32)
        KSUM = sb("KSUM", [P, KC, NG], F32)
        RKS = sb("RKS", [P, 2, KC], F32)
        CTXA = hid32[:, 3500:3500 + KC * P].rearrange("p (c n) -> p c n", c=KC)
        CTXM = hid32[:, 3200:3200 + KC * P].rearrange("p (c n) -> p c n", c=KC)
        CTX = hid32[:, 4000:4000 + KC * P].bitcast(F16).rearrange("p (s c n) -> p s c n", s=2, c=KC)
        M = sb("M", [P, 2, KC, D], F16)

        KR = KV[:, 0:KC * N].rearrange("p (c n) -> p c n", c=KC)
        V = KV[:TT, KC * N:KC * N + NT * D].bitcast(F16).rearrange("p (s n) -> p s n", s=2)
        KE = hid32[:, 0:KC * GT].rearrange("p (c n) -> p c n", c=KC)
        KT = hid32[:TT, KC * GT:KC * GT + 2 * TG * P].bitcast(F16).rearrange(
            "p (s m j c) -> p s m j c", s=2, m=KC, j=TG)
        XIN = QS
        DSTI, DSTF = KV[:TT, 0:ER].bitcast(I32), KV[:TT, ER:2 * ER]
        JUNK = KV[:TT, 2 * ER:2 * ER + NT * ER].rearrange("p (t n) -> p t n", t=NT)
        ONES = hid32[:, 2800:2800 + P]
        CNT = sb("CNT", [TT, NT + 1], F32)
        SEG = sb("SEG", [P, NT + 1], F32)
        GRI = sb("GRI", [P, NT], I32)
        GRF = hid32[:, 2400:2400 + 5 * (NT + 1)].rearrange("p (k t) -> p k t", k=5)
        KIDI = sb("KIDI", [P, 2], I32)
        KIDX = sb("KIDX", [P, 2, 2], F32)
        GMK = hid32[:, 2600:2600 + 4 * NT].rearrange("p (h k t) -> p h k t", h=2, k=2)
        LSF = sb("LSF", [P, 2, 2], F32)
        LROW = sb("LROW", [1, 512], I32)
        DIAG = KV[:, 0:512].rearrange("p (w h n) -> p w h n", w=2, h=2)
        TBF = sb("TBF", [P, 256], F32)
        IOTI = hid32[:, 0:TT].bitcast(I32)
        SELF = hid32[:2 * L, 200:200 + L * TT].rearrange("p (l c) -> p l c", l=L)
        BSF = hid32[:2 * L, 800:800 + 2 * D]
        BSR = hid32[:2 * L, 1400:1400 + 2 * D]
        BSH = hid32[:2 * L, 2000:2000 + D].bitcast(F16)
        EVEN = hid32[:2 * L, 2300:2302]
        IOTA = sb("IOTA", [P, TT], F16)
        IDXR = sb("IDXR", [P, RING, 4], I32)
        LOC = sb("LOC", [P, RING, 2], F32)
        OH = sb("OH", [P, RING, 2, TT], F16)
        GAT = KV[:, 0:RING * 2 * D].bitcast(F16).rearrange("p (r c n) -> p r c n", r=RING, c=2)
        GPR = sb("GPR", [P, 3 * GC + 3 * KC], F32)
        GW1 = wb32[:, 0:KC * GF]
        TH = KV[:, 0:GC * N].rearrange("p (c n) -> p c n", c=GC)
        ZT = hid32[:, 0:KC * GT].rearrange("p (c n) -> p c n", c=KC)
        Y = ft32.rearrange("p (c n) -> p c n", c=KC)
        BST = wb32[:, 3640:3640 + GC * 12 * NG].rearrange("p (c n) -> p c n", c=GC)
        BMV = sb("BMV", [P, GC, 2], F32)
        BVE = sb("BVE", [P, 4, GC], F32)
        ID64 = sb("ID64", [TT, TT], F16)
        MWC = 8195
        MWS = MWC // NG
        MW = KV[:, 0:MWC].bitcast(F16).rearrange("p (s n) -> p s n", s=2)
        STM = wb32[:, KC * GF:KC * GF + MWS]
        RW = sb("RW", [P, 2, KC * E], F16)
        RWF = wb32[:, 3600:3600 + 2 * KC * E].rearrange("p (s n) -> p s n", s=2)
        EB1 = sb("EB1", [P, E * KC], F32)
        EB2 = wb32[:E, 3300:3300 + D]
        LG = Z[:, 0:NT * E].rearrange("p (t e) -> p t e", e=E)
        RT = Z[:, NT * E:9 * NT * E].rearrange("p (k t e) -> p k t e", k=8, e=E)
        RM = Z[:, 2000:2000 + 6 * NT].rearrange("p (k t) -> p k t", k=6)
        R8 = sb("R8", [TT, E], F32)
        R8I = sb("R8I", [TT, E], I32)
        CB = Z[:, 9 * NT * E:10 * NT * E].rearrange("p (t e) -> p t e", e=E)
        CBG = wb32[:TT, 3560:3560 + TG * E]
        CT = wb32[:E, 2670:2670 + GT]
        XHL = QN[:, :, :].bitcast(F16)

        FFP = ctx.enter_context(nc.psum_tensor("FFP", [P, 4, 512], F32))
        PT = ctx.enter_context(nc.psum_tensor("PT", [P, 2, 512], F32))
        TM = ctx.enter_context(nc.psum_tensor("TM", [P, 2, 512], F32))

        KTP = [b.rearrange("p b c -> p (b c)")[:TT, :TG * P].rearrange("p (j c) -> p j c", j=TG)
               for b in (FFP[:, 0:2, :], PT[:, :, :])]

        class Unit:
            def __init__(self, k):
                self.ST = sb(f"ST{k}", [TT, TG, 6], F32)
                self.MV = sb(f"MV{k}", [TT, TG, 2], F32)
                self.VE = sb(f"VE{k}", [TT, TG], F32)
                self.RS = sb(f"RS{k}", [TT, TG], F32)
                self.MR = sb(f"MR{k}", [TT, TG], F32)
                self.stats = sem(f"ln{k}_stats")
                self.moments = sem(f"ln{k}_moments")
                self.scales = sem(f"ln{k}_scales")
                self.h = sem(f"ln{k}_h")
                self.turned = sem(f"ln{k}_turned")
                self.hi = sem(f"ln{k}_hi")
                self.lo = sem(f"ln{k}_lo")

        UX, U1, U2, U3 = Unit("x"), Unit("1"), Unit("2"), Unit("3")

        names = """list_step bn_step x_loaded x_used xn_hl_hi xn_hl_lo xn_stored z_init consts consts0 prm0_loaded prm_loaded wa_loaded wa_used wa_split wb_loaded wb_used wb_split k_mm k_evac k_max v_hi q_max qv_mm qv_evac q_exp q_sum q_rinv q_norm q_turned q_hi q_lo kmax_all k_bias ke ke_turned kt_hi kt_lo ctx_zero ctx_mm ctx_acc ctx_lo m_mm m_lo ao_mm ao_evac f1_mm g_hi g_lo f2_mm f2_evac eps_ready out_stored xhl_free held dst_loaded cnt cnt_mm g_list list_ready consts1 bias_step oh_loc oh_done agg_mm agg_add gw_loaded zs z_turned zt t_mm t_evac t_stat bn_mv bn_b xhl_loaded xhl_used th_relu th_hi th_lo y_mm y_evac y_stat r_relu r_turned x1 x_in_loaded x_in_used x_plus mw_loaded mw_used mw_split rw_lo x_tok log_mm log rt comb cbg cb_turned ct cb_mm cb_add e1_mm eg_hi eg_lo e2_mm e_out""".split()
        S = {n: sem(n) for n in names}
        idx_loaded = [sem(f"idx_loaded{u}") for u in range(NPAIR)]
        gathered = [sem(f"gathered{u}") for u in range(NPAIR)]

        block = ctx.enter_context(nc.Block())

        def hold(engine, semaphore, value):
            engine.wait_ge(semaphore, value)
            engine.sem_inc(S["held"], 1)

        def xt(t):
            return X[:, ds(t * D, D)]

        def ft(part, k, off, w):
            return FT[:, part, k, ds(off, w)]

        @block.sync
        def _(sp):
            sp.dma_start(X[:, 0:TG * D].rearrange("p (j d) -> p j d", j=TG),
                         a["x"][0:GT, :].rearrange("(j p) d -> p j d", j=TG)).then_inc(S["x_loaded"], 16)
            sp.dma_start(DSTI, a["dst"]).then_inc(S["dst_loaded"], 16)
            sp.dma_start(PR0[:, :], a["prm0"]).then_inc(S["prm0_loaded"], 16)
            sp.dma_start(EPSB[:, 0:1], a["eps"].broadcast_to([TT, 1])).then_inc(S["prm0_loaded"], 16)
            sp.dma_start(BSF, a["bias"]).then_inc(S["prm0_loaded"], 16)
            sp.sem_inc(S["xhl_free"], 1)

            def load_x(g):
                sp.dma_start(X[:, ds(g * (TG * D), TG * D)].rearrange("p (j d) -> p j d", j=TG),
                             a["x"].rearrange("(g j p) d -> g p j d", g=NG, j=TG)[ds(g, 1)]
                             .rearrange("a p j d -> p (a j) d")).then_inc(S["x_loaded"], 16)

            def load_wa0(g):
                sp.wait_ge(S["wa_used"], g + 1)
                sp.dma_start(STA[:, :], a["wa"][0, :, ds(g, 1), :].rearrange("p a c -> p (a c)"))\
                    .then_inc(S["wa_loaded"], 16)

            def store_xn(g):
                sp.wait_ge(S["xn_hl_lo"], g + 1)
                sp.dma_start(a["xn_hl"].rearrange("(g j p) d -> g p j d", g=NG, j=TG)[ds(g, 1)]
                             .rearrange("a p j d -> p (a j) d"), XHL).then_inc(S["xn_stored"], 16)
                sp.wait_ge(S["xn_stored"], 16 * g + 16)
                sp.sem_inc(S["xhl_free"], 1)

            load_wa0(0)
            with sp.Fori(0, NG - 1) as g:
                sp.wait_ge(S["x_loaded"], 16 * g + 16)
                load_x(g + 1)
                store_xn(g)
                load_wa0(g + 1)
            store_xn(NG - 1)
            sp.wait_ge(S["list_ready"], 3)

            def edges_of(n):
                for r in range(RING):
                    start = sp.value_load(LROW[0:1, ds(n * RING + r, 1)], min_val=0, max_val=EDGES)
                    sp.wait_ge(S["agg_mm"], n * RING + r + 1)
                    sp.wait_ge(S["oh_loc"], n * RING + r + 1)
                    sp.dma_start(IDXR[:, r, :], a["edges"][ds(start, EG), :].rearrange("(p c) w -> p (c w)", c=2))\
                        .then_inc(idx_loaded[r // 2], 16)

            with sp.Fori(0, L) as l:
                sp.wait_ge(U1.lo, 15 * l + 13)
                sp.dma_start(PRM[:, :], a["prm"][ds(l, 1)].rearrange("a p c -> p (a c)"))\
                    .then_inc(S["prm_loaded"], 16)
                with sp.Fori(0, NG) as g:
                    sp.wait_ge(S["wb_used"], l * NG + g + 1)
                    sp.dma_start(STB[:, :], a["wb"][ds(l, 1), :, ds(g, 1), :].rearrange("b p a c -> p (b a c)"))\
                        .then_inc(S["wb_loaded"], 16)
                edges_of(l * NG)

                def next_wa(l, g):
                    sp.wait_ge(S["wa_used"], l * NG + g + NG + 1)
                    sp.dma_start(STA[:, :], a["wa"][ds(l + 1, 1), :, ds(g, 1), :].rearrange("b p a c -> p (b a c)"))\
                        .then_inc(S["wa_loaded"], 16)
                with sp.Fori(0, NG - 1) as g:
                    next_wa(l, g)
                    edges_of(l * NG + g + 1)
                next_wa(l, NG - 1)
            sp.wait_ge(S["f2_evac"], L * NG * TG + 1)
            sp.dma_start(GW1, a["gw1"]).then_inc(S["gw_loaded"], 16)
            sp.dma_start(GPR[:, :], a["gprm"]).then_inc(S["gw_loaded"], 16)
            sp.dma_start(RWF[:, 0, :], a["rw"]).then_inc(S["gw_loaded"], 16)
            sp.dma_start(EB1[:, :], a["eb1"]).then_inc(S["gw_loaded"], 16)
            sp.dma_start(EB2, a["eb2"]).then_inc(S["gw_loaded"], 16)
            with sp.Fori(0, NG) as g:
                sp.wait_ge(S["xhl_used"], g + 1)
                sp.dma_start(XHL, a["xn_hl"].rearrange("(g j p) d -> g p j d", g=NG, j=TG)[ds(g, 1)]
                             .rearrange("a p j d -> p (a j) d")).then_inc(S["xhl_loaded"], 16)
            with sp.Fori(0, NG) as g:
                sp.wait_ge(S["x_in_used"], g + 1)
                sp.dma_start(XIN[:, :, :], a["x"].rearrange("(g j p) d -> g p j d", g=NG, j=TG)[ds(g, 1)]
                             .rearrange("a p j d -> p (a j) d")).then_inc(S["x_in_loaded"], 16)
                sp.wait_ge(S["mw_used"], g + 1)
                sp.dma_start(STM, a["mw"][:, ds(g, 1), :].rearrange("p a c -> p (a c)")).then_inc(S["mw_loaded"], 16)
            with sp.Fori(0, NG) as g:
                sp.wait_ge(S["e_out"], g * (E * TG) + E * TG + 1)
                sp.dma_start(a["out"].rearrange("(g j p) d -> g p j d", g=NG, j=TG)[ds(g, 1)].rearrange("a p j d -> p (a j) d"),
                             X[:, ds(g * (TG * D), TG * D)].rearrange("p (j d) -> p j d", j=TG))\
                    .then_inc(S["out_stored"], 16)
            sp.wait_ge(S["out_stored"], 16 * NG)
            if stop == "mix":
                sp.wait_ge(S["f2_evac"], L * NG * TG + 1)
                sp.wait_ge(S["xn_stored"], 16 * NG)
                sp.dma_start(a["out"].rearrange("(t p) d -> p t d", t=NT), X[:, :].rearrange("p (t d) -> p t d", t=NT))\
                    .then_inc(S["out_stored"], 16)
                sp.wait_ge(S["out_stored"], 16)

        @block.gpsimd
        def _(pool):
            pool.sem_inc(S["wa_used"], 1)
            pool.sem_inc(S["wb_used"], 1)
            pool.sem_inc(S["q_norm"], 1)
            pool.sem_inc(S["x_tok"], 1)
            pool.memset(EXPO[:, :], -0.5).then_inc(S["consts0"], 1)
            pool.memset(IDF[:, :], 0.0).then_inc(S["consts0"], 1)
            pool.memset(MASK[:, :], 1.0).then_inc(S["consts0"], 1)
            pool.memset(SELF, W_UP).then_inc(S["consts0"], 1)
            pool.iota(KIDI[:, :], pattern=[[P, 2]], base=0, channel_multiplier=1).then_inc(S["consts0"], 1)
            pool.iota(IOTI, pattern=[[1, TT]], base=0, channel_multiplier=0).then_inc(S["consts0"], 1)
            pool.iota(R8I[:, :], pattern=[[-1, E]], base=E, channel_multiplier=0).then_inc(S["consts0"], 1)
            pool.wait_ge(S["consts0"], 7)
            pool.affine_select(out=IDF[:, :], in_=IDF[:, :], compare_op=ALU.not_equal, fill=1.0, base=0,
                               pattern=[[-1, P]], channel_multiplier=1).then_inc(S["consts0"], 1)
            heads = MASK[:, :].rearrange("p (b c) -> p b c", c=DH)
            pool.affine_select(out=heads, in_=heads, compare_op=ALU.is_ge, fill=0.0, base=0,
                               pattern=[[-DH, P // DH], [0, DH]], channel_multiplier=1).then_inc(S["consts0"], 1)
            pool.affine_select(out=SELF, in_=SELF, compare_op=ALU.is_ge, fill=0.0, base=0,
                               pattern=[[-2, L], [0, TT]], channel_multiplier=1).then_inc(S["consts0"], 1)
            pool.wait_ge(S["consts0"], 10)
            pool.affine_select(out=SELF, in_=SELF, compare_op=ALU.is_ge, fill=0.0, base=1,
                               pattern=[[2, L], [0, TT]], channel_multiplier=-1).then_inc(S["consts1"], 1)
            hold(pool, S["consts1"], 1)
            pool.tensor_copy(SEL[:, :, :], SELF).then_inc(S["consts"], 1)
            pool.affine_select(out=heads, in_=heads, compare_op=ALU.is_ge, fill=0.0, base=DH - 1,
                               pattern=[[DH, P // DH], [0, DH]], channel_multiplier=-1).then_inc(S["consts"], 1)
            pool.tensor_copy(KIDX[:, 0, :], KIDI[:, :]).then_inc(S["consts"], 1)
            pool.tensor_copy(IOTA[:, :], IOTI).then_inc(S["consts"], 1)
            pool.tensor_copy(R8[:, :], R8I[:, :]).then_inc(S["consts"], 1)
            pool.memset(Z[:, NT * D:(NT + 1) * D], 0.0).then_inc(S["consts"], 1)
            pool.memset(ONES, 1.0).then_inc(S["consts"], 1)
            pool.memset(CNT[:, 0:1], 0.0).then_inc(S["consts"], 1)
            pool.memset(CNT[:, NT:NT + 1], float(ER)).then_inc(S["consts"], 1)
            pool.tensor_scalar(ID64[:, :], IDF[:TT, :TT], W_UP, 0.0, ALU.mult, ALU.add).then_inc(S["consts"], 1)

            def rstd(U, u):
                hold(pool, U.moments, (u + 1) * TG)
                pool.tensor_scalar(U.VE[:, :], U.MV[:, :, 1], 1.0, EPS, ALU.mult, ALU.add).then_inc(U.scales, 1)
                pool.wait_ge(U.scales, 3 * u + 1)
                pool.tensor_tensor(U.RS[:, :], U.VE[:, :], EXPO[:TT, 0:TG], ALU.pow).then_inc(U.scales, 1)
                pool.wait_ge(U.scales, 3 * u + 2)
                pool.tensor_tensor(U.MR[:, :], U.MV[:, :, 0], U.RS[:, :], ALU.mult).then_inc(U.scales, 1)

            def split_a(i, g):
                hold(pool, S["wa_split"], 3 * i + 1)
                pool.tensor_scalar(STA[:, :], STA[:, :], W_UP, 0.0, ALU.mult, ALU.add).then_inc(S["wa_split"], 1)
                pool.wait_ge(S["wa_split"], 3 * i + 2)
                pool.tensor_tensor(WAs[:, 1, ds(g * WAS, WAS)], STA[:, :], WAs[:, 0, ds(g * WAS, WAS)],
                                   ALU.subtract).then_inc(S["wa_split"], 1)
                hold(pool, S["wa_split"], 3 * i + 3)
                pool.sem_inc(S["wa_used"], 1)

            def split_b(i, g):
                hold(pool, S["wb_split"], 3 * i + 1)
                pool.tensor_scalar(STB[:, :], STB[:, :], W_UP, 0.0, ALU.mult, ALU.add).then_inc(S["wb_split"], 1)
                pool.wait_ge(S["wb_split"], 3 * i + 2)
                pool.tensor_tensor(WBs[:, 1, ds(g * WBS, WBS)], STB[:, :], WBs[:, 0, ds(g * WBS, WBS)],
                                   ALU.subtract).then_inc(S["wb_split"], 1)
                hold(pool, S["wb_split"], 3 * i + 3)
                pool.sem_inc(S["wb_used"], 1)

            rstd(UX, 0)
            with pool.Fori(0, NG - 1) as g:
                rstd(UX, g + 1)
                rstd(U1, g)
                split_a(g, g)
            rstd(U1, NG - 1)
            split_a(NG - 1, NG - 1)

            def gathers(n, slots):
                for r in slots:
                    pool.wait_ge(idx_loaded[r // 2], 32 * n + 32)
                    hold(pool, S["agg_mm"], n * RING + r + 1)
                    for c in range(2):
                        pool.indirect_dma_start(
                            out=GAT[:, r, c, :], out_offset=None, in_=a["xn_hl"],
                            in_offset=bass.IndirectOffsetOnAxis(ap=IDXR[:, r, 2 * c:2 * c + 1].bitcast(U32), axis=0))\
                            .then_inc(gathered[r // 2], 16)

            hold(pool, S["xn_stored"], 16 * NG)
            with pool.Fori(0, L) as l:
                with pool.Fori(0, NG) as g:
                    n = l * NG + g
                    pool.wait_ge(S["q_turned"], n * 3 + 1)
                    for j in range(TG):
                        pool.wait_ge(S["q_rinv"], n * TG + j + 1)
                        pool.tensor_tensor(QN[:, j, :].rearrange("p (h c) -> p h c", h=HEADS),
                                           QS[:, j, :].rearrange("p (h c) -> p h c", h=HEADS),
                                           RINV[:, j, :].unsqueeze(2).to_broadcast([TT, HEADS, DH]), ALU.mult)\
                            .then_inc(S["q_norm"], 1)
                    split_b(n, g)
                hold(pool, S["ke"], (l + 1) * NG * KC)
                gathers(l * NG, range(0, 6))
                rstd(U2, l * NG)
                gathers(l * NG, range(6, RING))
                with pool.Fori(0, NG - 1) as g:
                    n = l * NG + g
                    gathers(n + 1, range(0, 9))
                    rstd(U2, n + 1)
                    gathers(n + 1, range(9, RING))
                    rstd(U1, n + NG)
                    split_a(n + NG, g)
                split_a(l * NG + 2 * NG - 1, NG - 1)
                rstd(U1, l * NG + 2 * NG - 1)

            def bn_scales(i, chunks, g0, b0):
                pool.wait_ge(S["bn_mv"], (GC, GC + KC)[i])
                pool.tensor_scalar(BVE[:, 0, :chunks], BMV[:, :chunks, 1], 1.0, EPS, ALU.mult, ALU.add).then_inc(S["bn_step"], 1)
                pool.wait_ge(S["bn_step"], 4 * i + 1)
                pool.tensor_tensor(BVE[:, 1, :chunks], BVE[:, 0, :chunks], EXPO[:, :chunks], ALU.pow).then_inc(S["bn_step"], 1)
                pool.wait_ge(S["bn_step"], 4 * i + 2)
                pool.tensor_tensor(BVE[:, 2, :chunks], BVE[:, 1, :chunks], GPR[:, g0:g0 + chunks], ALU.mult).then_inc(S["bn_step"], 1)
                pool.wait_ge(S["bn_step"], 4 * i + 3)
                pool.tensor_tensor(BVE[:, 0, :chunks], BVE[:, 2, :chunks], BMV[:, :chunks, 0], ALU.mult).then_inc(S["bn_step"], 1)
                pool.wait_ge(S["bn_step"], 4 * i + 4)
                pool.tensor_tensor(BVE[:, 3, :chunks], GPR[:, b0:b0 + chunks], BVE[:, 0, :chunks], ALU.subtract).then_inc(S["bn_b"], 1)

            pool.wait_ge(S["gw_loaded"], 80)
            pool.tensor_scalar(RWF[:, 1, :], RWF[:, 0, :], W_UP, 0.0, ALU.mult, ALU.add).then_inc(S["rw_lo"], 1)
            pool.wait_ge(S["rw_lo"], 1)
            pool.tensor_copy(RW[:, 0, :], RWF[:, 1, :]).then_inc(S["rw_lo"], 1)
            pool.wait_ge(S["rw_lo"], 2)
            pool.tensor_tensor(RW[:, 1, :], RWF[:, 1, :], RW[:, 0, :], ALU.subtract).then_inc(S["rw_lo"], 1)
            bn_scales(0, GC, GC, 2 * GC)
            bn_scales(1, KC, 3 * GC + KC, 3 * GC + 2 * KC)
            pool.sem_inc(S["x_in_used"], 1)
            pool.sem_inc(S["mw_used"], 1)
            with pool.Fori(0, NG) as g:
                xg = X[:, ds(g * TG * D, TG * D)].rearrange("p (j d) -> p j d", j=TG)
                pool.wait_ge(S["x_in_loaded"], 16 * g + 16)
                pool.tensor_tensor(xg, xg, XIN[:, :, :], ALU.add).then_inc(S["x_plus"], 1)
                hold(pool, S["x_plus"], g + 1)
                pool.sem_inc(S["x_in_used"], 1)
                hold(pool, S["mw_loaded"], 16 * g + 16)
                pool.tensor_scalar(STM, STM, W_UP, 0.0, ALU.mult, ALU.add).then_inc(S["mw_split"], 1)
                hold(pool, S["mw_split"], 3 * g + 1)
                pool.tensor_copy(MW[:, 0, ds(g * MWS, MWS)], STM).then_inc(S["mw_split"], 1)
                pool.wait_ge(S["mw_split"], 3 * g + 2)
                pool.tensor_tensor(MW[:, 1, ds(g * MWS, MWS)], STM, MW[:, 0, ds(g * MWS, MWS)],
                                   ALU.subtract).then_inc(S["mw_split"], 1)
                hold(pool, S["mw_split"], 3 * g + 3)
                pool.sem_inc(S["mw_used"], 1)
            with pool.Fori(0, NG) as g:
                rstd(U3, g)
                xg = X[:, ds(g * TG * D, TG * D)].rearrange("p (j d) -> p j d", j=TG)
                pool.wait_ge(U3.h, (g + 1) * TG)
                pool.tensor_tensor(xg, xg, H1[:, :, :], ALU.add).then_inc(S["x_tok"], 1)

        @block.tensor
        def _(pe):
            pe.sem_inc(S["q_turned"], 1)
            pe.sem_inc(S["ke_turned"], 2)
            pe.sem_inc(S["ctx_mm"], 2)
            for c in ("y_mm", "cb_mm"):
                pe.sem_inc(S[c], 1)
            pe.sem_inc(S["r_turned"], 1)
            pe.sem_inc(S["z_turned"], 1)
            pe.sem_inc(S["agg_mm"], RING)
            for U in (U1, U2, U3):
                pe.sem_inc(U.turned, 1)

            def turn(U, u, H, free, pairs=(0, 1, 2)):
                for i in pairs:
                    off, w = PAIRS[i]
                    pe.wait_ge(U.h, u * TG + (2 * i + 2 if i < 2 else TG))
                    if i in free:
                        pe.wait_ge(*free[i])
                    for t in range(w // TT):
                        for c in range(KC):
                            last = pe.transpose(PT[:, i % 2, c * 250 + t * TT:c * 250 + (t + 1) * TT],
                                                H[:, 2 * i + t, c * P:(c + 1) * P], IDF[:TT, :TT])
                    last.then_inc(U.turned, 1)

            def mm3(out, lhs, rhs, chunks, more=False):
                for k in range(chunks):
                    for s, (x, y) in enumerate(PASSES):
                        last = pe.matmul(out, lhs(x, k), rhs(y, k), start=(k == 0 and s == 0),
                                         stop=(not more and k == chunks - 1 and s == len(PASSES) - 1))
                return last

            pe.wait_ge(S["consts"], 10)
            pe.wait_ge(S["cnt"], NT - 1)
            pe.matmul(TM[:, 0, 0:NT + 1], ONES[:TT], CNT[:, :], start=True, stop=True).then_inc(S["cnt_mm"], 1)
            pe.wait_ge(S["g_list"], 6)
            pe.matmul(TM[:, 1, :], ONES, DIAG.rearrange("p w h n -> p (w h n)"), start=True, stop=True).then_inc(S["cnt_mm"], 1)
            pe.wait_ge(S["list_ready"], 3)

            with pe.Fori(0, NG - 1) as g:
                turn(U1, g, H1, {0: (U1.lo, g * 3 + 1), 2: (U1.lo, g * 3 + 2)})

            def bias(out, l, w):
                return pe.matmul(out, SEL[:, ds(l, 1), :].rearrange("p a c -> p (a c)"), BIAS[:, w * D:(w + 1) * D],
                                 start=False, stop=True)

            def k_product(l, g, n):
                pe.wait_ge(U1.lo, 3 * n + 4)
                pe.wait_ge(S["k_evac"], 4 * n + 1)
                for m in range(KC):
                    for p, (off, w) in enumerate(PARTS):
                        mm3(FFP[:, 2 * m + p, :w],
                            lambda x, k: WAs[:, x, K0 + k * D + m * P:K0 + k * D + (m + 1) * P],
                            lambda y, k: ft(y, k, g * GT + off, w), KC).then_inc(S["k_mm"], 1)

            def qv_product(l, g, n, tiles=range(TG)):
                for j in tiles:
                    if j != 1:
                        pe.wait_ge(S["qv_evac"], n * TG + 1 + (j - 1 if j else 0))
                    mm3(TM[:TT, j % 2, :], lambda x, k: ft(x, k, g * GT + j * TT, TT),
                        lambda y, k: WAs[:, y, QV0 + k * 2 * D:QV0 + (k + 1) * 2 * D], KC).then_inc(S["qv_mm"], 1)

            def turn_q(n, pairs=(0, 1, 2)):
                for i in pairs:
                    off, w = PAIRS[i]
                    pe.wait_ge(S["q_norm"], n * TG + (2 * i + 2 if i < 2 else TG) + 1)
                    if i != 1:
                        pe.wait_ge(S["q_lo"], n * 3 + 1 + (1 if i else 0))
                    for t in range(w // TT):
                        for c in range(KC):
                            last = pe.transpose(PT[:, i % 2, c * 250 + t * TT:c * 250 + (t + 1) * TT],
                                                QN[:, 2 * i + t, c * P:(c + 1) * P], IDF[:TT, :TT])
                    last.then_inc(S["q_turned"], 1)

            def attention_out(l, g, n, first, second):
                for j in range(TG):
                    if j == 0:
                        pe.wait_ge(*first)
                        pe.wait_ge(S["q_lo"], 3 * n + 4)
                    if j == 1:
                        pe.wait_ge(*second)
                    if j > 1:
                        pe.wait_ge(S["ao_evac"], n * TG + j)
                    mm3(TM[:TT, j % 2, :D], lambda x, k: ft(x, k, g * GT + j * TT, TT),
                        lambda y, k: M[:, y, k, :], KC, more=True)
                    bias(TM[:TT, j % 2, :D], l, 0).then_inc(S["ao_mm"], 1)

            def aggregate(n, u, free):
                pe.wait_ge(S["oh_done"], n * RING + 2 * u + 2)
                pe.wait_ge(*free)
                for h in range(2):
                    r = 2 * u + h
                    pe.wait_ge(gathered[u], 64 * n + 64)
                    for c in range(2):
                        for s in range(2):
                            last = pe.matmul(TM[:TT, u % 2, h * D:(h + 1) * D], OH[:, r, c, :], GAT[:, r, c, s * D:(s + 1) * D],
                                             start=(c == 0 and s == 0), stop=(c == 1 and s == 1))
                    last.then_inc(S["agg_mm"], 1)

            def ff1(l, g, n, free):
                pe.wait_ge(U2.lo, 3 * n + 4)
                for m in range(FC):
                    if m >= 2:
                        pe.wait_ge(S["g_lo"], 16 * n + 2 * m - 2 + 1)
                    for p, (off, w) in enumerate(PARTS):
                        mm3(FFP[:, 2 * (m % 2) + p, :w],
                            lambda x, k: WBs[:, x, W10 + k * FF + m * P:W10 + k * FF + (m + 1) * P],
                            lambda y, k: ft(y, k, g * GT + off, w), KC).then_inc(S["f1_mm"], 1)
                    u = m - 1
                    if 0 <= u < NPAIR:
                        aggregate(n, u, free if u < 2 else (S["agg_add"], n * RING + 2 * u - 2 + 1))

            def ff2(l, n, j, free=None):
                if free is not None:
                    pe.wait_ge(*free)
                if j == 0:
                    pe.wait_ge(S["g_lo"], 16 * n + 17)
                elif j > 1:
                    pe.wait_ge(S["f2_evac"], n * TG + j)
                mm3(TM[:TT, j % 2, :D], lambda x, k: HID[:, x, k, j * TT:(j + 1) * TT],
                    lambda y, k: WBs[:, y, W20 + k * D:W20 + (k + 1) * D], FC, more=True)
                bias(TM[:TT, j % 2, :D], l, 1).then_inc(S["f2_mm"], 1)

            def step(l, g, n, free, before, after):
                ff1(l, g, n, free)
                banks = [(S["agg_add"], (n + 1) * RING - 1), (S["agg_add"], (n + 1) * RING + 1)]
                if before:
                    turn(U1, n + NG - 1, H1, {0: (U2.lo, 3 * n + 4), 2: (U1.lo, 3 * (n + NG - 1) + 2)}, (0, 1))
                if after:
                    attention_out(l, g + 1, n + 1, *banks)
                    banks = [(S["ao_evac"], (n + 2) * TG + 1), None]
                if before:
                    turn(U1, n + NG - 1, H1, {2: (U1.lo, 3 * (n + NG - 1) + 2)}, (2,))
                ff2(l, n, 0, banks[0])
                ff2(l, n, 1, banks[1])
                ff2(l, n, 2)
                if after:
                    turn(U2, n + 1, H2, {0: (U1.lo, 3 * (n + NG) + 1), 2: (U2.lo, 3 * (n + 1) + 2)}, (0, 1))
                ff2(l, n, 3)
                if after:
                    turn(U2, n + 1, H2, {0: (U1.lo, 3 * (n + NG) + 1), 2: (U2.lo, 3 * (n + 1) + 2)}, (2,))
                ff2(l, n, 4)

            with pe.Fori(0, L) as l:
                pe.wait_ge(S["wa_split"], 3 * (l * NG + NG))
                pe.wait_ge(S["f2_evac"], l * NG * TG + 1)
                k_product(l, 0, l * NG)
                qv_product(l, 0, l * NG, (0, 1))
                u4 = l * NG + NG - 1
                turn(U1, u4, H1, {0: (U2.lo, 3 * l * NG + 1)}, (0, 1))
                qv_product(l, 0, l * NG, (2,))
                turn(U1, u4, H1, {2: (U1.lo, 3 * u4 + 2)}, (2,))
                qv_product(l, 0, l * NG, (3, 4))
                with pe.Fori(1, NG) as g:
                    n = l * NG + g
                    k_product(l, g, n)
                    pe.wait_ge(U1.lo, 3 * (l * NG + NG) + 1)
                    turn_q(n - 1, (0, 1))
                    qv_product(l, g, n, (0,))
                    turn_q(n - 1, (2,))
                    qv_product(l, g, n, range(1, TG))
                def turn_k(g, m):
                    b = (l * NG + g) * KC
                    pe.wait_ge(S["ke"], b + m + 1)
                    pe.wait_ge(S["kt_lo"], b + m + 1)
                    for j in range(TG):
                        last = pe.transpose(KTP[m][:, j, :], KE[:, m, j * TT:(j + 1) * TT], IDF[:, :])
                    last.then_inc(S["ke_turned"], 1)

                def context(g, m):
                    b = (l * NG + g) * KC
                    pe.wait_ge(S["kt_lo"], b + m + 3)
                    pe.wait_ge(S["ctx_acc"], b + m + 1)
                    for j in range(TG):
                        for s, (x, y) in enumerate(PASSES):
                            last = pe.matmul(TM[:, m, :P], V[:, x, ds(g * (TG * D) + (j * D + m * P), P)],
                                             KT[:, y, m, j, :], start=(j == 0 and s == 0),
                                             stop=(j == TG - 1 and s == 2))
                    last.then_inc(S["ctx_mm"], 1)

                turn_k(0, 0)
                turn_q(l * NG + NG - 1)
                context(0, 0)
                pe.wait_ge(S["q_lo"], 3 * (l * NG + NG) + 1)
                turn_k(0, 1)
                with pe.Fori(1, NG) as g:
                    turn_k(g, 0)
                    context(g - 1, 1)
                    turn_k(g, 1)
                    context(g, 0)
                context(NG - 1, 1)
                pe.wait_ge(S["ctx_lo"], 3 * l + 3)
                for m in range(KC):
                    for s, (x, y) in enumerate(PASSES):
                        last = pe.matmul(FFP[:, 0, m * D:(m + 1) * D], CTX[:, x, m, :],
                                         WAs[:, y, WO0 + m * D:WO0 + (m + 1) * D], start=(s == 0), stop=(s == 2))
                last.then_inc(S["m_mm"], 1)
                pe.wait_ge(S["m_lo"], 6 * l + 6)
                pe.wait_ge(S["wb_split"], 3 * (l * NG + NG))
                n0 = l * NG
                attention_out(l, 0, n0, (S["ctx_acc"], (n0 + NG) * KC + 1), (S["ctx_acc"], (n0 + NG) * KC + 2))
                turn(U2, n0, H2, {0: (U1.lo, 3 * (n0 + NG) + 1), 2: (U2.lo, 3 * n0 + 2)})
                step(l, 0, n0, (S["ao_evac"], (n0 + 1) * TG + 1), False, True)
                with pe.Fori(1, NG - 1) as g:
                    n = l * NG + g
                    step(l, g, n, (S["f2_evac"], n * TG + 1), True, True)
                n4 = n0 + NG - 1
                step(l, NG - 1, n4, (S["f2_evac"], n4 * TG + 1), True, False)
            pe.wait_ge(S["gw_loaded"], 80)
            with pe.Fori(0, NG) as g:
                for i, (off, w) in enumerate(PAIRS):
                    pe.wait_ge(S["zs"], g + 1)
                    pe.wait_ge(S["zt"], 3 * g + 1 + (1 if i == 2 else 0))
                    for t in range(w // TT):
                        for c in range(KC):
                            last = pe.transpose(PT[:, i % 2, c * 250 + t * TT:c * 250 + (t + 1) * TT],
                                                H1[:, 2 * i + t, c * P:(c + 1) * P], IDF[:TT, :TT])
                    last.then_inc(S["z_turned"], 1)
                pe.wait_ge(S["zt"], 3 * g + 4)
                for m in range(GC):
                    for p, (off, w) in enumerate(PARTS):
                        pe.wait_ge(S["t_evac"], 8 * g + 2 * m + p + 1)
                        for k in range(KC):
                            last = pe.matmul(FFP[:, 2 * (m % 2) + p, :w], GW1[:, k * GF + m * P:k * GF + (m + 1) * P],
                                             ZT[:, k, off:off + w], start=(k == 0), stop=(k == KC - 1))
                        last.then_inc(S["t_mm"], 1)
            pe.wait_ge(S["wa_split"], 3 * (L + 1) * NG)
            with pe.Fori(0, NG) as g:
                pe.wait_ge(S["th_lo"], g * GC + GC)
                pe.wait_ge(S["xhl_loaded"], 16 * g + 16)
                for m in range(KC):
                    for p, (off, w) in enumerate(PARTS):
                        pe.wait_ge(S["y_evac"], 4 * g + 2 * m + p + 1)
                        out = FFP[:, 2 * m + p, :w]
                        for k in range(GC):
                            for s, (x, y) in enumerate(PASSES):
                                pe.matmul(out, WAs[:, x, k * D + m * P:k * D + (m + 1) * P], HID[:, y, k, off:off + w],
                                          start=(k == 0 and s == 0), stop=False, skip_group_check=True)
                        tiles = range(off // TT, (off + w) // TT)
                        for j in tiles:
                            for s in range(2):
                                last = pe.matmul(FFP[:, 2 * m + p, j * TT - off:(j + 1) * TT - off],
                                                 XHL[:, j, s * D + m * P:s * D + (m + 1) * P], ID64[:, :],
                                                 start=False, stop=(j == tiles[-1] and s == 1), skip_group_check=True)
                        last.then_inc(S["y_mm"], 1)
            with pe.Fori(0, NG) as g:
                pe.wait_ge(S["r_relu"], KC * (g + 1))
                for j in range(TG):
                    if j != 1:
                        pe.wait_ge(S["x1"], g * TG + (j if j else 1))
                    for c in range(KC):
                        last = pe.transpose(TM[:TT, j % 2, c * P:(c + 1) * P], ZT[:, c, j * TT:(j + 1) * TT], IDF[:, :])
                    last.then_inc(S["r_turned"], 1)
            pe.wait_ge(S["rw_lo"], 3)
            with pe.Fori(0, NG) as g:
                turn(U3, g, H1, {0: (U3.lo, 3 * g + 1), 2: (U3.lo, 3 * g + 2)})
                pe.wait_ge(U3.lo, 3 * g + 4)
                pe.wait_ge(S["log"], g + 1)
                for j in range(TG):
                    last = mm3(TM[:TT, 0, j * E:(j + 1) * E], lambda x, k: ft(x, k, g * GT + j * TT, TT),
                               lambda y, k: RW[:, y, k * E:(k + 1) * E], KC)
                last.then_inc(S["log_mm"], 1)
            with pe.Fori(0, NG) as g:
                pe.wait_ge(S["cbg"], g + 1)
                pe.wait_ge(S["ct"], 2 * g + 1)
                for j in range(TG):
                    last = pe.transpose(PT[:E, j // 4, (j % 4) * TT:(j % 4 + 1) * TT], CBG[:, j * E:(j + 1) * E], IDF[:TT, :TT])
                last.then_inc(S["cb_turned"], 1)
                pe.wait_ge(S["ct"], 2 * g + 3)
                for j in range(TG):
                    if j != 1:
                        pe.wait_ge(S["cb_add"], g * TG + (j if j else 1))
                    pe.matmul(TM[:TT, j % 2, :D], CT[:, j * TT:(j + 1) * TT], EB2, start=True, stop=True)\
                        .then_inc(S["cb_mm"], 1)
            pe.wait_ge(S["mw_split"], 3 * NG)
            pe.wait_ge(S["cb_add"], NT + 1)
            with pe.Fori(0, NG) as g:
                with pe.Fori(0, E // 2) as h:
                    for q in range(2):
                        e, x = h * 2 + q, g * E + h * 2 + q
                        for m in range(KC):
                            pe.wait_ge(S["eg_lo"], 4 * x + 2 * m + 2)
                            for p, (off, w) in enumerate(PARTS):
                                mm3(FFP[:, 2 * m + p, :w],
                                    lambda s, k: MW[:, s, ds(e * (4 * D) + (k * D + m * P), P)],
                                    lambda s, k: ft(s, k, g * GT + off, w), KC).then_inc(S["e1_mm"], 1)
                    for q in range(2):
                        e, x = h * 2 + q, g * E + h * 2 + q
                        pe.wait_ge(S["eg_lo"], 4 * x + 4 + 4)
                        for j in range(TG):
                            if j != 1:
                                pe.wait_ge(S["e_out"], x * TG + (j if j else 1))
                            mm3(TM[:TT, j % 2, :D], lambda s, k: HID[:, s, 2 * q + k, j * TT:(j + 1) * TT],
                                lambda s, k: MW[:, s, ds(e * (4 * D) + (2 * D + k * D), D)], KC).then_inc(S["e2_mm"], 1)

        @block.scalar
        def _(act):
            act.sem_inc(S["k_evac"], 1)

            def split_hi(stage, loaded, W, w, split, i, g):
                act.wait_ge(loaded, 16 * i + 16)
                act.activation(W[:, 0, ds(g * w, w)], stage[:, :], ACT.Copy, scale=W_UP).then_inc(split, 1)

            def split_hi_a(i, g):
                split_hi(STA, S["wa_loaded"], WAs, WAS, S["wa_split"], i, g)

            def ln_hi(U, u, g, scale, bias, pairs=(0, 1, 2)):
                for i in pairs:
                    off, w = PAIRS[i]
                    act.wait_ge(U.turned, 3 * u + i + 2)
                    for c in range(KC):
                        ps = PT[:, i % 2, c * 250:c * 250 + w]
                        act.activation(ft(0, c, g * GT + off, w), ps, ACT.Identity,
                                       bias=bias[:, c:c + 1], scale=scale[:, c:c + 1]).then_inc(U.hi, 1)
                        act.activation(ps, ps, ACT.Identity,
                                       bias=bias[:, c:c + 1], scale=scale[:, c:c + 1]).then_inc(U.hi, 1)

            act.wait_ge(S["prm0_loaded"], 48)
            act.activation(EPSB[:, 1:2], EPSB[:, 0:1], ACT.Identity, bias=1.0, scale=1.0).then_inc(S["eps_ready"], 1)
            act.wait_ge(S["eps_ready"], 1)
            def rows_of_xn(g):
                for j in range(TG):
                    act.wait_ge(UX.h, g * TG + j + 1)
                    if j == 0:
                        act.wait_ge(S["xhl_free"], g + 1)
                    act.activation(XHL[:, j, 0:D], xt(g * TG + j), ACT.Copy).then_inc(S["xn_hl_hi"], 1)
                    act.activation(Z[:, ds(g * (TG * D) + j * D, D)], xt(g * TG + j), ACT.Copy,
                                   scale=EPSB[:, 1:2]).then_inc(S["z_init"], 1)

            rows_of_xn(0)
            split_hi_a(0, 0)
            with act.Fori(1, NG) as g:
                rows_of_xn(g)
                split_hi_a(g, g)
                ln_hi(U1, g - 1, g - 1, PR0[:, 0:KC], PR0[:, KC:2 * KC])

            def q_hi(g, n, pairs=(0, 1, 2)):
                for i in pairs:
                    off, w = PAIRS[i]
                    act.wait_ge(S["q_turned"], 3 * n + i + 2)
                    act.activation(FT[:, 0, :, ds(g * GT + off, w)],
                                   PT[:, i % 2, 0:500].rearrange("p (c w) -> p c w", c=KC)[:, :, :w],
                                   ACT.Copy, scale=W_UP).then_inc(S["q_hi"], 1)

            def phase_a(l, g, n, with_q, with_ln=False):
                for m in range(KC):
                    for p, (off, w) in enumerate(PARTS):
                        act.wait_ge(S["k_mm"], 4 * n + 2 * m + p + 1)
                        act.activation(KR[:, m, ds(g * GT + off, w)], FFP[:, 2 * m + p, :w], ACT.Copy)\
                            .then_inc(S["k_evac"], 1)
                if with_q:
                    q_hi(g - 1, n - 1, (0, 1))
                for j in range(TG + 1):
                    if j < TG:
                        act.wait_ge(S["qv_mm"], n * TG + j + 1)
                        act.activation(V[:, 0, ds(g * (TG * D) + j * D, D)], TM[:TT, j % 2, D:2 * D], ACT.Copy)\
                            .then_inc(S["v_hi"], 1)
                    if j == 0 and with_q:
                        q_hi(g - 1, n - 1, (2,))
                    if j >= 1:
                        act.wait_ge(S["qv_evac"], n * TG + j + 1)
                        act.activation(QS[:, j - 1, :], QS[:, j - 1, :], ACT.Exp, scale=SCALE / W_UP)\
                            .then_inc(S["q_exp"], 1)
                    if j in (2, 3) and with_ln:
                        if j == 2:
                            act.wait_ge(S["prm_loaded"], 16 * l + 16)
                        ln_hi(U1, n + NG - 1, NG - 1, PRM[:, 16:18], PRM[:, 18:20], (0, 1) if j == 2 else (2,))
                hold(act, S["f2_evac"], l * NG * TG + 1)
                split_hi(STB, S["wb_loaded"], WBs, WBS, S["wb_split"], n, g)

            def gelu(n):
                for m in range(FC):
                    for p, (off, w) in enumerate(PARTS):
                        ps = FFP[:, 2 * (m % 2) + p, :w]
                        act.wait_ge(S["f1_mm"], 16 * n + 2 * m + p + 1)
                        act.activation(HID[:, 0, m, off:off + w], ps, ACT.Gelu, bias=PRM[:, 8 + m:9 + m],
                                       scale=1 / W_UP).then_inc(S["g_hi"], 1)
                        act.activation(ps, ps, ACT.Gelu, bias=PRM[:, 8 + m:9 + m],
                                       scale=1 / W_UP).then_inc(S["g_hi"], 1)

            with act.Fori(0, L) as l:
                n0 = l * NG
                phase_a(l, 0, n0, False, True)
                with act.Fori(1, NG) as g:
                    phase_a(l, g, l * NG + g, True)
                act.wait_ge(S["k_bias"], l + 1)
                def k_exp(g, m):
                    act.wait_ge(S["ke_turned"], (l * NG + g) * KC + m + 1)
                    act.activation(KE[:, m, :], KR[:, m, ds(g * GT, GT)], ACT.Exp, bias=NKB[:, m:m + 1],
                                   scale=SCALE / W_UP, accum_out=KSUM[:, m, ds(g, 1)]).then_inc(S["ke"], 1)

                def kt_hi(g, m):
                    b = (l * NG + g) * KC
                    act.wait_ge(S["ke_turned"], b + m + 3)
                    act.wait_ge(S["ctx_mm"], b + m + 1)
                    act.activation(KT[:, 0, m, :, :], KTP[m], ACT.Copy, scale=K_UP).then_inc(S["kt_hi"], 1)

                k_exp(0, 0)
                k_exp(0, 1)
                kt_hi(0, 0)
                q_hi(NG - 1, n0 + NG - 1)
                k_exp(1, 0)
                kt_hi(0, 1)
                with act.Fori(1, NG - 1) as g:
                    k_exp(g, 1)
                    kt_hi(g, 0)
                    k_exp(g + 1, 0)
                    kt_hi(g, 1)
                k_exp(NG - 1, 1)
                kt_hi(NG - 1, 0)
                kt_hi(NG - 1, 1)
                hold(act, S["m_mm"], l + 1)
                ln_hi(U2, n0, 0, PRM[:, 4:6], PRM[:, 6:8])
                gelu(n0)
                ln_hi(U2, n0 + 1, 1, PRM[:, 4:6], PRM[:, 6:8])
                split_hi_a(n0 + NG, 0)
                with act.Fori(1, NG - 1) as g:
                    n = l * NG + g
                    gelu(n)
                    ln_hi(U1, n + NG - 1, g - 1, PRM[:, 0:2], PRM[:, 2:4])
                    ln_hi(U2, n + 1, g + 1, PRM[:, 4:6], PRM[:, 6:8])
                    split_hi_a(n + NG, g)
                gelu(n0 + NG - 1)
                ln_hi(U1, n0 + 2 * NG - 2, NG - 2, PRM[:, 0:2], PRM[:, 2:4])
                split_hi_a(n0 + 2 * NG - 1, NG - 1)

            act.sem_inc(S["zt"], 1)
            act.sem_inc(S["t_evac"], 4)
            act.sem_inc(S["y_evac"], 4)
            act.sem_inc(S["ct"], 1)
            act.wait_ge(S["gw_loaded"], 80)
            with act.Fori(0, NG) as g:
                for i, (off, w) in enumerate(PAIRS):
                    act.wait_ge(S["z_turned"], 3 * g + i + 2)
                    act.activation(ZT[:, :, off:off + w],
                                   PT[:, i % 2, 0:500].rearrange("p (c w) -> p c w", c=KC)[:, :, :w],
                                   ACT.Copy).then_inc(S["zt"], 1)
                for m in range(GC):
                    for p, (off, w) in enumerate(PARTS):
                        act.wait_ge(S["t_mm"], 8 * g + 2 * m + p + 1)
                        act.activation(TH[:, m, ds(g * GT + off, w)], FFP[:, 2 * (m % 2) + p, :w], ACT.Identity,
                                       bias=GPR[:, m:m + 1]).then_inc(S["t_evac"], 1)
            act.wait_ge(S["bn_b"], 1)
            with act.Fori(0, NG) as g:
                for m in range(GC):
                    act.activation(TH[:, m, ds(g * GT, GT)], TH[:, m, ds(g * GT, GT)], ACT.Relu,
                                   bias=BVE[:, 3, m:m + 1], scale=BVE[:, 2, m:m + 1]).then_inc(S["th_relu"], 1)
                hold(act, S["y_mm"], 4 * g + 1)
                for m in range(GC):
                    hold(act, S["th_relu"], g * GC + m + 1)
                    act.activation(HID[:, 0, m, :], TH[:, m, ds(g * GT, GT)], ACT.Copy).then_inc(S["th_hi"], 1)
                for m in range(KC):
                    for p, (off, w) in enumerate(PARTS):
                        act.wait_ge(S["y_mm"], 4 * g + 2 * m + p + 2)
                        act.activation(Y[:, m, ds(g * GT + off, w)], FFP[:, 2 * m + p, :w], ACT.Identity,
                                       bias=GPR[:, 3 * GC + m:3 * GC + m + 1], scale=1 / W_UP).then_inc(S["y_evac"], 1)
            act.wait_ge(S["bn_b"], 2)
            with act.Fori(0, NG) as g:
                act.wait_ge(S["r_turned"], g * TG + 1)
                for c in range(KC):
                    act.activation(ZT[:, c, :], Y[:, c, ds(g * GT, GT)], ACT.Relu, bias=BVE[:, 3, c:c + 1],
                                   scale=BVE[:, 2, c:c + 1]).then_inc(S["r_relu"], 1)
            with act.Fori(0, NG) as g:
                for i, (off, w) in enumerate(PAIRS):
                    act.wait_ge(U3.turned, 3 * g + i + 2)
                    act.activation(FT[:, 0, :, ds(g * GT + off, w)],
                                   PT[:, i % 2, 0:500].rearrange("p (c w) -> p c w", c=KC)[:, :, :w],
                                   ACT.Copy).then_inc(U3.hi, 1)
            act.wait_ge(S["rt"], 2)
            act.activation(RT[:, 1, :, :], RT[:, 0, :, :], ACT.Exp).then_inc(S["rt"], 1)
            with act.Fori(0, NG) as g:
                act.wait_ge(S["cb_turned"], g + 1)
                act.wait_ge(S["cb_mm"], g * TG + 1)
                act.activation(CT[:, 0:4 * TT], PT[:E, 0, 0:4 * TT], ACT.Copy).then_inc(S["ct"], 1)
                act.activation(CT[:, 4 * TT:GT], PT[:E, 1, 0:TT], ACT.Copy).then_inc(S["ct"], 1)
            with act.Fori(0, NG) as g:
                with act.Fori(0, E // 2) as h:
                    for q in range(2):
                        e, x = h * 2 + q, g * E + h * 2 + q
                        for m in range(KC):
                            for p, (off, w) in enumerate(PARTS):
                                ps = FFP[:, 2 * m + p, :w]
                                hold(act, S["e1_mm"], 4 * x + 2 * m + p + 1)
                                act.activation(HID[:, 0, 2 * q + m, off:off + w], ps, ACT.Gelu,
                                               bias=EB1[:, ds(e * KC + m, 1)], scale=1 / W_UP).then_inc(S["eg_hi"], 1)
                                act.activation(ps, ps, ACT.Gelu, bias=EB1[:, ds(e * KC + m, 1)],
                                               scale=1 / W_UP).then_inc(S["eg_hi"], 1)

        @block.vector
        def _(v):
            for s, c in (("x_used", 1), ("qv_evac", 1), ("q_lo", 1), ("kt_lo", 2), ("ctx_acc", 2), ("ao_evac", 1),
                         ("f2_evac", 1), ("g_lo", 1)):
                v.sem_inc(S[s], c)
            v.sem_inc(U1.lo, 1)
            v.sem_inc(U2.lo, 1)
            v.sem_inc(U3.lo, 1)
            v.sem_inc(S["oh_loc"], RING)
            v.sem_inc(S["agg_add"], 1)
            for c in ("x1", "log", "cb_add", "e_out"):
                v.sem_inc(S[c], 1)
            v.sem_inc(S["eg_lo"], 4)

            def stats(U, u, src):
                for j in range(TG):
                    v.bn_stats(U.ST[:, j, :], src(j)).then_inc(U.stats, 1)
                hold(v, U.stats, u * TG + TG)
                for j in range(TG):
                    v.bn_aggr(U.MV[:, j, :], U.ST[:, j, :]).then_inc(U.moments, 1)

            def norm(U, u, src, dst):
                v.wait_ge(U.scales, 3 * u + 3)
                for j in range(TG):
                    v.tensor_scalar(dst(j), src(j), U.RS[:, j:j + 1], U.MR[:, j:j + 1], ALU.mult,
                                    ALU.subtract).then_inc(U.h, 1)

            def ln_lo(U, u, g, pairs=(0, 1, 2)):
                for i in pairs:
                    off, w = PAIRS[i]
                    v.wait_ge(U.hi, 12 * u + 4 * (i + 1))
                    v.tensor_tensor(FT[:, 1, :, ds(g * GT + off, w)],
                                    PT[:, i % 2, 0:500].rearrange("p (c w) -> p c w", c=KC)[:, :, :w],
                                    FT[:, 0, :, ds(g * GT + off, w)], ALU.subtract).then_inc(U.lo, 1)

            tile_of = lambda g: lambda j: X[:, ds(g * (TG * D) + j * D, D)]

            def first_norms(g, before, after):
                norm(UX, g, tile_of(g), tile_of(g))
                if after:
                    hold(v, S["x_loaded"], 16 * g + 32)
                    stats(UX, g + 1, tile_of(g + 1))
                if before:
                    v.wait_ge(U1.turned, 3 * (g - 1) + 1)
                    norm(U1, g - 1, tile_of(g - 1), lambda j: H1[:, j, :])
                hold(v, UX.h, (g + 1) * TG)
                stats(U1, g, tile_of(g))
                for j in range(TG):
                    v.wait_ge(S["xn_hl_hi"], g * TG + j + 1)
                    last = v.tensor_tensor(XHL[:, j, D:2 * D], tile_of(g)(j), XHL[:, j, 0:D], ALU.subtract)
                last.then_inc(S["xn_hl_lo"], 1)
                if before:
                    ln_lo(U1, g - 1, g - 1)

            hold(v, S["x_loaded"], 16)
            stats(UX, 0, tile_of(0))
            first_norms(0, False, True)
            v.wait_ge(S["dst_loaded"], 16)
            v.tensor_copy(DSTF, DSTI).then_inc(S["list_step"], 1)
            v.wait_ge(S["list_step"], 1)
            for t in range(1, NT):
                v.tensor_scalar(JUNK[:, t, :], DSTF, float(t * TT), 0.0, ALU.is_lt, ALU.add,
                                accum_out=CNT[:, t:t + 1]).then_inc(S["cnt"], 1)
            v.wait_ge(S["cnt_mm"], 1)
            v.tensor_copy(SEG[:, :], TM[:, 0, 0:NT + 1]).then_inc(S["list_step"], 1)
            v.wait_ge(S["list_step"], 2)
            v.tensor_tensor(GRF[:, 0, 0:NT], SEG[:, 1:NT + 1], SEG[:, 0:NT], ALU.subtract).then_inc(S["list_step"], 1)
            v.wait_ge(S["list_step"], 3)
            v.tensor_scalar(GRI[:, :], GRF[:, 0, 0:NT], 1 / EG, 255 / 512, ALU.mult, ALU.add).then_inc(S["list_step"], 1)
            v.wait_ge(S["list_step"], 4)
            v.tensor_copy(GRF[:, 1, 0:NT], GRI[:, :]).then_inc(S["list_step"], 1)
            v.memset(GRF[:, 4, :], 1.0).then_inc(S["list_step"], 1)
            v.memset(GRF[:, 3, 0:1], 0.0).then_inc(S["list_step"], 1)
            v.wait_ge(S["list_step"], 7)
            v.tensor_tensor_scan(GRF[:, 2, 0:NT], GRF[:, 4, 0:NT], GRF[:, 1, 0:NT], 0.0, ALU.mult, ALU.add)\
                .then_inc(S["list_step"], 1)
            v.wait_ge(S["list_step"], 8)
            v.scalar_tensor_tensor(GRF[:, 3, 1:NT + 1], GRF[:, 2, 0:NT], -float(EG), SEG[:, 1:NT + 1], ALU.mult, ALU.add)\
                .then_inc(S["list_step"], 1)
            v.wait_ge(S["list_step"], 9)
            v.tensor_tensor(GRF[:, 0, 0:NT], GRF[:, 3, 1:NT + 1], GRF[:, 3, 0:NT], ALU.subtract).then_inc(S["list_step"], 1)
            v.wait_ge(S["consts"], 10)
            v.tensor_scalar(KIDX[:, 1, :], KIDX[:, 0, :], float(EG), None, ALU.mult).then_inc(S["list_step"], 1)
            v.wait_ge(S["list_step"], 10)
            for h in range(2):
                v.tensor_scalar(GMK[:, h, 0, :], GRF[:, 2, 0:NT], KIDX[:, 0, h:h + 1], None, ALU.is_le).then_inc(S["list_step"], 1)
                v.wait_ge(S["list_step"], 11 + 2 * h + 1)
                v.tensor_tensor(GMK[:, h, 1, :], GMK[:, h, 0, :], GRF[:, 0, 0:NT], ALU.mult).then_inc(S["list_step"], 1)
            v.wait_ge(S["list_step"], 15)
            for h in range(2):
                v.tensor_reduce(LSF[:, h, 1:2], GMK[:, h, 0, :], AX, ALU.add).then_inc(S["list_step"], 1)
                v.tensor_reduce(LSF[:, h, 0:1], GMK[:, h, 1, :], AX, ALU.add).then_inc(S["list_step"], 1)
            v.wait_ge(S["list_step"], 19)
            v.tensor_tensor(KIDX[:, 0, :], LSF[:, :, 0], KIDX[:, 1, :], ALU.add).then_inc(S["list_step"], 1)
            v.wait_ge(S["list_step"], 20)
            v.tensor_scalar(LSF[:, :, 0], KIDX[:, 0, :], float(EDGES), None, ALU.min).then_inc(S["g_list"], 1)
            v.wait_ge(S["cnt"], NT - 1)
            v.wait_ge(S["g_list"], 1)
            for w in range(2):
                for h in range(2):
                    v.tensor_scalar(DIAG[:, w, h, :], IDF[:, :], LSF[:, h, w:w + 1], None, ALU.mult).then_inc(S["g_list"], 1)
            v.wait_ge(S["prm0_loaded"], 48)
            v.tensor_scalar(BSF[:, 0:D], BSF[:, 0:D], W_UP, None, ALU.mult).then_inc(S["bias_step"], 1)
            v.tensor_reduce(EVEN[:, 0:1], IDF[:2 * L, 0:2 * L].rearrange("p (l w) -> p w l", w=2)[:, 0, :], AX, ALU.add).then_inc(S["bias_step"], 1)
            v.tensor_reduce(EVEN[:, 1:2], IDF[:2 * L, 0:2 * L].rearrange("p (l w) -> p w l", w=2)[:, 1, :], AX, ALU.add).then_inc(S["bias_step"], 1)
            v.wait_ge(S["bias_step"], 3)
            v.tensor_copy(BSH, BSF).then_inc(S["bias_step"], 1)
            v.wait_ge(S["bias_step"], 4)
            v.tensor_tensor(BSR, BSF, BSH, ALU.subtract).then_inc(S["bias_step"], 1)
            v.wait_ge(S["bias_step"], 5)
            v.tensor_scalar(BSR, BSR, EVEN[:, 1:2], None, ALU.mult).then_inc(S["bias_step"], 1)
            v.wait_ge(S["bias_step"], 6)
            v.scalar_tensor_tensor(BIAS[:, :], BSH, EVEN[:, 0:1], BSR, ALU.mult, ALU.add).then_inc(S["g_list"], 1)
            v.wait_ge(S["cnt_mm"], 2)
            v.tensor_copy(LROW[0:1, :], TM[0:1, 1, :]).then_inc(S["list_ready"], 1)
            v.tensor_scalar(TBF[:, :], TM[:, 1, 256:512], float(TT), None, ALU.mult).then_inc(S["list_ready"], 1)
            hold(v, S["list_ready"], 2)
            v.sem_inc(S["list_ready"], 1)

            with v.Fori(1, NG - 1) as g:
                first_norms(g, True, True)
            first_norms(NG - 1, True, False)
            v.wait_ge(U1.turned, 3 * (NG - 1) + 1)
            norm(U1, NG - 1, tile_of(NG - 1), lambda j: H1[:, j, :])
            hold(v, S["z_init"], NT)

            def one_hot(n, u):
                hold(v, idx_loaded[u], 32 * n + 32)
                for r in (2 * u, 2 * u + 1):
                    v.tensor_scalar(LOC[:, r, :], IDXR[:, r, :].rearrange("p (c w) -> p w c", w=2)[:, 1, :],
                                    TBF[:, ds(n * RING + r, 1)], None, ALU.subtract).then_inc(S["oh_loc"], 1)
                v.wait_ge(S["agg_mm"], n * RING + 2 * u + 2)
                for r in (2 * u, 2 * u + 1):
                    v.wait_ge(S["oh_loc"], (n + 1) * RING + r + 1)
                    for c in range(2):
                        last = v.tensor_scalar(OH[:, r, c, :], IOTA[:, :], LOC[:, r, c:c + 1], None, ALU.is_equal)
                    last.then_inc(S["oh_done"], 1)

            def sums(n, u):
                for h in range(2):
                    r = 2 * u + h
                    tile = v.value_load(LROW[0:1, ds(256 + (n * RING + r), 1)], min_val=0, max_val=NT)
                    z = Z[:, ds(tile * D, D)]
                    v.wait_ge(S["agg_mm"], (n + 1) * RING + 2 * u + 2)
                    v.wait_ge(S["agg_add"], n * RING + r + 1)
                    v.tensor_tensor(z, TM[:TT, u % 2, h * D:(h + 1) * D], z, ALU.add).then_inc(S["agg_add"], 1)

            def q_lo(g, n, pairs=(0, 1, 2)):
                for i in pairs:
                    off, w = PAIRS[i]
                    v.wait_ge(S["q_hi"], 3 * n + i + 1)
                    v.scalar_tensor_tensor(FT[:, 1, :, ds(g * GT + off, w)],
                                           PT[:, i % 2, 0:500].rearrange("p (c w) -> p c w", c=KC)[:, :, :w], W_UP,
                                           FT[:, 0, :, ds(g * GT + off, w)], ALU.mult, ALU.subtract)\
                        .then_inc(S["q_lo"], 1)

            def phase_a(g, n, with_q, with_ln=False):
                if with_q:
                    q_lo(g - 1, n - 1, (0, 1))
                v.wait_ge(S["k_evac"], 4 * n + 5)
                v.tensor_reduce(KMX[:, :, ds(g, 1)].rearrange("p c a -> p (c a)"), KR[:, :, ds(g * GT, GT)], AX, ALU.max)\
                    .then_inc(S["k_max"], 1)
                v.wait_ge(S["q_norm"], n * TG + 1)
                for j in range(TG + 1):
                    if j < TG:
                        q = TM[:TT, j % 2, 0:D].rearrange("p (h c) -> p h c", h=HEADS)
                        v.wait_ge(S["v_hi"], n * TG + j + 1)
                        v.tensor_reduce(QMX[:, j, :], q, AX, ALU.max).then_inc(S["q_max"], 1)
                        v.tensor_tensor(V[:, 1, ds(g * (TG * D) + j * D, D)], TM[:TT, j % 2, D:2 * D],
                                        V[:, 0, ds(g * (TG * D) + j * D, D)], ALU.subtract)
                        v.wait_ge(S["q_max"], n * TG + j + 1)
                        v.tensor_tensor(QS[:, j, :].rearrange("p (h c) -> p h c", h=HEADS), q,
                                        QMX[:, j, :].unsqueeze(2).to_broadcast([TT, HEADS, DH]), ALU.subtract)\
                            .then_inc(S["qv_evac"], 1)
                    if j == 0 and with_q:
                        q_lo(g - 1, n - 1, (2,))
                    if j in (2, 3) and with_ln:
                        ln_lo(U1, n + NG - 1, NG - 1, (0, 1) if j == 2 else (2,))
                    if j >= 1:
                        v.wait_ge(S["q_exp"], n * TG + j)
                        v.tensor_reduce(QSUM[:, j - 1, :], QS[:, j - 1, :].rearrange("p (h c) -> p h c", h=HEADS),
                                        AX, ALU.add).then_inc(S["q_sum"], 1)
                        v.wait_ge(S["q_sum"], n * TG + j)
                        v.reciprocal(RINV[:, j - 1, :], QSUM[:, j - 1, :]).then_inc(S["q_rinv"], 1)

            A_S, F_S = 1 / (W_UP * W_UP), 1 / W_UP

            def residual(n, g, done, scale, evac, j):
                x = X[:, ds(g * (TG * D) + j * D, D)]
                v.wait_ge(done, n * TG + j + 1)
                v.scalar_tensor_tensor(x, TM[:TT, j % 2, :D], scale, x, ALU.mult, ALU.add).then_inc(evac, 1)

            def tile_stats(U, u, g, evac, n, j):
                hold(v, evac, n * TG + j + 2)
                v.bn_stats(U.ST[:, j, :], X[:, ds(g * (TG * D) + j * D, D)]).then_inc(U.stats, 1)

            def moments(U, u):
                hold(v, U.stats, u * TG + TG)
                for j in range(TG):
                    v.bn_aggr(U.MV[:, j, :], U.ST[:, j, :]).then_inc(U.moments, 1)

            def normalise(U, u, g, H):
                v.wait_ge(U.turned, 3 * u + 1)
                norm(U, u, lambda j: X[:, ds(g * (TG * D) + j * D, D)], lambda j: H[:, j, :])

            def gelu_lo(n, m):
                for p, (off, w) in enumerate(PARTS):
                    v.wait_ge(S["g_hi"], 32 * n + 2 * (2 * m + p) + 2)
                    v.tensor_tensor(HID[:, 1, m, off:off + w], FFP[:, 2 * (m % 2) + p, :w],
                                    HID[:, 0, m, off:off + w], ALU.subtract).then_inc(S["g_lo"], 1)

            def step(g, n, before, after):
                ao = lambda j: residual(n + 1, g + 1, S["ao_mm"], A_S, S["ao_evac"], j)
                st2 = lambda j: tile_stats(U2, n + 1, g + 1, S["ao_evac"], n + 1, j)
                out = lambda j: residual(n, g, S["f2_mm"], F_S, S["f2_evac"], j)
                st1 = lambda j: tile_stats(U1, n + NG, g, S["f2_evac"], n, j)
                lo1 = lambda i: ln_lo(U1, n + NG - 1, g - 1, (i,)) if before else None
                lo2 = lambda i: ln_lo(U2, n + 1, g + 1, (i,)) if after else None
                for m in range(FC):
                    gelu_lo(n, m)
                    if m == 0 and before:
                        normalise(U1, n + NG - 1, g - 1, H1)
                    if 1 <= m <= NPAIR:
                        sums(n, m - 1)
                    if 3 <= m <= 5 and after:
                        one_hot(n + 1, m - 3)
                if after:
                    ao(0)
                    ao(1)
                    lo1(0)
                    ao(2)
                    st2(0)
                    st2(1)
                    ao(3)
                    st2(2)
                    ao(4)
                    lo1(1)
                    st2(3)
                    st2(4)
                    moments(U2, n + 1)
                else:
                    lo1(0)
                    lo1(1)
                lo1(2)
                out(0)
                if after:
                    normalise(U2, n + 1, g + 1, H2)
                    one_hot(n + 1, 3)
                out(1)
                st1(0)
                if after:
                    one_hot(n + 1, 4)
                out(2)
                st1(1)
                lo2(0)
                lo2(1)
                if after:
                    one_hot(n + 1, 5)
                out(3)
                st1(2)
                lo2(2)
                out(4)
                st1(3)
                st1(4)
                moments(U1, n + NG)

            with v.Fori(0, L) as l:
                n0 = l * NG
                phase_a(0, n0, False, True)
                with v.Fori(1, NG) as g:
                    phase_a(g, l * NG + g, True)
                v.wait_ge(S["k_max"], n0 + NG)
                v.tensor_reduce(KM[:, :], KMX[:, :, :], AX, ALU.max).then_inc(S["kmax_all"], 1)
                v.memset(CTXA[:, :, :], 0.0).then_inc(S["ctx_zero"], 1)
                v.wait_ge(S["kmax_all"], l + 1)
                v.tensor_scalar(NKB[:, :], KM[:, :], -SCALE / W_UP, None, ALU.mult).then_inc(S["k_bias"], 1)
                hold(v, S["ctx_zero"], l + 1)
                def kt_lo(g, m):
                    v.wait_ge(S["kt_hi"], (l * NG + g) * KC + m + 1)
                    v.scalar_tensor_tensor(KT[:, 1, m, :, :], KTP[m], K_UP, KT[:, 0, m, :, :], ALU.mult, ALU.subtract)\
                        .then_inc(S["kt_lo"], 1)

                def ctx_add(g, m):
                    b = (l * NG + g) * KC
                    v.wait_ge(S["ctx_mm"], b + m + 3)
                    v.wait_ge(S["ctx_acc"], b + m + 1)
                    v.tensor_tensor(CTXA[:, m, :], TM[:, m, :P], CTXA[:, m, :], ALU.add).then_inc(S["ctx_acc"], 1)

                kt_lo(0, 0)
                q_lo(NG - 1, n0 + NG - 1)
                ctx_add(0, 0)
                kt_lo(0, 1)
                with v.Fori(1, NG) as g:
                    kt_lo(g, 0)
                    ctx_add(g - 1, 1)
                    kt_lo(g, 1)
                    ctx_add(g, 0)
                ctx_add(NG - 1, 1)
                v.wait_ge(S["ke"], (n0 + NG) * KC)
                v.tensor_reduce(RKS[:, 0, :], KSUM[:, :, :], AX, ALU.add).then_inc(S["m_lo"], 1)
                v.wait_ge(S["m_lo"], 6 * l + 1)
                v.reciprocal(RKS[:, 1, :], RKS[:, 0, :]).then_inc(S["m_lo"], 1)
                v.wait_ge(S["m_lo"], 6 * l + 2)
                v.wait_ge(S["ctx_acc"], (n0 + NG) * KC + 2)
                v.scalar_tensor_tensor(CTXM[:, :, :], CTXA[:, :, :], C_DOWN, MASK[:, :].unsqueeze(1).to_broadcast([P, KC, P]),
                                       ALU.mult, ALU.mult).then_inc(S["ctx_lo"], 1)
                v.wait_ge(S["ctx_lo"], 3 * l + 1)
                v.tensor_copy(CTX[:, 0, :, :], CTXM[:, :, :]).then_inc(S["ctx_lo"], 1)
                v.wait_ge(S["ctx_lo"], 3 * l + 2)
                v.tensor_tensor(CTX[:, 1, :, :], CTXM[:, :, :], CTX[:, 0, :, :], ALU.subtract).then_inc(S["ctx_lo"], 1)
                v.wait_ge(S["m_mm"], l + 1)
                for m in range(KC):
                    v.tensor_scalar(M[:, 0, m, :], FFP[:, 0, m * D:(m + 1) * D], RKS[:, 1, m:m + 1], None, ALU.mult)\
                        .then_inc(S["m_lo"], 1)
                for m in range(KC):
                    v.wait_ge(S["m_lo"], 6 * l + 3 + m)
                    v.scalar_tensor_tensor(M[:, 1, m, :], FFP[:, 0, m * D:(m + 1) * D], RKS[:, 1, m:m + 1],
                                           M[:, 0, m, :], ALU.mult, ALU.subtract).then_inc(S["m_lo"], 1)
                for j in range(TG + 1):
                    if j < TG:
                        residual(n0, 0, S["ao_mm"], A_S, S["ao_evac"], j)
                    if j >= 1:
                        tile_stats(U2, n0, 0, S["ao_evac"], n0, j - 1)
                moments(U2, n0)
                normalise(U2, n0, 0, H2)
                ln_lo(U2, n0, 0)
                for u in range(NPAIR):
                    one_hot(n0, u)
                step(0, n0, False, True)
                with v.Fori(1, NG - 1) as g:
                    step(g, l * NG + g, True, True)
                n4 = n0 + NG - 1
                step(NG - 1, n4, True, False)
                normalise(U1, n4 + NG, NG - 1, H1)

            v.wait_ge(U1.h, (L + 1) * NT)
            hold(v, S["agg_add"], L * NG * RING + 1)
            with v.Fori(0, NG) as g:
                v.wait_ge(S["z_turned"], 3 * g + 1)
                v.tensor_copy(H1[:, :, :], Z[:, ds(g * (TG * D), TG * D)].rearrange("p (j d) -> p j d", j=TG)).then_inc(S["zs"], 1)
                for m in range(GC):
                    for p, (off, w) in enumerate(PARTS):
                        hold(v, S["t_evac"], 8 * g + 2 * m + p + 5)
                        v.bn_stats(BST[:, m, ds(g * 12 + p * 6, 6)], TH[:, m, ds(g * GT + off, w)]).then_inc(S["t_stat"], 1)
            v.wait_ge(S["t_stat"], NG * GC * 2)
            for m in range(GC):
                v.bn_aggr(BMV[:, m, :], BST[:, m, :]).then_inc(S["bn_mv"], 1)
            hold(v, S["bn_b"], 1)
            v.sem_inc(S["xhl_used"], 1)
            with v.Fori(0, NG) as g:
                for m in range(GC):
                    v.wait_ge(S["th_hi"], g * GC + m + 1)
                    v.tensor_tensor(HID[:, 1, m, :], TH[:, m, ds(g * GT, GT)], HID[:, 0, m, :], ALU.subtract)\
                        .then_inc(S["th_lo"], 1)
                for m in range(KC):
                    for p, (off, w) in enumerate(PARTS):
                        hold(v, S["y_evac"], 4 * g + 2 * m + p + 5)
                        v.bn_stats(BST[:, m, ds(g * 12 + p * 6, 6)], Y[:, m, ds(g * GT + off, w)]).then_inc(S["y_stat"], 1)
                v.sem_inc(S["xhl_used"], 1)
            v.wait_ge(S["y_stat"], NG * KC * 2)
            for m in range(KC):
                v.bn_aggr(BMV[:, m, :], BST[:, m, :]).then_inc(S["bn_mv"], 1)
            hold(v, S["bn_mv"], GC + KC)
            with v.Fori(0, NG) as g:
                for j in range(TG):
                    x = X[:, ds(g * (TG * D) + j * D, D)]
                    if j == 0:
                        v.wait_ge(S["x_plus"], g + 1)
                    v.wait_ge(S["r_turned"], g * TG + j + 2)
                    v.tensor_tensor(x, TM[:TT, j % 2, :D], x, ALU.add).then_inc(S["x1"], 1)
            hold(v, S["x1"], NT + 1)
            with v.Fori(0, NG) as g:
                tile = lambda j: X[:, ds(g * (TG * D) + j * D, D)]
                stats(U3, g, tile)
                v.wait_ge(U3.turned, 3 * g + 1)
                v.wait_ge(S["x_tok"], g + 1)
                norm(U3, g, tile, lambda j: H1[:, j, :])
                for i, (off, w) in enumerate(PAIRS):
                    v.wait_ge(U3.hi, 3 * g + i + 1)
                    v.tensor_tensor(FT[:, 1, :, ds(g * GT + off, w)],
                                    PT[:, i % 2, 0:500].rearrange("p (c w) -> p c w", c=KC)[:, :, :w],
                                    FT[:, 0, :, ds(g * GT + off, w)], ALU.subtract).then_inc(U3.lo, 1)
                v.wait_ge(S["log_mm"], g + 1)
                v.tensor_scalar(LG[:, ds(g * TG, TG), :].rearrange("p t e -> p (t e)"), TM[:TT, 0, 0:TG * E], 1 / W_UP, None,
                                ALU.mult).then_inc(S["log"], 1)
            wide = lambda k: RT[:, k, :, :]
            per = lambda k: RM[:, k, :].unsqueeze(2).to_broadcast([TT, NT, E])
            r8 = R8[:, :].unsqueeze(1).to_broadcast([TT, NT, E])
            v.wait_ge(S["log"], NG + 1)
            v.tensor_reduce(RM[:, 0, :], LG[:, :, :], AX, ALU.max).then_inc(S["rt"], 1)
            v.wait_ge(S["rt"], 1)
            v.tensor_tensor(wide(0), LG[:, :, :], per(0), ALU.subtract).then_inc(S["rt"], 1)
            v.wait_ge(S["rt"], 3)
            v.tensor_reduce(RM[:, 1, :], wide(1), AX, ALU.add).then_inc(S["rt"], 1)
            v.wait_ge(S["rt"], 4)
            v.reciprocal(RM[:, 2, :], RM[:, 1, :]).then_inc(S["rt"], 1)
            v.wait_ge(S["rt"], 5)
            v.tensor_tensor(wide(2), wide(1), per(2), ALU.mult).then_inc(S["rt"], 1)
            n = 6
            src = 2
            for k in range(2):
                v.wait_ge(S["rt"], n)
                v.tensor_reduce(RM[:, 3 + k, :], wide(src), AX, ALU.max).then_inc(S["rt"], 1)
                v.wait_ge(S["rt"], n + 1)
                v.tensor_tensor(wide(3), wide(src), per(3 + k), ALU.is_equal).then_inc(S["rt"], 1)
                v.wait_ge(S["rt"], n + 2)
                v.tensor_tensor(wide(4), wide(3), r8, ALU.mult).then_inc(S["rt"], 1)
                v.wait_ge(S["rt"], n + 3)
                v.tensor_reduce(RM[:, 5, :], wide(4), AX, ALU.max).then_inc(S["rt"], 1)
                v.wait_ge(S["rt"], n + 4)
                v.tensor_tensor(wide(5 + k), wide(4), per(5), ALU.is_equal).then_inc(S["rt"], 1)
                n += 5
                if k == 0:
                    v.wait_ge(S["rt"], n)
                    v.scalar_tensor_tensor(wide(7), wide(5), -2.0, wide(2), ALU.mult, ALU.add).then_inc(S["rt"], 1)
                    n += 1
                    src = 7
            v.wait_ge(S["rt"], n)
            v.tensor_tensor(RM[:, 0, :], RM[:, 3, :], RM[:, 4, :], ALU.add).then_inc(S["rt"], 1)
            v.tensor_tensor(wide(0), wide(5), wide(6), ALU.add).then_inc(S["rt"], 1)
            v.wait_ge(S["rt"], n + 2)
            v.tensor_scalar(RM[:, 1, :], RM[:, 0, :], 1e-12, None, ALU.max).then_inc(S["rt"], 1)
            v.tensor_tensor(wide(1), wide(0), wide(2), ALU.mult).then_inc(S["rt"], 1)
            v.wait_ge(S["rt"], n + 4)
            v.reciprocal(RM[:, 2, :], RM[:, 1, :]).then_inc(S["rt"], 1)
            v.wait_ge(S["rt"], n + 5)
            v.tensor_tensor(wide(3), wide(1), per(2), ALU.mult).then_inc(S["rt"], 1)
            v.wait_ge(S["rt"], n + 6)
            v.tensor_scalar(CB[:, :, :], wide(3), 1 / W_UP, None, ALU.mult).then_inc(S["comb"], 1)
            hold(v, S["comb"], 1)
            with v.Fori(0, NG) as g:
                v.wait_ge(S["ct"], 2 * g + 1)
                v.tensor_copy(CBG, RT[:, 3, ds(g * TG, TG), :].rearrange("p t e -> p (t e)")).then_inc(S["cbg"], 1)
                for j in range(TG):
                    x = X[:, ds(g * (TG * D) + j * D, D)]
                    if j == 0:
                        v.wait_ge(S["x_tok"], g + 2)
                    v.wait_ge(S["cb_mm"], g * TG + j + 2)
                    v.tensor_tensor(x, TM[:TT, j % 2, :D], x, ALU.add).then_inc(S["cb_add"], 1)
            hold(v, S["cb_add"], NT + 1)
            with v.Fori(0, NG) as g:
                with v.Fori(0, E // 2) as h:
                    for q in range(2):
                        x = g * E + h * 2 + q
                        for m in range(KC):
                            for p, (off, w) in enumerate(PARTS):
                                v.wait_ge(S["eg_hi"], 8 * x + 4 * m + 2 * p + 2)
                                v.tensor_tensor(HID[:, 1, 2 * q + m, off:off + w], FFP[:, 2 * m + p, :w],
                                                HID[:, 0, 2 * q + m, off:off + w], ALU.subtract).then_inc(S["eg_lo"], 1)
                    for q in range(2):
                        e, x = h * 2 + q, g * E + h * 2 + q
                        for j in range(TG):
                            xt_ = X[:, ds(g * (TG * D) + j * D, D)]
                            v.wait_ge(S["e2_mm"], x * TG + j + 1)
                            v.wait_ge(S["e_out"], x * TG + 1)
                            v.scalar_tensor_tensor(xt_, TM[:TT, j % 2, :D],
                                                   CB[:, :, :].rearrange("p t e -> p (t e)")[:, ds(g * (TG * E) + e + j * E, 1)],
                                                   xt_, ALU.mult, ALU.add).then_inc(S["e_out"], 1)


_SHAPES = {}


def kernel(**inputs):
    import numpy as np
    import concourse.bacc as bacc
    from concourse.bass_utils import run_bass_kernel_spmd

    i = {k: np.asarray(v) for k, v in inputs.items()}

    def cols(w):
        w = w.reshape(*w.shape[:-2], w.shape[-2] // P, P, w.shape[-1])
        w = np.moveaxis(w, -3, -2)
        return w.reshape(*w.shape[:-2], -1)

    def pad(w, n):
        return np.concatenate([w, np.zeros((*w.shape[:-1], n - w.shape[-1]), w.dtype)], -1)

    wa = pad(np.concatenate([cols(np.concatenate([i["L0_mix_Wq"], i["L0_mix_Wv"]], -1)), cols(i["L0_mix_Wk"]),
                             cols(i["L0_mix_Wo"])], -1), WA)
    wa = np.concatenate([wa, pad(cols(i["L0_gnn_W2"]), WA)[None]], 0)
    wb = pad(np.concatenate([cols(i["L0_mix_W1"]), cols(i["L0_mix_W2"])], -1), WB)

    def vec(b):
        return np.swapaxes(b.reshape(*b.shape[:-1], -1, P), -1, -2)

    g1, b1 = vec(i["L0_mix_ln1_g"]), vec(i["L0_mix_ln1_b"])
    nxt = lambda t: np.concatenate([t[1:], np.zeros_like(t[:1])], 0)
    prm = np.concatenate([nxt(g1), nxt(b1), vec(i["L0_mix_ln2_g"]), vec(i["L0_mix_ln2_b"]), vec(i["L0_mix_b1"]), g1, b1], -1)
    data = {
        "x": i["x"],
        "prm0": np.concatenate([g1[0], b1[0]], -1),
        "prm": prm,
        "bias": np.repeat(np.concatenate([i["L0_mix_bo"], i["L0_mix_b2"]], -1), 2, axis=0),
        "eps": i["L0_gnn_eps_gin"].reshape(1, 1),
        "wa": wa.reshape(L + 1, P, NG, WAS),
        "wb": wb.reshape(L, P, NG, WBS),
        "dst": i["dst"].reshape(TT, ER),
        "edges": np.concatenate([np.stack([i["src"], i["dst"]], -1), np.zeros((EG, 2), i["src"].dtype)], 0),
        "gw1": cols(i["L0_gnn_W1"]),
        "gprm": np.concatenate([vec(i["L0_gnn_" + k]) for k in ("b1", "g1", "bt1", "b2", "g2", "bt2")], -1),
        "rw": cols(i["L0_ffn_router_w"].T),
        "eb1": np.moveaxis(vec(i["L0_ffn_b1"]), 1, 0).reshape(P, -1), "eb2": i["L0_ffn_b2"],
        "mw": pad(np.moveaxis(np.concatenate([cols(i["L0_ffn_w1"]), cols(i["L0_ffn_w2"])], -1), 1, 0).reshape(P, -1), 8195)
        .reshape(P, NG, -1),
    }
    data = {k: np.ascontiguousarray(w) for k, w in data.items()}
    nc = bacc.Bacc("TRN2", target_bir_lowering=False, num_devices=1)
    aps = {k: nc.dram_tensor(f"in_{k}", w.shape, mybir.dt.from_np(w.dtype), kind="ExternalInput").ap()
           for k, w in data.items()}
    aps["xn_hl"] = nc.dram_tensor("xn_hl", [N, 2 * D], F16).ap()
    aps["out"] = nc.dram_tensor("out_0", [N, D], F32, kind="ExternalOutput").ap()
    build(nc, aps, stop=STOP)
    r = run_bass_kernel_spmd(nc, [{f"in_{k}": w for k, w in data.items()}], core_ids=[0])
    return r.results[0]["out_0"]


STOP = ""
```

```python
from contextlib import ExitStack

import concourse.bass as bass
from concourse import mybir

F32 = mybir.dt.float32
F16 = mybir.dt.float16
I32 = mybir.dt.int32
U32 = mybir.dt.uint32
ALU = mybir.AluOpType
ACT = mybir.ActivationFunctionType
AX = mybir.AxisListType.X
ds = bass.ds

N, D, L, E = 3125, 256, 4, 8
P = 128
TT = 125
TG = 5
GT = TT * TG
NG = N // GT
NT = N // TT
KC = D // P
FF = 4 * D
FC = FF // P
HEADS, DH = 8, 32
SCALE = DH ** -0.25
EPS = 1e-5
EDGES = 50000
ER = EDGES // TT
EC = 4
EG = EC * P
UNITS = EDGES // EG + NT
NA = 8
RING = 6
EXTRA = UNITS - L * NG * RING
assert 0 < EXTRA <= 2
GF = 2 * D
GC = GF // P

W_UP = 64.0
K_UP = 256.0
C_DOWN = 1.0 / (W_UP * K_UP)
PARTS = ((0, 375), (375, 250))
PAIRS = ((0, 250), (250, 250), (500, 125))
PASSES = ((0, 0), (0, 1), (1, 0))

QV0, K0, WO0, WA = 0, KC * 2 * D, KC * 3 * D, 2050
W10, W20, WB = 0, KC * FF, 4100
WAS, WBS = WA // NG, WB // NG
NPRM = 6 * KC + FC
MWC = 8195
MWS = MWC // NG


def build(nc, a):
    ctx = ExitStack()
    with ctx:
        def sb(name, shape, dt):
            return ctx.enter_context(nc.sbuf_tensor(name, shape, dt))

        def sem(name):
            return ctx.enter_context(nc.semaphore(name))

        X = sb("X", [TT, NT * D], F32)
        Z = sb("Z", [TT, (NT + 1) * D], F32)
        ft32 = sb("FT", [P, KC * N], F32)[:, :]
        FT = ft32.bitcast(F16).rearrange("p (s c n) -> p s c n", s=2, c=KC)
        KV = sb("KV", [P, 12800], F32)
        WAs = sb("WAs", [P, 2, WA], F16)
        wb32 = sb("WBs", [P, WB], F32)[:, :]
        hid32 = sb("HID", [P, FC * GT], F32)[:, :]
        WBs = wb32.bitcast(F16).rearrange("p (s n) -> p s n", s=2)
        HID = hid32.bitcast(F16).rearrange("p (s c n) -> p s c n", s=2, c=FC)
        H1 = sb("H1", [TT, TG, D], F32)
        QS = sb("QS", [TT, TG, D], F32)
        H2 = QS
        QN = sb("QN", [TT, TG, D], F32)
        STA = sb("STA", [P, WAS], F32)
        STB = sb("STB", [P, WBS], F32)
        BIAS = sb("BIAS", [2 * L, 2 * D], F16)
        SEL = sb("SEL", [2 * L, L, TT], F16)
        PRM = sb("PRM", [P, NPRM], F32)
        PR0 = sb("PR0", [P, 2 * KC], F32)
        IDF = sb("IDF", [P, P], F32)
        MASK = sb("MASK", [P, P], F32)
        EPSB = sb("EPSB", [TT, 2], F32)
        EXPO = sb("EXPO", [P, 8], F32)
        QMX = sb("QMX", [TT, TG, HEADS], F32)
        QSUM = sb("QSUM", [TT, TG, HEADS], F32)
        RINV = sb("RINV", [TT, TG, HEADS], F32)
        KMX = sb("KMX", [P, KC, 3], F32)
        KM = sb("KM", [P, KC], F32)
        NKB = sb("NKB", [P, KC], F32)
        KDIF = sb("KDIF", [P, KC], F32)
        FAC = sb("FAC", [P, KC], F32)
        KSG = sb("KSG", [P, KC, 3], F32)
        KS = sb("KS", [P, KC], F32)
        RKS = sb("RKS", [P, KC], F32)
        CTXA = hid32[:, 3500:3500 + KC * P].rearrange("p (c n) -> p c n", c=KC)
        CTXM = hid32[:, 3200:3200 + KC * P].rearrange("p (c n) -> p c n", c=KC)
        CTX = hid32[:, 4000:4000 + KC * P].bitcast(F16).rearrange("p (s c n) -> p s c n", s=2, c=KC)
        M = sb("M", [P, 2, KC, D], F16)

        V0 = 11400
        V = KV[:TT, V0:V0 + TG * D].bitcast(F16).rearrange("p (s n) -> p s n", s=2)
        KE = hid32[:, 0:KC * GT].rearrange("p (c n) -> p c n", c=KC)
        KT = hid32[:TT, KC * GT:KC * GT + 2 * TG * P].bitcast(F16).rearrange(
            "p (s m j c) -> p s m j c", s=2, m=KC, j=TG)
        XIN = QS
        DSTI, DSTF = KV[:TT, 0:ER].bitcast(I32), KV[:TT, ER:2 * ER]
        EDGI = hid32[:, 2750:2750 + NT + 1].bitcast(I32)
        EDGF = sb("EDGF", [P, NT + 1], F32)[:, :]
        JUNK = KV[:TT, 2 * ER:2 * ER + NT * ER // 2].bitcast(F16).rearrange("p (t n) -> p t n", t=NT)
        XNH = KV[:TT, 12800 - NT * D:12800].bitcast(F16)
        ONES = hid32[:, 2800:2800 + P]
        CNT = sb("CNT", [TT, NT + 1], F32)
        SEG = sb("SEG", [P, NT + 1], F32)
        SEGI = sb("SEGI", [P, NT + 1], I32)
        GRI = sb("GRI", [P, NT], I32)
        GRF = hid32[:, 2400:2400 + 5 * (NT + 1)].rearrange("p (k t) -> p k t", k=5)
        KIDI = sb("KIDI", [P, 2], I32)
        KIDX = sb("KIDX", [P, 2, 2], F32)
        GMK = hid32[:, 2600:2600 + 4 * NT].rearrange("p (h k t) -> p h k t", h=2, k=2)
        LSF = sb("LSF", [P, 2, 2], F32)
        LROW = sb("LROW", [1, 512], I32)
        DIAG = KV[:, 0:512].rearrange("p (w h n) -> p w h n", w=2, h=2)
        TBF = sb("TBF", [P, 256], F32)
        IOTI = hid32[:, 0:TT].bitcast(I32)
        SELF = hid32[:2 * L, 200:200 + L * TT].rearrange("p (l c) -> p l c", l=L)
        BSF = hid32[:2 * L, 800:800 + 2 * D]
        BSR = hid32[:2 * L, 1400:1400 + 2 * D]
        BSH = hid32[:2 * L, 2000:2000 + D].bitcast(F16)
        EVEN = hid32[:2 * L, 2300:2302]
        IOTA = sb("IOTA", [P, TT], F16)
        IDXR = sb("IDXR", [P, RING, 2 * EC], I32)
        LOC = sb("LOC", [P, RING, EC], F32)
        OH = sb("OH", [P, RING, EC, TT], F16)
        GAT = KV[:, 0:RING * EC * D].bitcast(F16).rearrange("p (r c n) -> p r c n", r=RING, c=EC)
        GPR = sb("GPR", [P, 3 * GC + 3 * KC], F32)
        GW1 = wb32[:, 0:KC * GF]
        TH = KV[:, 0:GC * N].rearrange("p (c n) -> p c n", c=GC)
        ZT = hid32[:, 0:2 * KC * GT].rearrange("p (u c n) -> p u c n", u=2, c=KC)
        Y = TH[:, GC - KC:, :]
        BST = wb32[:, 3640:3640 + GC * 12 * NG].rearrange("p (c n) -> p c n", c=GC)
        BMV = sb("BMV", [P, GC, 2], F32)
        BVE = sb("BVE", [P, 4, GC], F32)
        ID64 = sb("ID64", [TT, TT], F16)
        MW = KV[:, 0:MWC].bitcast(F16).rearrange("p (s n) -> p s n", s=2)
        STM = wb32[:, KC * GF:KC * GF + MWS]
        RW = sb("RW", [P, 2, KC * E], F16)
        RWF = wb32[:, 3600:3600 + 2 * KC * E].rearrange("p (s n) -> p s n", s=2)
        EB1 = sb("EB1", [P, E * KC], F32)
        EB2 = wb32[:E, 3300:3300 + D]
        LG = Z[:, 0:NT * E].rearrange("p (t e) -> p t e", e=E)
        RT = Z[:, NT * E:9 * NT * E].rearrange("p (k t e) -> p k t e", k=8, e=E)
        RM = Z[:, 2000:2000 + 6 * NT].rearrange("p (k t) -> p k t", k=6)
        R8 = sb("R8", [TT, E], F32)
        R8I = sb("R8I", [TT, E], I32)
        CB = Z[:, 9 * NT * E:10 * NT * E].rearrange("p (t e) -> p t e", e=E)
        CBG = wb32[:TT, 3560:3560 + TG * E]
        CT = wb32[:E, 2670:2670 + GT]
        XHL2 = (QN[:, :, :].bitcast(F16), QS[:, :, :].bitcast(F16))

        FFP = ctx.enter_context(nc.psum_tensor("FFP", [P, 4, 512], F32))
        PT = ctx.enter_context(nc.psum_tensor("PT", [P, 2, 512], F32))
        TM = ctx.enter_context(nc.psum_tensor("TM", [P, 2, 512], F32))

        KTP = [b.rearrange("p b c -> p (b c)")[:TT, :TG * P].rearrange("p (j c) -> p j c", j=TG)
               for b in (FFP[:, 0:2, :], FFP[:, 2:4, :])]

        class Unit:
            def __init__(self, k):
                self.ST = sb(f"ST{k}", [TT, TG, 6], F32)
                self.MV = sb(f"MV{k}", [TT, TG, 2], F32)
                self.VE = sb(f"VE{k}", [TT, TG], F32)
                self.RS = sb(f"RS{k}", [TT, TG], F32)
                self.MR = sb(f"MR{k}", [TT, TG], F32)
                self.stats = sem(f"ln{k}_stats")
                self.moments = sem(f"ln{k}_moments")
                self.scales = sem(f"ln{k}_scales")
                self.h = sem(f"ln{k}_h")
                self.turned = sem(f"ln{k}_turned")
                self.hi = sem(f"ln{k}_hi")
                self.lo = sem(f"ln{k}_lo")

        UX, U1, U2, U3 = Unit("x"), Unit("1"), Unit("2"), Unit("3")

        names = """edge_consts dst_float list_step bn_step x_loaded xn_hl_hi xn_hl_lo xn_stored z_init ctx_scl fac ctx_turned k_sum consts consts0 prm0_loaded prm_loaded wa_loaded wa_used wa_split wb_loaded wb_used wb_split k_mm k_max v_hi q_max qv_mm qv_evac q_exp q_sum q_rinv q_norm q_turned q_hi q_lo ke ke_turned kt_hi kt_lo ctx_zero ctx_mm ctx_acc ctx_lo m_mm m_hi m_lo ao_mm ao_evac f1_mm g_hi g_lo f2_mm f2_evac eps_ready out_stored held dst_loaded cnt cnt_mm g_list list_ready consts1 bias_step oh_loc oh_done agg_mm agg_add gw_loaded zs z_turned zt t_mm t_evac t_stat bn_mv bn_b xhl_loaded xhl_used th_relu th_hi th_lo y_mm y_evac y_stat r_relu r_turned x1 x_in_loaded x_in_used x_plus mw_loaded mw_used mw_split rw_lo x_tok log_mm log rt comb cbg cb_turned ct cb_mm cb_add e1_mm eg_hi eg_lo e2_mm e_out""".split()
        S = {n: sem(n) for n in names}
        idx_loaded = [sem(f"idx_loaded{u}") for u in range(RING)]
        gathered = [sem(f"gathered{u}") for u in range(RING)]

        block = ctx.enter_context(nc.Block())

        def by_twos(engine, body):
            with engine.Fori(0, NG // 2) as i:
                for u in range(2):
                    body(2 * i + u, u, False)
            body(NG - 1, (NG - 1) % 2, True)

        def hold(engine, semaphore, value):
            engine.wait_ge(semaphore, value)
            engine.sem_inc(S["held"], 1)

        def xt(t):
            return X[:, ds(t * D, D)]

        def ft(part, k, off, w):
            return FT[:, part, k, ds(off, w)]

        @block.sync
        def _(sp):
            sp.dma_start(X[:, 0:TG * D].rearrange("p (j d) -> p j d", j=TG),
                         a["x"][0:GT, :].rearrange("(j p) d -> p j d", j=TG)).then_inc(S["x_loaded"], 16)
            sp.dma_start(DSTI, a["dst"]).then_inc(S["dst_loaded"], 16)
            sp.dma_start(PR0[:, :], a["prm0"]).then_inc(S["prm0_loaded"], 16)
            sp.dma_start(EPSB[:, 0:1], a["eps"].broadcast_to([TT, 1])).then_inc(S["prm0_loaded"], 16)
            sp.dma_start(BSF, a["bias"]).then_inc(S["prm0_loaded"], 16)

            def load_x(g):
                sp.dma_start(X[:, ds(g * (TG * D), TG * D)].rearrange("p (j d) -> p j d", j=TG),
                             a["x"].rearrange("(g j p) d -> g p j d", g=NG, j=TG)[ds(g, 1)]
                             .rearrange("a p j d -> p (a j) d")).then_inc(S["x_loaded"], 16)

            def load_wa0(g):
                sp.wait_ge(S["wa_used"], g + 1)
                sp.dma_start(STA[:, :], a["wa"][0, :, ds(g, 1), :].rearrange("p a c -> p (a c)"))\
                    .then_inc(S["wa_loaded"], 16)

            def store_xn(g):
                sp.wait_ge(S["xn_hl_lo"], g + 1)
                sp.dma_start(a["xn_hl"].rearrange("(g j p) d -> g p j d", g=NG, j=TG)[ds(g, 1)]
                             .rearrange("a p j d -> p (a j) d"),
                             XNH[:, ds(g * (TG * 2 * D), TG * 2 * D)].rearrange("p (j d) -> p j d", j=TG))\
                    .then_inc(S["xn_stored"], 16)

            load_wa0(0)
            with sp.Fori(0, NG - 1) as g:
                sp.wait_ge(S["x_loaded"], 16 * g + 16)
                load_x(g + 1)
            with sp.Fori(0, NG - 1) as g:
                store_xn(g)
                load_wa0(g + 1)
            store_xn(NG - 1)
            sp.wait_ge(S["list_ready"], 3)

            def edges_of(n, units=range(RING)):
                for r in units:
                    start = sp.value_load(LROW[0:1, ds(n * RING + r, 1)], min_val=0, max_val=EDGES)
                    sp.wait_ge(S["agg_mm"], n * RING + r + 1)
                    sp.wait_ge(S["oh_loc"], n * RING + r + 1)
                    sp.dma_start(IDXR[:, r, :], a["edges"][ds(start, EG), :].rearrange("(p c) w -> p (c w)", c=EC))\
                        .then_inc(idx_loaded[r], 16)

            edges_of(0, range(EXTRA))
            with sp.Fori(0, L) as l:
                sp.wait_ge(U1.lo, 15 * l + 13)
                sp.dma_start(PRM[:, :], a["prm"][ds(l, 1)].rearrange("a p c -> p (a c)"))\
                    .then_inc(S["prm_loaded"], 16)
                def load_wb(l, g):
                    sp.wait_ge(S["wb_used"], l * NG + g + 1)
                    sp.dma_start(STB[:, :], a["wb"][ds(l, 1), :, ds(g, 1), :].rearrange("b p a c -> p (b a c)"))\
                        .then_inc(S["wb_loaded"], 16)

                load_wb(l, 0)
                edges_of(l * NG, range(EXTRA, RING))
                with sp.Fori(1, NG) as g:
                    load_wb(l, g)

                def next_wa(l, g):
                    sp.wait_ge(S["wa_used"], l * NG + g + NG + 1)
                    sp.dma_start(STA[:, :], a["wa"][ds(l + 1, 1), :, ds(g, 1), :].rearrange("b p a c -> p (b a c)"))\
                        .then_inc(S["wa_loaded"], 16)
                with sp.Fori(0, NG - 1) as g:
                    next_wa(l, g)
                    edges_of(l * NG + g + 1)
                next_wa(l, NG - 1)
                edges_of(l * NG + NG, range(EXTRA))
            sp.wait_ge(S["f2_evac"], L * NG * TG + 1)
            sp.dma_start(GW1, a["gw1"]).then_inc(S["gw_loaded"], 16)
            sp.dma_start(GPR[:, :], a["gprm"]).then_inc(S["gw_loaded"], 16)
            sp.dma_start(RWF[:, 0, :], a["rw"]).then_inc(S["gw_loaded"], 16)
            sp.dma_start(EB1[:, :], a["eb1"]).then_inc(S["gw_loaded"], 16)
            sp.dma_start(EB2, a["eb2"]).then_inc(S["gw_loaded"], 16)
            with sp.Fori(0, NG) as g:
                sp.wait_ge(S["x_in_used"], g + 1)
                sp.dma_start(XIN[:, :, :], a["x"].rearrange("(g j p) d -> g p j d", g=NG, j=TG)[ds(g, 1)]
                             .rearrange("a p j d -> p (a j) d")).then_inc(S["x_in_loaded"], 16)
            sp.wait_ge(S["x_plus"], NG)

            def load_xn(g, u):
                sp.wait_ge(S["xhl_used"], g + 1)
                sp.wait_ge(S["xhl_loaded"], 16 * g + 16)
                sp.dma_start(XHL2[u], a["xn_hl"].rearrange("(g j p) d -> g p j d", g=NG, j=TG)[ds(g, 1)]
                             .rearrange("a p j d -> p (a j) d")).then_inc(S["xhl_loaded"], 16)

            sp.sem_inc(S["xhl_loaded"], 16)
            by_twos(sp, lambda g, u, last: load_xn(g, u))
            with sp.Fori(0, NG) as g:
                sp.wait_ge(S["mw_used"], g + 1)
                sp.dma_start(STM, a["mw"][:, ds(g, 1), :].rearrange("p a c -> p (a c)")).then_inc(S["mw_loaded"], 16)
            with sp.Fori(0, NG) as g:
                sp.wait_ge(S["e_out"], g * (E * TG) + E * TG + 1)
                sp.dma_start(a["out"].rearrange("(g j p) d -> g p j d", g=NG, j=TG)[ds(g, 1)].rearrange("a p j d -> p (a j) d"),
                             X[:, ds(g * (TG * D), TG * D)].rearrange("p (j d) -> p j d", j=TG))\
                    .then_inc(S["out_stored"], 16)
            sp.wait_ge(S["out_stored"], 16 * NG)
        @block.gpsimd
        def _(pool):
            pool.sem_inc(S["wa_used"], 1)
            pool.sem_inc(S["wb_used"], 1)
            pool.sem_inc(S["q_norm"], 1)
            pool.sem_inc(S["x_tok"], 1)

            def rstd(U, u):
                hold(pool, U.moments, (u + 1) * TG)
                pool.tensor_scalar(U.VE[:, :], U.MV[:, :, 1], 1.0, EPS, ALU.mult, ALU.add).then_inc(U.scales, 1)
                pool.wait_ge(U.scales, 3 * u + 1)
                pool.tensor_tensor(U.RS[:, :], U.VE[:, :], EXPO[:TT, 0:TG], ALU.pow).then_inc(U.scales, 1)
                pool.wait_ge(U.scales, 3 * u + 2)
                pool.tensor_tensor(U.MR[:, :], U.MV[:, :, 0], U.RS[:, :], ALU.mult).then_inc(U.scales, 1)

            pool.memset(EXPO[:, :], -0.5).then_inc(S["consts0"], 1)
            pool.memset(IDF[:, :], 0.0).then_inc(S["consts0"], 1)
            pool.memset(MASK[:, :], 1.0).then_inc(S["consts0"], 1)
            pool.memset(SELF, W_UP).then_inc(S["consts0"], 1)
            pool.iota(KIDI[:, :], pattern=[[P, 2]], base=0, channel_multiplier=1).then_inc(S["consts0"], 1)
            pool.iota(IOTI, pattern=[[1, TT]], base=0, channel_multiplier=0).then_inc(S["consts0"], 1)
            pool.iota(R8I[:, :], pattern=[[-1, E]], base=E, channel_multiplier=0).then_inc(S["consts0"], 1)
            pool.iota(EDGI, pattern=[[TT, NT + 1]], base=0, channel_multiplier=0).then_inc(S["consts0"], 1)
            pool.wait_ge(S["consts0"], 8)
            pool.tensor_copy(EDGF, EDGI).then_inc(S["edge_consts"], 1)
            pool.wait_ge(S["edge_consts"], 1)
            pool.tensor_scalar(EDGF, EDGF, 1.0, -0.5, ALU.mult, ALU.add).then_inc(S["edge_consts"], 1)
            pool.affine_select(out=IDF[:, :], in_=IDF[:, :], compare_op=ALU.not_equal, fill=1.0, base=0,
                               pattern=[[-1, P]], channel_multiplier=1).then_inc(S["consts0"], 1)
            heads = MASK[:, :].rearrange("p (b c) -> p b c", c=DH)
            pool.affine_select(out=heads, in_=heads, compare_op=ALU.is_ge, fill=0.0, base=0,
                               pattern=[[-DH, P // DH], [0, DH]], channel_multiplier=1).then_inc(S["consts0"], 1)
            rstd(UX, 0)
            pool.affine_select(out=SELF, in_=SELF, compare_op=ALU.is_ge, fill=0.0, base=0,
                               pattern=[[-2, L], [0, TT]], channel_multiplier=1).then_inc(S["consts0"], 1)
            pool.wait_ge(S["consts0"], 11)
            pool.affine_select(out=SELF, in_=SELF, compare_op=ALU.is_ge, fill=0.0, base=1,
                               pattern=[[2, L], [0, TT]], channel_multiplier=-1).then_inc(S["consts1"], 1)
            hold(pool, S["consts1"], 1)
            pool.tensor_copy(SEL[:, :, :], SELF).then_inc(S["consts"], 1)
            pool.affine_select(out=heads, in_=heads, compare_op=ALU.is_ge, fill=0.0, base=DH - 1,
                               pattern=[[DH, P // DH], [0, DH]], channel_multiplier=-1).then_inc(S["consts"], 1)
            pool.tensor_copy(KIDX[:, 0, :], KIDI[:, :]).then_inc(S["consts"], 1)
            pool.tensor_copy(IOTA[:, :], IOTI).then_inc(S["consts"], 1)
            pool.tensor_copy(R8[:, :], R8I[:, :]).then_inc(S["consts"], 1)
            pool.memset(Z[:, NT * D:(NT + 1) * D], 0.0).then_inc(S["consts"], 1)
            pool.memset(ONES, 1.0).then_inc(S["consts"], 1)
            pool.memset(CNT[:, 0:1], -float(ER)).then_inc(S["consts"], 1)
            pool.memset(CNT[:, NT:NT + 1], float(ER)).then_inc(S["consts"], 1)
            pool.tensor_scalar(ID64[:, :], IDF[:TT, :TT], W_UP, 0.0, ALU.mult, ALU.add).then_inc(S["consts"], 1)

            def split_a(i, g):
                hold(pool, S["wa_split"], 3 * i + 1)
                pool.tensor_scalar(STA[:, :], STA[:, :], W_UP, 0.0, ALU.mult, ALU.add).then_inc(S["wa_split"], 1)
                pool.wait_ge(S["wa_split"], 3 * i + 2)
                pool.tensor_tensor(WAs[:, 1, ds(g * WAS, WAS)], STA[:, :], WAs[:, 0, ds(g * WAS, WAS)],
                                   ALU.subtract).then_inc(S["wa_split"], 1)
                hold(pool, S["wa_split"], 3 * i + 3)
                pool.sem_inc(S["wa_used"], 1)

            def split_b(i, g):
                hold(pool, S["wb_split"], 3 * i + 1)
                pool.tensor_scalar(STB[:, :], STB[:, :], W_UP, 0.0, ALU.mult, ALU.add).then_inc(S["wb_split"], 1)
                pool.wait_ge(S["wb_split"], 3 * i + 2)
                pool.tensor_tensor(WBs[:, 1, ds(g * WBS, WBS)], STB[:, :], WBs[:, 0, ds(g * WBS, WBS)],
                                   ALU.subtract).then_inc(S["wb_split"], 1)
                hold(pool, S["wb_split"], 3 * i + 3)
                pool.sem_inc(S["wb_used"], 1)

            with pool.Fori(0, NG - 1) as g:
                rstd(UX, g + 1)
                rstd(U1, g)
                split_a(g, g)
            rstd(U1, NG - 1)
            split_a(NG - 1, NG - 1)

            def gathers(n, slots):
                for r in slots:
                    pool.wait_ge(idx_loaded[r], 16 * n + 16)
                    hold(pool, S["agg_mm"], n * RING + r + 1)
                    for c in range(EC):
                        pool.indirect_dma_start(
                            out=GAT[:, r, c, :], out_offset=None, in_=a["xn_hl"],
                            in_offset=bass.IndirectOffsetOnAxis(ap=IDXR[:, r, 2 * c:2 * c + 1].bitcast(U32), axis=0))\
                            .then_inc(gathered[r], 16)

            hold(pool, S["xn_stored"], 16 * NG)
            gathers(0, range(EXTRA))
            with pool.Fori(0, L) as l:
                def phase_a(g):
                    n = l * NG + g
                    pool.wait_ge(S["q_turned"], n * 3 + 1)
                    for j in range(TG):
                        pool.wait_ge(S["q_rinv"], 2 * n + (1 if j < 3 else 2))
                        pool.tensor_tensor(QN[:, j, :].rearrange("p (h c) -> p h c", h=HEADS),
                                           QS[:, j, :].rearrange("p (h c) -> p h c", h=HEADS),
                                           RINV[:, j, :].unsqueeze(2).to_broadcast([TT, HEADS, DH]), ALU.mult)\
                            .then_inc(S["q_norm"], 1)
                    split_b(n, g)

                phase_a(0)
                with pool.Fori(1, NG) as g:
                    phase_a(g)
                gathers(l * NG, range(EXTRA, 4))
                rstd(U2, l * NG)
                gathers(l * NG, range(4, RING))
                with pool.Fori(0, NG - 1) as g:
                    n = l * NG + g
                    gathers(n + 1, range(0, 4))
                    rstd(U2, n + 1)
                    gathers(n + 1, range(4, RING))
                    rstd(U1, n + NG)
                    split_a(n + NG, g)
                split_a(l * NG + 2 * NG - 1, NG - 1)
                gathers(l * NG + NG, range(EXTRA))
                rstd(U1, l * NG + 2 * NG - 1)

            def bn_scales(i, chunks, g0, b0):
                pool.wait_ge(S["bn_mv"], (GC, GC + KC)[i])
                pool.tensor_scalar(BVE[:, 0, :chunks], BMV[:, :chunks, 1], 1.0, EPS, ALU.mult, ALU.add).then_inc(S["bn_step"], 1)
                pool.wait_ge(S["bn_step"], 4 * i + 1)
                pool.tensor_tensor(BVE[:, 1, :chunks], BVE[:, 0, :chunks], EXPO[:, :chunks], ALU.pow).then_inc(S["bn_step"], 1)
                pool.wait_ge(S["bn_step"], 4 * i + 2)
                pool.tensor_tensor(BVE[:, 2, :chunks], BVE[:, 1, :chunks], GPR[:, g0:g0 + chunks], ALU.mult).then_inc(S["bn_step"], 1)
                pool.wait_ge(S["bn_step"], 4 * i + 3)
                pool.tensor_tensor(BVE[:, 0, :chunks], BVE[:, 2, :chunks], BMV[:, :chunks, 0], ALU.mult).then_inc(S["bn_step"], 1)
                pool.wait_ge(S["bn_step"], 4 * i + 4)
                pool.tensor_tensor(BVE[:, 3, :chunks], GPR[:, b0:b0 + chunks], BVE[:, 0, :chunks], ALU.subtract).then_inc(S["bn_b"], 1)

            pool.wait_ge(S["gw_loaded"], 80)
            pool.tensor_scalar(RWF[:, 1, :], RWF[:, 0, :], W_UP, 0.0, ALU.mult, ALU.add).then_inc(S["rw_lo"], 1)
            pool.wait_ge(S["rw_lo"], 1)
            pool.tensor_copy(RW[:, 0, :], RWF[:, 1, :]).then_inc(S["rw_lo"], 1)
            pool.wait_ge(S["rw_lo"], 2)
            pool.tensor_tensor(RW[:, 1, :], RWF[:, 1, :], RW[:, 0, :], ALU.subtract).then_inc(S["rw_lo"], 1)
            hold(pool, U1.h, (L + 1) * NT)
            pool.sem_inc(S["x_in_used"], 1)
            with pool.Fori(0, NG) as g:
                xg = X[:, ds(g * TG * D, TG * D)].rearrange("p (j d) -> p j d", j=TG)
                pool.wait_ge(S["x_in_loaded"], 16 * g + 16)
                pool.tensor_tensor(xg, xg, XIN[:, :, :], ALU.add).then_inc(S["x_plus"], 1)
                hold(pool, S["x_plus"], g + 1)
                pool.sem_inc(S["x_in_used"], 1)
            bn_scales(0, GC, GC, 2 * GC)
            bn_scales(1, KC, 3 * GC + KC, 3 * GC + 2 * KC)

            def add_tokens(g):
                xg = X[:, ds(g * TG * D, TG * D)].rearrange("p (j d) -> p j d", j=TG)
                pool.wait_ge(U3.h, (g + 1) * TG)
                pool.tensor_tensor(xg, xg, H1[:, :, :], ALU.add).then_inc(S["x_tok"], 1)

            rstd(U3, 0)
            with pool.Fori(1, NG) as g:
                add_tokens(g - 1)
                rstd(U3, g)
            add_tokens(NG - 1)

        @block.tensor
        def _(pe):
            pe.sem_inc(S["q_turned"], 1)
            pe.sem_inc(S["ke_turned"], 2)
            pe.sem_inc(S["ctx_mm"], 2)
            for c in ("y_mm", "cb_mm"):
                pe.sem_inc(S[c], 1)
            pe.sem_inc(S["r_turned"], 1)
            pe.sem_inc(S["z_turned"], 1)
            pe.sem_inc(S["agg_mm"], RING)
            for U in (U1, U2, U3):
                pe.sem_inc(U.turned, 1)

            def turn(U, u, H, free, pairs=(0, 1, 2)):
                for i in pairs:
                    off, w = PAIRS[i]
                    pe.wait_ge(U.h, u * TG + (2 * i + 2 if i < 2 else TG))
                    if i in free:
                        pe.wait_ge(*free[i])
                    for t in range(w // TT):
                        for c in range(KC):
                            last = pe.transpose(PT[:, i % 2, c * 250 + t * TT:c * 250 + (t + 1) * TT],
                                                H[:, 2 * i + t, c * P:(c + 1) * P], IDF[:TT, :TT])
                    last.then_inc(U.turned, 1)

            def mm3(out, lhs, rhs, chunks, more=False):
                for k in range(chunks):
                    for s, (x, y) in enumerate(PASSES):
                        last = pe.matmul(out, lhs(x, k), rhs(y, k), start=(k == 0 and s == 0),
                                         stop=(not more and k == chunks - 1 and s == len(PASSES) - 1))
                return last

            pe.wait_ge(S["consts"], 10)
            turn(U1, 0, H1, {2: (U1.lo, 2)})
            pe.wait_ge(S["cnt"], NT - 1)
            pe.matmul(TM[:, 0, 0:NT + 1], ONES[:TT], CNT[:, :], start=True, stop=True).then_inc(S["cnt_mm"], 1)
            turn(U1, 1, H1, {0: (U1.lo, 4)}, (0, 1))
            pe.wait_ge(S["g_list"], 6)
            pe.matmul(TM[:, 1, :], ONES, DIAG.rearrange("p w h n -> p (w h n)"), start=True, stop=True).then_inc(S["cnt_mm"], 1)
            turn(U1, 1, H1, {2: (U1.lo, 5)}, (2,))
            pe.wait_ge(S["list_ready"], 3)

            with pe.Fori(2, NG - 1) as g:
                turn(U1, g, H1, {0: (U1.lo, g * 3 + 1), 2: (U1.lo, g * 3 + 2)})

            def bias(out, l, w):
                return pe.matmul(out, SEL[:, ds(l, 1), :].rearrange("p a c -> p (a c)"), BIAS[:, w * D:(w + 1) * D],
                                 start=False, stop=True)

            def k_product(l, g, n):
                pe.wait_ge(U1.lo, 3 * n + 4)
                pe.wait_ge(S["kt_lo"], KC * n + KC)
                for m in range(KC):
                    for p, (off, w) in enumerate(PARTS):
                        mm3(FFP[:, 2 * m + p, :w],
                            lambda x, k: WAs[:, x, K0 + k * D + m * P:K0 + k * D + (m + 1) * P],
                            lambda y, k: ft(y, k, g * GT + off, w), KC).then_inc(S["k_mm"], 1)

            def qv_product(l, g, n, tiles=range(TG)):
                for j in tiles:
                    if j != 1:
                        pe.wait_ge(S["qv_evac"], n * TG + 1 + (j - 1 if j else 0))
                    mm3(TM[:TT, j % 2, :], lambda x, k: ft(x, k, g * GT + j * TT, TT),
                        lambda y, k: WAs[:, y, QV0 + k * 2 * D:QV0 + (k + 1) * 2 * D], KC).then_inc(S["qv_mm"], 1)

            def turn_q(n, pairs=(0, 1, 2)):
                for i in pairs:
                    off, w = PAIRS[i]
                    pe.wait_ge(S["q_norm"], n * TG + (2 * i + 2 if i < 2 else TG) + 1)
                    if i != 1:
                        pe.wait_ge(S["q_lo"], n * 3 + 1 + (1 if i else 0))
                    for t in range(w // TT):
                        for c in range(KC):
                            last = pe.transpose(PT[:, i % 2, c * 250 + t * TT:c * 250 + (t + 1) * TT],
                                                QN[:, 2 * i + t, c * P:(c + 1) * P], IDF[:TT, :TT])
                    last.then_inc(S["q_turned"], 1)

            def attention_out(l, g, n, first, second):
                for j in range(TG):
                    if j == 0:
                        pe.wait_ge(*first)
                        pe.wait_ge(S["q_lo"], 3 * n + 4)
                    if j == 1:
                        pe.wait_ge(*second)
                    if j > 1:
                        pe.wait_ge(S["ao_evac"], n * TG + j)
                    mm3(TM[:TT, j % 2, :D], lambda x, k: ft(x, k, g * GT + j * TT, TT),
                        lambda y, k: M[:, y, k, :], KC, more=True)
                    bias(TM[:TT, j % 2, :D], l, 0).then_inc(S["ao_mm"], 1)

            def aggregate(n, u, free):
                pe.wait_ge(S["oh_done"], n * RING + u + 1)
                pe.wait_ge(*free)
                pe.wait_ge(gathered[u], 16 * EC * n + 16 * EC)
                for c in range(EC):
                    for s in range(2):
                        last = pe.matmul(TM[:TT, u % 2, :D], OH[:, u, c, :], GAT[:, u, c, s * D:(s + 1) * D],
                                         start=(c == 0 and s == 0), stop=(c == EC - 1 and s == 1))
                last.then_inc(S["agg_mm"], 1)

            def ff1(l, g, n, free):
                pe.wait_ge(U2.lo, 3 * n + 4)
                for m in range(FC):
                    if m >= 2:
                        pe.wait_ge(S["g_lo"], 16 * n + 2 * m - 2 + 1)
                    for p, (off, w) in enumerate(PARTS):
                        mm3(FFP[:, 2 * (m % 2) + p, :w],
                            lambda x, k: WBs[:, x, W10 + k * FF + m * P:W10 + k * FF + (m + 1) * P],
                            lambda y, k: ft(y, k, g * GT + off, w), KC).then_inc(S["f1_mm"], 1)
                    u = m - 1
                    if 0 <= u < RING:
                        aggregate(n, u, free if u < 2 else (S["agg_add"], n * RING + u))

            def ff2(l, n, j, free=None):
                if free is not None:
                    pe.wait_ge(*free)
                if j == 0:
                    pe.wait_ge(S["g_lo"], 16 * n + 17)
                elif j > 1:
                    pe.wait_ge(S["f2_evac"], n * TG + j)
                mm3(TM[:TT, j % 2, :D], lambda x, k: HID[:, x, k, j * TT:(j + 1) * TT],
                    lambda y, k: WBs[:, y, W20 + k * D:W20 + (k + 1) * D], FC, more=True)
                bias(TM[:TT, j % 2, :D], l, 1).then_inc(S["f2_mm"], 1)

            def step(l, g, n, free, before, after):
                ff1(l, g, n, free)
                banks = [(S["agg_add"], (n + 1) * RING), (S["agg_add"], (n + 1) * RING + 1)]
                if before:
                    turn(U1, n + NG - 1, H1, {0: (U2.lo, 3 * n + 4), 2: (U1.lo, 3 * (n + NG - 1) + 2)}, (0, 1))
                if after:
                    attention_out(l, g + 1, n + 1, *banks)
                    banks = [(S["ao_evac"], (n + 2) * TG + 1), None]
                if before:
                    turn(U1, n + NG - 1, H1, {2: (U1.lo, 3 * (n + NG - 1) + 2)}, (2,))
                ff2(l, n, 0, banks[0])
                ff2(l, n, 1, banks[1])
                ff2(l, n, 2)
                if after:
                    turn(U2, n + 1, H2, {0: (U1.lo, 3 * (n + NG) + 1), 2: (U2.lo, 3 * (n + 1) + 2)}, (0, 1))
                ff2(l, n, 3)
                if after:
                    turn(U2, n + 1, H2, {0: (U1.lo, 3 * (n + NG) + 1), 2: (U2.lo, 3 * (n + 1) + 2)}, (2,))
                ff2(l, n, 4)

            with pe.Fori(0, L) as l:
                pe.wait_ge(S["wa_split"], 3 * (l * NG + NG))
                pe.wait_ge(S["f2_evac"], l * NG * TG + 1)
                def turn_k(n, m):
                    pe.wait_ge(S["ke"], 4 * n + 2 * m + 2)
                    for j in range(TG):
                        last = pe.transpose(KTP[m][:, j, :], KE[:, m, j * TT:(j + 1) * TT], IDF[:, :])
                    last.then_inc(S["ke_turned"], 1)

                def context(n):
                    pe.wait_ge(U1.lo, 3 * (l * NG + NG) + 1)
                    pe.wait_ge(S["q_lo"], 3 * n + 1)
                    pe.wait_ge(S["qv_evac"], (n + 1) * TG + 1)
                    for m in range(KC):
                        pe.wait_ge(S["kt_lo"], KC * n + m + 3)
                        for j in range(TG):
                            for s, (x, y) in enumerate(PASSES):
                                last = pe.matmul(PT[:, m, :P], KT[:, x, m, j, :], V[:, y, j * D + m * P:j * D + (m + 1) * P],
                                                 start=(j == 0 and s == 0), stop=(j == TG - 1 and s == 2))
                        last.then_inc(S["ctx_mm"], 1)

                k_product(l, 0, l * NG)
                qv_product(l, 0, l * NG, (0,))
                u4 = l * NG + NG - 1
                qv_product(l, 0, l * NG, (1,))
                turn(U1, u4, H1, {0: (U2.lo, 3 * l * NG + 1)}, (0, 1))
                turn_k(l * NG, 0)
                qv_product(l, 0, l * NG, (2,))
                turn(U1, u4, H1, {2: (U1.lo, 3 * u4 + 2)}, (2,))
                turn_k(l * NG, 1)
                qv_product(l, 0, l * NG, (3, 4))
                with pe.Fori(1, NG) as g:
                    n = l * NG + g
                    k_product(l, g, n)
                    context(n - 1)
                    qv_product(l, g, n, (0, 1))
                    pe.wait_ge(S["ctx_acc"], KC * n + KC)
                    turn_q(n - 1, (0, 1))
                    turn_k(n, 0)
                    turn_q(n - 1, (2,))
                    qv_product(l, g, n, (2,))
                    turn_k(n, 1)
                    qv_product(l, g, n, (3, 4))
                context(l * NG + NG - 1)
                pe.wait_ge(S["ctx_acc"], KC * (l * NG + NG) + KC)
                for m in range(KC):
                    last = pe.transpose(FFP[:, 1, m * P:(m + 1) * P], CTXA[:, m, :], IDF[:, :])
                last.then_inc(S["ctx_turned"], 1)
                turn_q(l * NG + NG - 1)
                pe.wait_ge(S["ctx_lo"], 3 * l + 3)
                for m in range(KC):
                    for s, (x, y) in enumerate(PASSES):
                        last = pe.matmul(FFP[:, 0, m * D:(m + 1) * D], CTX[:, x, m, :],
                                         WAs[:, y, WO0 + m * D:WO0 + (m + 1) * D], start=(s == 0), stop=(s == 2))
                last.then_inc(S["m_mm"], 1)
                pe.wait_ge(S["m_lo"], 3 * l + 3)
                pe.wait_ge(S["wb_split"], 3 * (l * NG + NG))
                n0 = l * NG
                attention_out(l, 0, n0, (S["qv_evac"], (n0 + NG) * TG + 1), (S["qv_evac"], (n0 + NG) * TG + 1))
                turn(U2, n0, H2, {0: (U1.lo, 3 * (n0 + NG) + 1), 2: (U2.lo, 3 * n0 + 2)})
                step(l, 0, n0, (S["ao_evac"], (n0 + 1) * TG + 1), False, True)
                with pe.Fori(1, NG - 1) as g:
                    n = l * NG + g
                    step(l, g, n, (S["f2_evac"], n * TG + 1), True, True)
                n4 = n0 + NG - 1
                step(l, NG - 1, n4, (S["f2_evac"], n4 * TG + 1), True, False)

            def turn_z(g, copied=True):
                rows = H1 if copied else Z[:, 0:TG * D].rearrange("p (j d) -> p j d", j=TG)
                if copied:
                    pe.wait_ge(S["zs"], g)
                for i, (off, w) in enumerate(PAIRS):
                    pe.wait_ge(S["zt"], 3 * g + 1 + (1 if i == 2 else 0))
                    for t in range(w // TT):
                        for c in range(KC):
                            last = pe.transpose(PT[:, i % 2, c * 250 + t * TT:c * 250 + (t + 1) * TT],
                                                rows[:, 2 * i + t, c * P:(c + 1) * P], IDF[:TT, :TT])
                    last.then_inc(S["z_turned"], 1)

            def gnn1(g, u, last_group):
                pe.wait_ge(S["zt"], 3 * g + 4)
                for m in range(GC):
                    for p, (off, w) in enumerate(PARTS):
                        pe.wait_ge(S["t_evac"], 8 * g + 2 * m + p + 1)
                        for k in range(KC):
                            last = pe.matmul(FFP[:, 2 * (m % 2) + p, :w], GW1[:, k * GF + m * P:k * GF + (m + 1) * P],
                                             ZT[:, u, k, off:off + w], start=(k == 0), stop=(k == KC - 1))
                        last.then_inc(S["t_mm"], 1)
                    if m == 1 and not last_group:
                        turn_z(g + 1)

            def gnn2(g, u, last_group):
                for m in range(KC):
                    for p, (off, w) in enumerate(PARTS):
                        pe.wait_ge(S["y_evac"], 4 * g + 2 * m + p + 1)
                        out = FFP[:, 2 * m + p, :w]
                        for k in range(GC):
                            if (m, p) == (0, 0):
                                pe.wait_ge(S["th_lo"], g * GC + k + 1)
                            for s, (x, y) in enumerate(PASSES):
                                pe.matmul(out, WAs[:, x, k * D + m * P:k * D + (m + 1) * P],
                                          HID[:, y, GC * u + k, off:off + w],
                                          start=(k == 0 and s == 0), stop=False, skip_group_check=True)
                        tiles = range(off // TT, (off + w) // TT)
                        if (m, p) == (0, 0):
                            pe.wait_ge(S["xhl_loaded"], 16 * g + 32)
                        for j in tiles:
                            for s in range(2):
                                last = pe.matmul(FFP[:, 2 * m + p, j * TT - off:(j + 1) * TT - off],
                                                 XHL2[u][:, j, s * D + m * P:s * D + (m + 1) * P], ID64[:, :],
                                                 start=False, stop=(j == tiles[-1] and s == 1), skip_group_check=True)
                        last.then_inc(S["y_mm"], 1)

            pe.wait_ge(S["agg_add"], L * NG * RING + 1)
            pe.wait_ge(U1.lo, 3 * (L + 1) * NG - 2)
            turn_z(0, False)
            for u in range(EXTRA):
                aggregate(L * NG, u, (S["f2_evac"], L * NG * TG + 1))
            pe.wait_ge(S["gw_loaded"], 80)
            by_twos(pe, gnn1)
            pe.wait_ge(S["wa_split"], 3 * (L + 1) * NG)
            by_twos(pe, gnn2)

            def turn_r(g, u):
                pe.wait_ge(S["r_relu"], KC * (g + 1))
                for j in range(TG):
                    if j != 1:
                        pe.wait_ge(S["x1"], g * TG + (j if j else 1))
                    for c in range(KC):
                        last = pe.transpose(TM[:TT, j % 2, c * P:(c + 1) * P], ZT[:, u, c, j * TT:(j + 1) * TT], IDF[:, :])
                    last.then_inc(S["r_turned"], 1)

            def logits(g):
                pe.wait_ge(U3.lo, 3 * g + 4)
                pe.wait_ge(S["log"], g + 1)
                for j in range(TG):
                    last = mm3(FFP[:TT, 0, j * E:(j + 1) * E], lambda x, k: ft(x, k, g * GT + j * TT, TT),
                               lambda y, k: RW[:, y, k * E:(k + 1) * E], KC)
                last.then_inc(S["log_mm"], 1)

            pe.wait_ge(S["rw_lo"], 3)
            pe.wait_ge(S["y_evac"], 4 * NG + 4)
            turn_r(0, 0)
            turn_r(1, 1)
            for g in range(NG):
                free = {0: (U3.lo, 3 * g + 1), 2: (U3.lo, 3 * g + 2)}
                turn(U3, g, H1, free, (0, 1))
                if g + 2 < NG:
                    turn_r(g + 2, g % 2)
                turn(U3, g, H1, free, (2,))
                logits(g)

            def turn_combine(g):
                pe.wait_ge(S["cbg"], g + 1)
                pe.wait_ge(S["ct"], 2 * g + 1)
                for j in range(TG):
                    last = pe.transpose(PT[:E, j // 4, (j % 4) * TT:(j % 4 + 1) * TT], CBG[:, j * E:(j + 1) * E], IDF[:TT, :TT])
                last.then_inc(S["cb_turned"], 1)

            def combine_b2(g, tiles):
                for j in tiles:
                    if j == 0:
                        pe.wait_ge(S["ct"], 2 * g + 3)
                    if j == 0:
                        pe.wait_ge(S["e_out"], g * (E * TG) + 1)
                    if j > 1:
                        pe.wait_ge(S["cb_add"], g * TG + j)
                    pe.matmul(TM[:TT, j % 2, :D], CT[:, j * TT:(j + 1) * TT], EB2, start=True, stop=True)\
                        .then_inc(S["cb_mm"], 1)

            def e1(g, e, m):
                pe.wait_ge(S["eg_lo"], 4 * (g * E + e) + 2 * m + 2)
                for p, (off, w) in enumerate(PARTS):
                    mm3(FFP[:, 2 * m + p, :w],
                        lambda s, k: MW[:, s, ds(e * (4 * D) + (k * D + m * P), P)],
                        lambda s, k: ft(s, k, g * GT + off, w), KC).then_inc(S["e1_mm"], 1)

            def e2(g, e, q, tiles):
                x = g * E + e
                for j in tiles:
                    if j == 0:
                        pe.wait_ge(S["eg_lo"], 4 * x + 4 + 4)
                    if j != 1:
                        pe.wait_ge(S["e_out"], x * TG + (j if j else 1))
                    mm3(TM[:TT, j % 2, :D], lambda s, k: HID[:, s, 2 * q + k, j * TT:(j + 1) * TT],
                        lambda s, k: MW[:, s, ds(e * (4 * D) + (2 * D + k * D), D)], KC).then_inc(S["e2_mm"], 1)

            def expert_step(g, e, q, following):
                if following:
                    e1(*following, 0)
                e2(g, e, q, (0, 1))
                if following:
                    e1(*following, 1)
                e2(g, e, q, (2, 3, 4))

            def expert_group(g, last):
                combine_b2(g, (0, 1))
                e1(g, 1, 0)
                combine_b2(g, (2, 3))
                e1(g, 1, 1)
                combine_b2(g, (4,))
                pe.wait_ge(S["cb_add"], (g + 1) * TG + 1)
                e2(g, 0, 0, range(TG))
                expert_step(g, 1, 1, (g, 2))
                with pe.Fori(1, E // 2 - 1) as h:
                    expert_step(g, h * 2, 0, (g, h * 2 + 1))
                    expert_step(g, h * 2 + 1, 1, (g, h * 2 + 2))
                if not last:
                    turn_combine(g + 1)
                expert_step(g, E - 2, 0, (g, E - 1))
                expert_step(g, E - 1, 1, None if last else (g + 1, 0))

            pe.wait_ge(S["mw_used"], NG + 1)
            pe.wait_ge(S["log"], NG + 1)
            e1(0, 0, 0)
            e1(0, 0, 1)
            turn_combine(0)
            with pe.Fori(0, NG - 1) as g:
                expert_group(g, False)
            expert_group(NG - 1, True)

        @block.scalar
        def _(act):
            def split_hi(stage, loaded, W, w, split, i, g):
                act.wait_ge(loaded, 16 * i + 16)
                act.activation(W[:, 0, ds(g * w, w)], stage[:, :], ACT.Copy, scale=W_UP).then_inc(split, 1)

            def split_hi_a(i, g):
                split_hi(STA, S["wa_loaded"], WAs, WAS, S["wa_split"], i, g)

            def ln_hi(U, u, g, scale, bias, pairs=(0, 1, 2)):
                for i in pairs:
                    off, w = PAIRS[i]
                    act.wait_ge(U.turned, 3 * u + i + 2)
                    for c in range(KC):
                        ps = PT[:, i % 2, c * 250:c * 250 + w]
                        act.activation(ft(0, c, g * GT + off, w), ps, ACT.Identity,
                                       bias=bias[:, c:c + 1], scale=scale[:, c:c + 1]).then_inc(U.hi, 1)
                        act.activation(ps, ps, ACT.Identity,
                                       bias=bias[:, c:c + 1], scale=scale[:, c:c + 1]).then_inc(U.hi, 1)

            act.wait_ge(S["prm0_loaded"], 48)
            act.activation(EPSB[:, 1:2], EPSB[:, 0:1], ACT.Identity, bias=1.0, scale=1.0).then_inc(S["eps_ready"], 1)
            act.wait_ge(S["eps_ready"], 1)
            def rows_of_xn(g):
                for j in range(TG):
                    act.wait_ge(UX.h, g * TG + j + 1)
                    act.activation(XNH[:, ds(g * (TG * 2 * D) + j * 2 * D, D)], xt(g * TG + j), ACT.Copy).then_inc(S["xn_hl_hi"], 1)
                    act.activation(Z[:, ds(g * (TG * D) + j * D, D)], xt(g * TG + j), ACT.Copy,
                                   scale=EPSB[:, 1:2]).then_inc(S["z_init"], 1)

            rows_of_xn(0)
            split_hi_a(0, 0)
            act.wait_ge(S["edge_consts"], 2)
            act.wait_ge(S["dst_float"], 1)

            def count_edges(tiles):
                for t in tiles:
                    act.activation(JUNK[:, t, :], DSTF, ACT.Sign, bias=EDGF[:TT, t:t + 1], scale=-1.0,
                                   accum_out=CNT[:, t:t + 1]).then_inc(S["cnt"], 1)

            count_edges(range(1, NA))
            rows_of_xn(1)
            split_hi_a(1, 1)
            ln_hi(U1, 0, 0, PR0[:, 0:KC], PR0[:, KC:2 * KC])
            count_edges(range(NA, NT))
            with act.Fori(2, NG) as g:
                rows_of_xn(g)
                split_hi_a(g, g)
                ln_hi(U1, g - 1, g - 1, PR0[:, 0:KC], PR0[:, KC:2 * KC])

            def q_hi(g, n, pairs=(0, 1, 2)):
                for i in pairs:
                    off, w = PAIRS[i]
                    act.wait_ge(S["q_turned"], 3 * n + i + 2)
                    act.activation(FT[:, 0, :, ds(g * GT + off, w)],
                                   PT[:, i % 2, 0:500].rearrange("p (c w) -> p c w", c=KC)[:, :, :w],
                                   ACT.Copy, scale=W_UP).then_inc(S["q_hi"], 1)

            def phase_a(l, g, n, with_q):
                act.wait_ge(S["k_max"], 8 * n + 7)
                act.activation(FAC[:, :], KDIF[:, :], ACT.Exp, scale=SCALE / W_UP).then_inc(S["fac"], 1)
                def v_hi(j):
                    act.wait_ge(S["qv_mm"], n * TG + j + 1)
                    act.activation(V[:, 0, j * D:(j + 1) * D], TM[:TT, j % 2, D:2 * D], ACT.Copy).then_inc(S["v_hi"], 1)

                for m in range(KC):
                    for p, (off, w) in enumerate(PARTS):
                        if p == 0:
                            if m == 1:
                                v_hi(0)
                                if with_q:
                                    q_hi(g - 1, n - 1, (0, 1))
                            act.wait_ge(S["ke_turned"], KC * n + m + 1)
                        act.activation(KE[:, m, off:off + w], FFP[:, 2 * m + p, :w], ACT.Exp, bias=NKB[:, m:m + 1],
                                       scale=SCALE / W_UP, accum_out=KSG[:, m, p:p + 1]).then_inc(S["ke"], 1)

                def q_exp(j):
                    act.wait_ge(S["qv_evac"], n * TG + j + 2)
                    act.activation(QS[:, j, :], QS[:, j, :], ACT.Exp, scale=SCALE / W_UP).then_inc(S["q_exp"], 1)

                def kt_hi(m):
                    act.wait_ge(S["ke_turned"], KC * n + m + 3)
                    act.wait_ge(S["ctx_mm"], KC * n + m + 1)
                    act.activation(KT[:, 0, m, :, :], KTP[m], ACT.Copy, scale=K_UP).then_inc(S["kt_hi"], 1)

                def early(pairs):
                    if with_q:
                        q_hi(g - 1, n - 1, pairs)
                    else:
                        ln_hi(U1, n + NG - 1, NG - 1, PRM[:, 16:18], PRM[:, 18:20], pairs)

                if not with_q:
                    act.wait_ge(S["prm_loaded"], 16 * l + 16)
                v_hi(1)
                if not with_q:
                    early((0, 1))
                q_exp(0)
                if with_q:
                    early((2,))
                kt_hi(0)
                v_hi(2)
                if not with_q:
                    early((2,))
                q_exp(1)
                kt_hi(1)
                v_hi(3)
                q_exp(2)
                v_hi(4)
                q_exp(3)
                q_exp(4)
                hold(act, S["f2_evac"], l * NG * TG + 1)
                split_hi(STB, S["wb_loaded"], WBs, WBS, S["wb_split"], n, g)

            def gelu(n):
                for m in range(FC):
                    for p, (off, w) in enumerate(PARTS):
                        ps = FFP[:, 2 * (m % 2) + p, :w]
                        act.wait_ge(S["f1_mm"], 16 * n + 2 * m + p + 1)
                        act.activation(HID[:, 0, m, off:off + w], ps, ACT.Gelu, bias=PRM[:, 8 + m:9 + m],
                                       scale=1 / W_UP).then_inc(S["g_hi"], 1)
                        act.activation(ps, ps, ACT.Gelu, bias=PRM[:, 8 + m:9 + m],
                                       scale=1 / W_UP).then_inc(S["g_hi"], 1)

            hold(act, S["xn_stored"], 16 * NG)
            with act.Fori(0, L) as l:
                n0 = l * NG
                phase_a(l, 0, n0, False)
                with act.Fori(1, NG) as g:
                    phase_a(l, g, l * NG + g, True)
                q_hi(NG - 1, n0 + NG - 1)
                act.wait_ge(S["m_lo"], 3 * l + 1)
                hold(act, S["m_mm"], l + 1)
                for m in range(KC):
                    act.activation(M[:, 0, m, :], FFP[:, 0, m * D:(m + 1) * D], ACT.Copy, scale=RKS[:, m:m + 1])\
                        .then_inc(S["m_hi"], 1)
                ln_hi(U2, n0, 0, PRM[:, 4:6], PRM[:, 6:8])
                gelu(n0)
                ln_hi(U2, n0 + 1, 1, PRM[:, 4:6], PRM[:, 6:8])
                split_hi_a(n0 + NG, 0)
                with act.Fori(1, NG - 1) as g:
                    n = l * NG + g
                    gelu(n)
                    ln_hi(U1, n + NG - 1, g - 1, PRM[:, 0:2], PRM[:, 2:4])
                    ln_hi(U2, n + 1, g + 1, PRM[:, 4:6], PRM[:, 6:8])
                    split_hi_a(n + NG, g)
                gelu(n0 + NG - 1)
                ln_hi(U1, n0 + 2 * NG - 2, NG - 2, PRM[:, 0:2], PRM[:, 2:4])
                split_hi_a(n0 + 2 * NG - 1, NG - 1)

            act.sem_inc(S["zt"], 1)
            act.sem_inc(S["t_evac"], 4)
            act.sem_inc(S["y_evac"], 4)
            act.sem_inc(S["ct"], 1)

            def zt_copy(g, u):
                for i, (off, w) in enumerate(PAIRS):
                    act.wait_ge(S["z_turned"], 3 * g + i + 2)
                    act.activation(ZT[:, u, :, off:off + w],
                                   PT[:, i % 2, 0:500].rearrange("p (c w) -> p c w", c=KC)[:, :, :w],
                                   ACT.Copy).then_inc(S["zt"], 1)

            def gnn1(g, u, last):
                for m in range(GC):
                    for p, (off, w) in enumerate(PARTS):
                        act.wait_ge(S["t_mm"], 8 * g + 2 * m + p + 1)
                        act.activation(TH[:, m, ds(g * GT + off, w)], FFP[:, 2 * (m % 2) + p, :w], ACT.Identity,
                                       bias=GPR[:, m:m + 1]).then_inc(S["t_evac"], 1)
                    if m == 1 and not last:
                        zt_copy(g + 1, 1 - u)

            def relu_hi(g, u):
                for m in range(GC):
                    act.activation(HID[:, 0, GC * u + m, :], TH[:, m, ds(g * GT, GT)], ACT.Relu,
                                   bias=BVE[:, 3, m:m + 1], scale=BVE[:, 2, m:m + 1]).then_inc(S["th_hi"], 1)
                    act.activation(TH[:, m, ds(g * GT, GT)], TH[:, m, ds(g * GT, GT)], ACT.Relu,
                                   bias=BVE[:, 3, m:m + 1], scale=BVE[:, 2, m:m + 1]).then_inc(S["th_relu"], 1)

            def gnn2(g, u, last):
                if not last:
                    relu_hi(g + 1, 1 - u)
                for m in range(KC):
                    for p, (off, w) in enumerate(PARTS):
                        hold(act, S["y_mm"], 4 * g + 2 * m + p + 2)
                        act.activation(Y[:, m, ds(g * GT + off, w)], FFP[:, 2 * m + p, :w], ACT.Identity,
                                       bias=GPR[:, 3 * GC + m:3 * GC + m + 1], scale=1 / W_UP).then_inc(S["y_evac"], 1)

            zt_copy(0, 0)
            act.wait_ge(S["gw_loaded"], 80)
            by_twos(act, gnn1)
            hold(act, S["bn_b"], 1)
            relu_hi(0, 0)
            by_twos(act, gnn2)
            act.wait_ge(S["bn_b"], 2)
            hold(act, S["th_lo"], NG * GC)

            def relu_out(g, u):
                for c in range(KC):
                    act.activation(ZT[:, u, c, :], Y[:, c, ds(g * GT, GT)], ACT.Relu, bias=BVE[:, 3, c:c + 1],
                                   scale=BVE[:, 2, c:c + 1]).then_inc(S["r_relu"], 1)

            def mw_hi(g):
                hold(act, S["mw_loaded"], 16 * g + 16)
                act.activation(MW[:, 0, ds(g * MWS, MWS)], STM, ACT.Copy, scale=W_UP).then_inc(S["mw_split"], 1)

            def tokens_hi(g, pairs):
                for i in pairs:
                    off, w = PAIRS[i]
                    act.wait_ge(U3.turned, 3 * g + i + 2)
                    act.activation(FT[:, 0, :, ds(g * GT + off, w)],
                                   PT[:, i % 2, 0:500].rearrange("p (c w) -> p c w", c=KC)[:, :, :w],
                                   ACT.Copy).then_inc(U3.hi, 1)

            relu_out(0, 0)
            relu_out(1, 1)
            mw_hi(0)
            hold(act, S["r_turned"], TG + 1)
            relu_out(2, 0)
            for g in range(NG):
                tokens_hi(g, (0, 1))
                if g + 1 < NG:
                    mw_hi(g + 1)
                tokens_hi(g, (2,))
                if g + 3 < NG:
                    hold(act, S["r_turned"], (g + 2) * TG + 1)
                    relu_out(g + 3, (g + 1) % 2)
            act.wait_ge(S["rt"], 2)
            act.activation(RT[:, 1, :, :], RT[:, 0, :, :], ACT.Exp).then_inc(S["rt"], 1)

            def combine_up(g):
                act.wait_ge(S["cb_turned"], g + 1)
                act.wait_ge(S["cb_mm"], g * TG + 1)
                act.activation(CT[:, 0:4 * TT], PT[:E, 0, 0:4 * TT], ACT.Copy).then_inc(S["ct"], 1)
                act.activation(CT[:, 4 * TT:GT], PT[:E, 1, 0:TT], ACT.Copy).then_inc(S["ct"], 1)

            def expert_gelu(g, e, q):
                x = g * E + e
                for m in range(KC):
                    for p, (off, w) in enumerate(PARTS):
                        ps = FFP[:, 2 * m + p, :w]
                        hold(act, S["e1_mm"], 4 * x + 2 * m + p + 1)
                        act.activation(HID[:, 0, 2 * q + m, off:off + w], ps, ACT.Gelu,
                                       bias=EB1[:, ds(e * KC + m, 1)], scale=1 / W_UP).then_inc(S["eg_hi"], 1)
                        act.activation(ps, ps, ACT.Gelu, bias=EB1[:, ds(e * KC + m, 1)],
                                       scale=1 / W_UP).then_inc(S["eg_hi"], 1)

            def expert_group(g, last):
                with act.Fori(0, E // 2 - 1) as h:
                    expert_gelu(g, h * 2 + 1, 1)
                    expert_gelu(g, h * 2 + 2, 0)
                if not last:
                    combine_up(g + 1)
                expert_gelu(g, E - 1, 1)
                if not last:
                    expert_gelu(g + 1, 0, 0)

            expert_gelu(0, 0, 0)
            combine_up(0)
            with act.Fori(0, NG - 1) as g:
                expert_group(g, False)
            expert_group(NG - 1, True)

        @block.vector
        def _(v):
            for s, c in (("qv_evac", 1), ("q_lo", 1), ("kt_lo", 2), ("ctx_acc", 2), ("ao_evac", 1),
                         ("f2_evac", 1), ("g_lo", 1)):
                v.sem_inc(S[s], c)
            v.sem_inc(U1.lo, 1)
            v.sem_inc(U2.lo, 1)
            v.sem_inc(U3.lo, 1)
            v.sem_inc(S["oh_loc"], RING)
            v.sem_inc(S["agg_add"], 1)
            v.sem_inc(S["k_sum"], 1)
            for c in ("x1", "log", "cb_add", "e_out", "mw_used"):
                v.sem_inc(S[c], 1)
            v.sem_inc(S["eg_lo"], 4)

            def stats(U, u, src):
                for j in range(TG):
                    v.bn_stats(U.ST[:, j, :], src(j)).then_inc(U.stats, 1)
                hold(v, U.stats, u * TG + TG)
                for j in range(TG):
                    v.bn_aggr(U.MV[:, j, :], U.ST[:, j, :]).then_inc(U.moments, 1)

            def norm(U, u, src, dst):
                v.wait_ge(U.scales, 3 * u + 3)
                for j in range(TG):
                    v.tensor_scalar(dst(j), src(j), U.RS[:, j:j + 1], U.MR[:, j:j + 1], ALU.mult,
                                    ALU.subtract).then_inc(U.h, 1)

            def ln_lo(U, u, g, pairs=(0, 1, 2)):
                for i in pairs:
                    off, w = PAIRS[i]
                    v.wait_ge(U.hi, 12 * u + 4 * (i + 1))
                    v.tensor_tensor(FT[:, 1, :, ds(g * GT + off, w)],
                                    PT[:, i % 2, 0:500].rearrange("p (c w) -> p c w", c=KC)[:, :, :w],
                                    FT[:, 0, :, ds(g * GT + off, w)], ALU.subtract).then_inc(U.lo, 1)

            tile_of = lambda g: lambda j: X[:, ds(g * (TG * D) + j * D, D)]

            def norm_x(g):
                norm(UX, g, tile_of(g), tile_of(g))

            def stats_x(g):
                hold(v, S["x_loaded"], 16 * g + 16)
                stats(UX, g, tile_of(g))

            def norm_1(g):
                v.wait_ge(U1.turned, 3 * g + 1)
                norm(U1, g, tile_of(g), lambda j: H1[:, j, :])

            def stats_1(g):
                hold(v, UX.h, (g + 1) * TG)
                stats(U1, g, tile_of(g))
                for j in range(TG):
                    v.wait_ge(S["xn_hl_hi"], g * TG + j + 1)
                    last = v.tensor_tensor(XNH[:, ds(g * (TG * 2 * D) + (j * 2 * D + D), D)], tile_of(g)(j),
                                           XNH[:, ds(g * (TG * 2 * D) + j * 2 * D, D)], ALU.subtract)
                last.then_inc(S["xn_hl_lo"], 1)

            def first_norms(g, load=True, more=True):
                ln_lo(U1, g - 1, g - 1, (0,))
                if more:
                    norm_x(g + 1)
                ln_lo(U1, g - 1, g - 1, (1,))
                if load:
                    stats_x(g + 2)
                ln_lo(U1, g - 1, g - 1, (2,))
                norm_1(g)
                if more:
                    stats_1(g + 1)

            stats_x(0)
            v.wait_ge(S["dst_loaded"], 16)
            v.tensor_copy(DSTF, DSTI).then_inc(S["dst_float"], 1)
            norm_x(0)
            stats_x(1)
            stats_1(0)
            norm_x(1)
            stats_x(2)
            norm_1(0)
            stats_1(1)
            first_norms(1)
            v.wait_ge(S["cnt_mm"], 1)
            v.tensor_scalar(SEGI[:, :], TM[:, 0, 0:NT + 1], 0.5, EDGES / 2, ALU.mult, ALU.add).then_inc(S["list_step"], 1)
            v.wait_ge(S["list_step"], 1)
            v.tensor_copy(SEG[:, :], SEGI[:, :]).then_inc(S["list_step"], 1)
            v.wait_ge(S["list_step"], 2)
            v.tensor_tensor(GRF[:, 0, 0:NT], SEG[:, 1:NT + 1], SEG[:, 0:NT], ALU.subtract).then_inc(S["list_step"], 1)
            v.wait_ge(S["list_step"], 3)
            v.tensor_scalar(GRI[:, :], GRF[:, 0, 0:NT], 1 / EG, (EG - 1) / (2 * EG), ALU.mult, ALU.add).then_inc(S["list_step"], 1)
            v.wait_ge(S["list_step"], 4)
            v.tensor_copy(GRF[:, 1, 0:NT], GRI[:, :]).then_inc(S["list_step"], 1)
            v.memset(GRF[:, 4, :], 1.0).then_inc(S["list_step"], 1)
            v.memset(GRF[:, 3, 0:1], 0.0).then_inc(S["list_step"], 1)
            v.wait_ge(S["list_step"], 7)
            v.tensor_tensor_scan(GRF[:, 2, 0:NT], GRF[:, 4, 0:NT], GRF[:, 1, 0:NT], 0.0, ALU.mult, ALU.add)\
                .then_inc(S["list_step"], 1)
            v.wait_ge(S["list_step"], 8)
            v.scalar_tensor_tensor(GRF[:, 3, 1:NT + 1], GRF[:, 2, 0:NT], -float(EG), SEG[:, 1:NT + 1], ALU.mult, ALU.add)\
                .then_inc(S["list_step"], 1)
            v.wait_ge(S["list_step"], 9)
            v.tensor_tensor(GRF[:, 0, 0:NT], GRF[:, 3, 1:NT + 1], GRF[:, 3, 0:NT], ALU.subtract).then_inc(S["list_step"], 1)
            v.wait_ge(S["consts"], 10)
            v.tensor_scalar(KIDX[:, 1, :], KIDX[:, 0, :], float(EG), None, ALU.mult).then_inc(S["list_step"], 1)
            v.wait_ge(S["list_step"], 10)
            for h in range(2):
                v.tensor_scalar(GMK[:, h, 0, :], GRF[:, 2, 0:NT], KIDX[:, 0, h:h + 1], None, ALU.is_le).then_inc(S["list_step"], 1)
                v.wait_ge(S["list_step"], 11 + 2 * h + 1)
                v.tensor_tensor(GMK[:, h, 1, :], GMK[:, h, 0, :], GRF[:, 0, 0:NT], ALU.mult).then_inc(S["list_step"], 1)
            v.wait_ge(S["list_step"], 15)
            for h in range(2):
                v.tensor_reduce(LSF[:, h, 1:2], GMK[:, h, 0, :], AX, ALU.add).then_inc(S["list_step"], 1)
                v.tensor_reduce(LSF[:, h, 0:1], GMK[:, h, 1, :], AX, ALU.add).then_inc(S["list_step"], 1)
            v.wait_ge(S["list_step"], 19)
            v.tensor_tensor(KIDX[:, 0, :], LSF[:, :, 0], KIDX[:, 1, :], ALU.add).then_inc(S["list_step"], 1)
            v.wait_ge(S["list_step"], 20)
            v.tensor_scalar(LSF[:, :, 0], KIDX[:, 0, :], float(EDGES), None, ALU.min).then_inc(S["g_list"], 1)
            v.wait_ge(S["cnt"], NT - 1)
            v.wait_ge(S["g_list"], 1)
            for w in range(2):
                for h in range(2):
                    v.tensor_scalar(DIAG[:, w, h, :], IDF[:, :], LSF[:, h, w:w + 1], None, ALU.mult).then_inc(S["g_list"], 1)
            v.wait_ge(S["prm0_loaded"], 48)
            v.tensor_scalar(BSF[:, 0:D], BSF[:, 0:D], W_UP, None, ALU.mult).then_inc(S["bias_step"], 1)
            v.tensor_reduce(EVEN[:, 0:1], IDF[:2 * L, 0:2 * L].rearrange("p (l w) -> p w l", w=2)[:, 0, :], AX, ALU.add).then_inc(S["bias_step"], 1)
            v.tensor_reduce(EVEN[:, 1:2], IDF[:2 * L, 0:2 * L].rearrange("p (l w) -> p w l", w=2)[:, 1, :], AX, ALU.add).then_inc(S["bias_step"], 1)
            v.wait_ge(S["bias_step"], 3)
            v.tensor_copy(BSH, BSF).then_inc(S["bias_step"], 1)
            v.wait_ge(S["bias_step"], 4)
            v.tensor_tensor(BSR, BSF, BSH, ALU.subtract).then_inc(S["bias_step"], 1)
            v.wait_ge(S["bias_step"], 5)
            v.tensor_scalar(BSR, BSR, EVEN[:, 1:2], None, ALU.mult).then_inc(S["bias_step"], 1)
            v.wait_ge(S["bias_step"], 6)
            v.scalar_tensor_tensor(BIAS[:, :], BSH, EVEN[:, 0:1], BSR, ALU.mult, ALU.add).then_inc(S["g_list"], 1)
            v.wait_ge(S["cnt_mm"], 2)
            v.tensor_copy(LROW[0:1, :], TM[0:1, 1, :]).then_inc(S["list_ready"], 1)
            v.tensor_scalar(TBF[:, :], TM[:, 1, 256:512], float(TT), None, ALU.mult).then_inc(S["list_ready"], 1)
            hold(v, S["list_ready"], 2)
            v.sem_inc(S["list_ready"], 1)

            with v.Fori(2, NG - 2) as g:
                first_norms(g)
            first_norms(NG - 2, False)
            first_norms(NG - 1, False, False)
            hold(v, S["z_init"], NT)

            def one_hot(n, u):
                hold(v, idx_loaded[u], 16 * n + 16)
                v.tensor_scalar(LOC[:, u, :], IDXR[:, u, :].rearrange("p (c w) -> p w c", w=2)[:, 1, :],
                                TBF[:, ds(n * RING + u, 1)], None, ALU.subtract).then_inc(S["oh_loc"], 1)
                v.wait_ge(S["agg_mm"], n * RING + u + 1)
                v.wait_ge(S["oh_loc"], (n + 1) * RING + u + 1)
                for c in range(EC):
                    last = v.tensor_scalar(OH[:, u, c, :], IOTA[:, :], LOC[:, u, c:c + 1], None, ALU.is_equal)
                last.then_inc(S["oh_done"], 1)

            def sums(n, u):
                tile = v.value_load(LROW[0:1, ds(256 + (n * RING + u), 1)], min_val=0, max_val=NT)
                z = Z[:, ds(tile * D, D)]
                v.wait_ge(S["agg_mm"], (n + 1) * RING + u + 1)
                v.wait_ge(S["agg_add"], n * RING + u + 1)
                v.tensor_tensor(z, TM[:TT, u % 2, :D], z, ALU.add).then_inc(S["agg_add"], 1)

            def q_lo(g, n, pairs=(0, 1, 2)):
                for i in pairs:
                    off, w = PAIRS[i]
                    v.wait_ge(S["q_hi"], 3 * n + i + 1)
                    v.scalar_tensor_tensor(FT[:, 1, :, ds(g * GT + off, w)],
                                           PT[:, i % 2, 0:500].rearrange("p (c w) -> p c w", c=KC)[:, :, :w], W_UP,
                                           FT[:, 0, :, ds(g * GT + off, w)], ALU.mult, ALU.subtract)\
                        .then_inc(S["q_lo"], 1)

            def kt_lo(n, m):
                v.wait_ge(S["kt_hi"], KC * n + m + 1)
                v.scalar_tensor_tensor(KT[:, 1, m, :, :], KTP[m], K_UP, KT[:, 0, m, :, :], ALU.mult, ALU.subtract)\
                    .then_inc(S["kt_lo"], 1)

            def ctx_add(n):
                for m in range(KC):
                    v.wait_ge(S["ctx_mm"], KC * n + m + 3)
                    v.wait_ge(S["ctx_scl"], KC * n + m + 1)
                    v.tensor_tensor(CTXA[:, m, :], PT[:, m, :P], CTXA[:, m, :], ALU.add).then_inc(S["ctx_acc"], 1)

            def phase_a(l, g, n, with_q):
                for m in range(KC):
                    for p, (off, w) in enumerate(PARTS):
                        v.wait_ge(S["k_mm"], 4 * n + 2 * m + p + 1)
                        v.tensor_reduce(KMX[:, m, p:p + 1], FFP[:, 2 * m + p, :w], AX, ALU.max).then_inc(S["k_max"], 1)
                v.wait_ge(S["ctx_zero"], 3 * l + 3)
                v.wait_ge(S["k_max"], 8 * n + 4)
                v.tensor_reduce(KM[:, :], KMX[:, :, :], AX, ALU.max).then_inc(S["k_max"], 1)
                v.wait_ge(S["k_max"], 8 * n + 5)
                v.tensor_tensor(KDIF[:, :], KMX[:, :, 2], KM[:, :], ALU.subtract).then_inc(S["k_max"], 1)
                v.tensor_scalar(NKB[:, :], KM[:, :], -SCALE / W_UP, None, ALU.mult).then_inc(S["k_max"], 1)
                v.wait_ge(S["k_max"], 8 * n + 6)
                v.tensor_copy(KMX[:, :, 2], KM[:, :]).then_inc(S["k_max"], 1)
                if with_q:
                    ctx_add(n - 1)
                v.wait_ge(S["fac"], n + 1)
                for m in range(KC):
                    v.wait_ge(S["ctx_acc"], KC * n + m + 1)
                    v.tensor_scalar(CTXA[:, m, :], CTXA[:, m, :], FAC[:, m:m + 1], None, ALU.mult).then_inc(S["ctx_scl"], 1)
                v.wait_ge(S["k_sum"], 2 * n + 1)
                v.tensor_tensor(KSG[:, :, 2], KS[:, :], FAC[:, :], ALU.mult).then_inc(S["k_sum"], 1)

                def qv(j):
                    if j == 0:
                        v.wait_ge(S["q_norm"], n * TG + 1)
                    q = TM[:TT, j % 2, 0:D].rearrange("p (h c) -> p h c", h=HEADS)
                    v.wait_ge(S["v_hi"], n * TG + j + 1)
                    v.tensor_reduce(QMX[:, j, :], q, AX, ALU.max).then_inc(S["q_max"], 1)
                    v.tensor_tensor(V[:, 1, j * D:(j + 1) * D], TM[:TT, j % 2, D:2 * D], V[:, 0, j * D:(j + 1) * D],
                                    ALU.subtract)
                    v.wait_ge(S["q_max"], n * TG + j + 1)
                    v.tensor_tensor(QS[:, j, :].rearrange("p (h c) -> p h c", h=HEADS), q,
                                    QMX[:, j, :].unsqueeze(2).to_broadcast([TT, HEADS, DH]), ALU.subtract)\
                        .then_inc(S["qv_evac"], 1)

                def q_sum(i):
                    j0, j1 = ((0, 3), (3, TG))[i]
                    v.wait_ge(S["q_exp"], n * TG + j1)
                    v.tensor_reduce(QSUM[:, j0:j1, :].rearrange("p j h -> p (j h)"),
                                    QS[:, j0:j1, :].rearrange("p j (h c) -> p (j h) c", h=HEADS),
                                    AX, ALU.add).then_inc(S["q_sum"], 1)
                    v.wait_ge(S["q_sum"], 2 * n + i + 1)
                    v.reciprocal(RINV[:, j0:j1, :], QSUM[:, j0:j1, :]).then_inc(S["q_rinv"], 1)

                def early(pairs):
                    if with_q:
                        q_lo(g - 1, n - 1, pairs)
                    else:
                        ln_lo(U1, n + NG - 1, NG - 1, pairs)

                qv(0)
                if with_q:
                    early((0, 1))
                qv(1)
                if not with_q:
                    early((0, 1))
                if with_q:
                    early((2,))
                kt_lo(n, 0)
                qv(2)
                if not with_q:
                    early((2,))
                kt_lo(n, 1)
                qv(3)
                q_sum(0)
                v.wait_ge(S["ke"], 4 * n + 4)
                v.wait_ge(S["k_sum"], 2 * n + 2)
                v.tensor_reduce(KS[:, :], KSG[:, :, :], AX, ALU.add).then_inc(S["k_sum"], 1)
                qv(4)
                q_sum(1)

            A_S, F_S = 1 / (W_UP * W_UP), 1 / W_UP

            def residual(n, g, done, scale, evac, j):
                x = X[:, ds(g * (TG * D) + j * D, D)]
                v.wait_ge(done, n * TG + j + 1)
                v.scalar_tensor_tensor(x, TM[:TT, j % 2, :D], scale, x, ALU.mult, ALU.add).then_inc(evac, 1)

            def tile_stats(U, u, g, evac, n, j):
                hold(v, evac, n * TG + j + 2)
                v.bn_stats(U.ST[:, j, :], X[:, ds(g * (TG * D) + j * D, D)]).then_inc(U.stats, 1)

            def moments(U, u):
                hold(v, U.stats, u * TG + TG)
                for j in range(TG):
                    v.bn_aggr(U.MV[:, j, :], U.ST[:, j, :]).then_inc(U.moments, 1)

            def normalise(U, u, g, H):
                v.wait_ge(U.turned, 3 * u + 1)
                norm(U, u, lambda j: X[:, ds(g * (TG * D) + j * D, D)], lambda j: H[:, j, :])

            def gelu_lo(n, m):
                for p, (off, w) in enumerate(PARTS):
                    v.wait_ge(S["g_hi"], 32 * n + 2 * (2 * m + p) + 2)
                    v.tensor_tensor(HID[:, 1, m, off:off + w], FFP[:, 2 * (m % 2) + p, :w],
                                    HID[:, 0, m, off:off + w], ALU.subtract).then_inc(S["g_lo"], 1)

            def step(g, n, before, after, first=False):
                ao = lambda j: residual(n + 1, g + 1, S["ao_mm"], A_S, S["ao_evac"], j)
                st2 = lambda j: tile_stats(U2, n + 1, g + 1, S["ao_evac"], n + 1, j)
                out = lambda j: residual(n, g, S["f2_mm"], F_S, S["f2_evac"], j)
                st1 = lambda j: tile_stats(U1, n + NG, g, S["f2_evac"], n, j)
                lo1 = lambda i: ln_lo(U1, n + NG - 1, g - 1, (i,)) if before else None
                lo2 = lambda i: ln_lo(U2, n + 1, g + 1, (i,)) if after else None
                for m in range(FC):
                    gelu_lo(n, m)
                    if m == 0 and before:
                        normalise(U1, n + NG - 1, g - 1, H1)
                    if 1 <= m <= RING:
                        sums(n, m - 1)
                    if first and EXTRA + 1 + m < RING:
                        one_hot(n, EXTRA + 1 + m)
                    if 3 <= m <= 5 and after:
                        one_hot(n + 1, m - 3)
                if after:
                    ao(0)
                    ao(1)
                    lo1(0)
                    ao(2)
                    st2(0)
                    st2(1)
                    ao(3)
                    st2(2)
                    ao(4)
                    lo1(1)
                    st2(3)
                    st2(4)
                    moments(U2, n + 1)
                else:
                    lo1(0)
                    lo1(1)
                lo1(2)
                out(0)
                if after:
                    normalise(U2, n + 1, g + 1, H2)
                    one_hot(n + 1, 3)
                out(1)
                st1(0)
                if after:
                    one_hot(n + 1, 4)
                out(2)
                st1(1)
                lo2(0)
                lo2(1)
                if after:
                    one_hot(n + 1, 5)
                out(3)
                st1(2)
                lo2(2)
                out(4)
                st1(3)
                st1(4)
                moments(U1, n + NG)

            for u in range(EXTRA):
                one_hot(0, u)
            with v.Fori(0, L) as l:
                n0 = l * NG
                v.memset(CTXA[:, :, :], 0.0).then_inc(S["ctx_zero"], 1)
                v.memset(KS[:, :], 0.0).then_inc(S["ctx_zero"], 1)
                v.memset(KMX[:, :, 2], -1e30).then_inc(S["ctx_zero"], 1)
                phase_a(l, 0, n0, False)
                with v.Fori(1, NG) as g:
                    phase_a(l, g, l * NG + g, True)
                ctx_add(n0 + NG - 1)
                v.wait_ge(S["k_sum"], 2 * (n0 + NG) + 1)
                v.reciprocal(RKS[:, :], KS[:, :]).then_inc(S["m_lo"], 1)
                v.wait_ge(S["ctx_turned"], l + 1)
                ctx_t = FFP[:, 1, 0:KC * P].rearrange("p (c n) -> p c n", c=KC)
                heads = MASK[:, :].unsqueeze(1).to_broadcast([P, KC, P])
                v.scalar_tensor_tensor(CTX[:, 0, :, :], ctx_t, C_DOWN, heads, ALU.mult, ALU.mult).then_inc(S["ctx_lo"], 1)
                v.scalar_tensor_tensor(CTXM[:, :, :], ctx_t, C_DOWN, heads, ALU.mult, ALU.mult).then_inc(S["ctx_lo"], 1)
                v.wait_ge(S["ctx_lo"], 3 * l + 2)
                v.tensor_tensor(CTX[:, 1, :, :], CTXM[:, :, :], CTX[:, 0, :, :], ALU.subtract).then_inc(S["ctx_lo"], 1)
                q_lo(NG - 1, n0 + NG - 1)
                for m in range(KC):
                    v.wait_ge(S["m_hi"], KC * l + KC)
                    v.scalar_tensor_tensor(M[:, 1, m, :], FFP[:, 0, m * D:(m + 1) * D], RKS[:, m:m + 1],
                                           M[:, 0, m, :], ALU.mult, ALU.subtract).then_inc(S["m_lo"], 1)
                for j in range(TG + 1):
                    if j < TG:
                        residual(n0, 0, S["ao_mm"], A_S, S["ao_evac"], j)
                    if j >= 1:
                        tile_stats(U2, n0, 0, S["ao_evac"], n0, j - 1)
                moments(U2, n0)
                one_hot(n0, EXTRA)
                normalise(U2, n0, 0, H2)
                ln_lo(U2, n0, 0)
                step(0, n0, False, True, True)
                with v.Fori(1, NG - 1) as g:
                    step(g, l * NG + g, True, True)
                n4 = n0 + NG - 1
                step(NG - 1, n4, True, False)
                for u in range(EXTRA):
                    one_hot(n0 + NG, u)
                normalise(U1, n4 + NG, NG - 1, H1)

            v.wait_ge(U1.h, (L + 1) * NT)
            hold(v, S["agg_add"], L * NG * RING + 1)

            def z_copy(g):
                v.wait_ge(S["z_turned"], 3 * g + 1)
                v.tensor_copy(H1[:, :, :], Z[:, ds(g * (TG * D), TG * D)].rearrange("p (j d) -> p j d", j=TG)).then_inc(S["zs"], 1)

            def gnn1(g, u, last):
                if not last:
                    z_copy(g + 1)
                for m in range(GC):
                    for p, (off, w) in enumerate(PARTS):
                        hold(v, S["t_evac"], 8 * g + 2 * m + p + 5)
                        v.bn_stats(BST[:, m, ds(g * 12 + p * 6, 6)], TH[:, m, ds(g * GT + off, w)]).then_inc(S["t_stat"], 1)

            def th_lo(g, u):
                for m in range(GC):
                    v.wait_ge(S["th_hi"], g * GC + m + 1)
                    v.wait_ge(S["th_relu"], g * GC + m + 1)
                    v.tensor_tensor(HID[:, 1, GC * u + m, :], TH[:, m, ds(g * GT, GT)], HID[:, 0, GC * u + m, :],
                                    ALU.subtract).then_inc(S["th_lo"], 1)

            def gnn2(g, u, last):
                if not last:
                    th_lo(g + 1, 1 - u)
                for m in range(KC):
                    for p, (off, w) in enumerate(PARTS):
                        hold(v, S["y_evac"], 4 * g + 2 * m + p + 5)
                        v.bn_stats(BST[:, m, ds(g * 12 + p * 6, 6)], Y[:, m, ds(g * GT + off, w)]).then_inc(S["y_stat"], 1)
                v.sem_inc(S["xhl_used"], 1)

            for u in range(EXTRA):
                sums(L * NG, u)
            hold(v, S["agg_add"], UNITS + 1)
            by_twos(v, gnn1)
            v.wait_ge(S["t_stat"], NG * GC * 2)
            for m in range(GC):
                v.bn_aggr(BMV[:, m, :], BST[:, m, :]).then_inc(S["bn_mv"], 1)
            hold(v, S["bn_b"], 1)
            v.sem_inc(S["xhl_used"], 2)
            th_lo(0, 0)
            by_twos(v, gnn2)
            v.wait_ge(S["y_stat"], NG * KC * 2)
            for m in range(KC):
                v.bn_aggr(BMV[:, m, :], BST[:, m, :]).then_inc(S["bn_mv"], 1)
            hold(v, S["bn_mv"], GC + KC)

            def residual_gnn(g):
                for j in range(TG):
                    x = X[:, ds(g * (TG * D) + j * D, D)]
                    v.wait_ge(S["r_turned"], g * TG + j + 2)
                    v.tensor_tensor(x, TM[:TT, j % 2, :D], x, ALU.add).then_inc(S["x1"], 1)

            def tokens_lo(g, pairs):
                for i in pairs:
                    off, w = PAIRS[i]
                    v.wait_ge(U3.hi, 3 * g + i + 1)
                    v.tensor_tensor(FT[:, 1, :, ds(g * GT + off, w)],
                                    PT[:, i % 2, 0:500].rearrange("p (c w) -> p c w", c=KC)[:, :, :w],
                                    FT[:, 0, :, ds(g * GT + off, w)], ALU.subtract).then_inc(U3.lo, 1)

            def mw_lo(g):
                v.wait_ge(S["mw_split"], g + 1)
                v.scalar_tensor_tensor(MW[:, 1, ds(g * MWS, MWS)], STM, W_UP, MW[:, 0, ds(g * MWS, MWS)], ALU.mult,
                                       ALU.subtract).then_inc(S["mw_used"], 1)

            def logits(g):
                v.wait_ge(S["log_mm"], g + 1)
                v.tensor_scalar(LG[:, ds(g * TG, TG), :].rearrange("p t e -> p (t e)"), FFP[:TT, 0, 0:TG * E],
                                1 / W_UP, None, ALU.mult).then_inc(S["log"], 1)

            def last_norm(g, before, following, after_that):
                v.wait_ge(U3.turned, 3 * g + 1)
                v.wait_ge(S["x_tok"], g + 1)
                norm(U3, g, tile_of(g), lambda j: H1[:, j, :])
                if following:
                    hold(v, S["x1"], (g + 2) * TG + 1)
                    stats(U3, g + 1, tile_of(g + 1))
                tokens_lo(g, (0, 1))
                if after_that:
                    residual_gnn(g + 2)
                if before:
                    logits(g - 1)
                tokens_lo(g, (2,))
                if following:
                    mw_lo(g + 1)

            v.wait_ge(S["x_plus"], NG)
            residual_gnn(0)
            hold(v, S["x1"], TG + 1)
            stats(U3, 0, tile_of(0))
            mw_lo(0)
            residual_gnn(1)
            last_norm(0, False, True, True)
            with v.Fori(1, NG - 2) as g:
                last_norm(g, True, True, True)
            last_norm(NG - 2, True, True, False)
            last_norm(NG - 1, True, False, False)
            logits(NG - 1)
            wide = lambda k: RT[:, k, :, :]
            per = lambda k: RM[:, k, :].unsqueeze(2).to_broadcast([TT, NT, E])
            r8 = R8[:, :].unsqueeze(1).to_broadcast([TT, NT, E])
            v.wait_ge(S["log"], NG + 1)
            v.tensor_reduce(RM[:, 0, :], LG[:, :, :], AX, ALU.max).then_inc(S["rt"], 1)
            v.wait_ge(S["rt"], 1)
            v.tensor_tensor(wide(0), LG[:, :, :], per(0), ALU.subtract).then_inc(S["rt"], 1)
            v.wait_ge(S["rt"], 3)
            v.tensor_reduce(RM[:, 1, :], wide(1), AX, ALU.add).then_inc(S["rt"], 1)
            v.wait_ge(S["rt"], 4)
            v.reciprocal(RM[:, 2, :], RM[:, 1, :]).then_inc(S["rt"], 1)
            v.wait_ge(S["rt"], 5)
            v.tensor_tensor(wide(2), wide(1), per(2), ALU.mult).then_inc(S["rt"], 1)
            n = 6
            src = 2
            for k in range(2):
                v.wait_ge(S["rt"], n)
                v.tensor_reduce(RM[:, 3 + k, :], wide(src), AX, ALU.max).then_inc(S["rt"], 1)
                v.wait_ge(S["rt"], n + 1)
                v.tensor_tensor(wide(3), wide(src), per(3 + k), ALU.is_equal).then_inc(S["rt"], 1)
                v.wait_ge(S["rt"], n + 2)
                v.tensor_tensor(wide(4), wide(3), r8, ALU.mult).then_inc(S["rt"], 1)
                v.wait_ge(S["rt"], n + 3)
                v.tensor_reduce(RM[:, 5, :], wide(4), AX, ALU.max).then_inc(S["rt"], 1)
                v.wait_ge(S["rt"], n + 4)
                v.tensor_tensor(wide(5 + k), wide(4), per(5), ALU.is_equal).then_inc(S["rt"], 1)
                n += 5
                if k == 0:
                    v.wait_ge(S["rt"], n)
                    v.scalar_tensor_tensor(wide(7), wide(5), -2.0, wide(2), ALU.mult, ALU.add).then_inc(S["rt"], 1)
                    n += 1
                    src = 7
            v.wait_ge(S["rt"], n)
            v.tensor_tensor(RM[:, 0, :], RM[:, 3, :], RM[:, 4, :], ALU.add).then_inc(S["rt"], 1)
            v.tensor_tensor(wide(0), wide(5), wide(6), ALU.add).then_inc(S["rt"], 1)
            v.wait_ge(S["rt"], n + 2)
            v.tensor_scalar(RM[:, 1, :], RM[:, 0, :], 1e-12, None, ALU.max).then_inc(S["rt"], 1)
            v.tensor_tensor(wide(1), wide(0), wide(2), ALU.mult).then_inc(S["rt"], 1)
            v.wait_ge(S["rt"], n + 4)
            v.reciprocal(RM[:, 2, :], RM[:, 1, :]).then_inc(S["rt"], 1)
            v.wait_ge(S["rt"], n + 5)
            v.tensor_tensor(wide(3), wide(1), per(2), ALU.mult).then_inc(S["rt"], 1)
            v.wait_ge(S["rt"], n + 6)
            v.tensor_scalar(CB[:, :, :], wide(3), 1 / W_UP, None, ALU.mult).then_inc(S["comb"], 1)
            hold(v, S["comb"], 1)

            def combine_tile(g):
                v.wait_ge(S["ct"], 2 * g + 1)
                v.tensor_copy(CBG, RT[:, 3, ds(g * TG, TG), :].rearrange("p t e -> p (t e)")).then_inc(S["cbg"], 1)

            def expert_lo(g, e, q, m, p):
                off, w = PARTS[p]
                v.wait_ge(S["eg_hi"], 8 * (g * E + e) + 4 * m + 2 * p + 2)
                v.tensor_tensor(HID[:, 1, 2 * q + m, off:off + w], FFP[:, 2 * m + p, :w],
                                HID[:, 0, 2 * q + m, off:off + w], ALU.subtract).then_inc(S["eg_lo"], 1)

            def expert_out(g, e, j):
                x = g * E + e
                xt_ = X[:, ds(g * (TG * D) + j * D, D)]
                v.wait_ge(S["e2_mm"], x * TG + j + 1)
                v.wait_ge(S["e_out"], x * TG + 1)
                v.scalar_tensor_tensor(xt_, TM[:TT, j % 2, :D],
                                       CB[:, :, :].rearrange("p t e -> p (t e)")[:, ds(g * (TG * E) + e + j * E, 1)],
                                       xt_, ALU.mult, ALU.add).then_inc(S["e_out"], 1)

            def expert_step(g, e, following, q):
                lo = lambda m, p: expert_lo(*following, q, m, p) if following else None
                lo(0, 0)
                expert_out(g, e, 0)
                lo(0, 1)
                expert_out(g, e, 1)
                expert_out(g, e, 2)
                lo(1, 0)
                lo(1, 1)
                expert_out(g, e, 3)
                expert_out(g, e, 4)

            def combine_add(g, tiles):
                for j in tiles:
                    x = X[:, ds(g * (TG * D) + j * D, D)]
                    if j == 0:
                        v.wait_ge(S["x_tok"], g + 2)
                    v.wait_ge(S["cb_mm"], g * TG + j + 2)
                    v.tensor_tensor(x, TM[:TT, j % 2, :D], x, ALU.add).then_inc(S["cb_add"], 1)

            def expert_group(g, last):
                combine_add(g, (0, 1))
                expert_lo(g, 1, 1, 0, 0)
                combine_add(g, (2,))
                expert_lo(g, 1, 1, 0, 1)
                combine_add(g, (3, 4))
                v.wait_ge(S["cb_add"], (g + 1) * TG + 1)
                expert_lo(g, 1, 1, 1, 0)
                expert_lo(g, 1, 1, 1, 1)
                for j in range(TG):
                    expert_out(g, 0, j)
                expert_step(g, 1, (g, 2), 0)
                with v.Fori(1, E // 2 - 1) as h:
                    expert_step(g, h * 2, (g, h * 2 + 1), 1)
                    expert_step(g, h * 2 + 1, (g, h * 2 + 2), 0)
                if not last:
                    combine_tile(g + 1)
                expert_step(g, E - 2, (g, E - 1), 1)
                expert_step(g, E - 1, None if last else (g + 1, 0), 0)

            combine_tile(0)
            for m in range(KC):
                for p in range(2):
                    expert_lo(0, 0, 0, m, p)
            with v.Fori(0, NG - 1) as g:
                expert_group(g, False)
            expert_group(NG - 1, True)


def kernel(**inputs):
    import numpy as np
    import concourse.bacc as bacc
    from concourse.bass_utils import run_bass_kernel_spmd

    i = {k: np.asarray(v) for k, v in inputs.items()}

    def cols(w):
        w = w.reshape(*w.shape[:-2], w.shape[-2] // P, P, w.shape[-1])
        w = np.moveaxis(w, -3, -2)
        return w.reshape(*w.shape[:-2], -1)

    def pad(w, n):
        return np.concatenate([w, np.zeros((*w.shape[:-1], n - w.shape[-1]), w.dtype)], -1)

    wa = pad(np.concatenate([cols(np.concatenate([i["L0_mix_Wq"], i["L0_mix_Wv"]], -1)), cols(i["L0_mix_Wk"]),
                             cols(i["L0_mix_Wo"])], -1), WA)
    wa = np.concatenate([wa, pad(cols(i["L0_gnn_W2"]), WA)[None]], 0)
    wb = pad(np.concatenate([cols(i["L0_mix_W1"]), cols(i["L0_mix_W2"])], -1), WB)

    def vec(b):
        return np.swapaxes(b.reshape(*b.shape[:-1], -1, P), -1, -2)

    g1, b1 = vec(i["L0_mix_ln1_g"]), vec(i["L0_mix_ln1_b"])
    nxt = lambda t: np.concatenate([t[1:], np.zeros_like(t[:1])], 0)
    prm = np.concatenate([nxt(g1), nxt(b1), vec(i["L0_mix_ln2_g"]), vec(i["L0_mix_ln2_b"]), vec(i["L0_mix_b1"]), g1, b1], -1)
    data = {
        "x": i["x"],
        "prm0": np.concatenate([g1[0], b1[0]], -1),
        "prm": prm,
        "bias": np.repeat(np.concatenate([i["L0_mix_bo"], i["L0_mix_b2"]], -1), 2, axis=0),
        "eps": i["L0_gnn_eps_gin"].reshape(1, 1),
        "wa": wa.reshape(L + 1, P, NG, WAS),
        "wb": wb.reshape(L, P, NG, WBS),
        "dst": i["dst"].reshape(TT, ER),
        "edges": np.concatenate([np.stack([i["src"], i["dst"]], -1), np.tile(np.array([[0, -1]], i["src"].dtype), (EG, 1))], 0),
        "gw1": cols(i["L0_gnn_W1"]),
        "gprm": np.concatenate([vec(i["L0_gnn_" + k]) for k in ("b1", "g1", "bt1", "b2", "g2", "bt2")], -1),
        "rw": cols(i["L0_ffn_router_w"].T),
        "eb1": np.moveaxis(vec(i["L0_ffn_b1"]), 1, 0).reshape(P, -1), "eb2": i["L0_ffn_b2"],
        "mw": pad(np.moveaxis(np.concatenate([cols(i["L0_ffn_w1"]), cols(i["L0_ffn_w2"])], -1), 1, 0).reshape(P, -1), MWC)
        .reshape(P, NG, -1),
    }
    data = {k: np.ascontiguousarray(w) for k, w in data.items()}
    nc = bacc.Bacc("TRN2", target_bir_lowering=False, num_devices=1)
    aps = {k: nc.dram_tensor(f"in_{k}", w.shape, mybir.dt.from_np(w.dtype), kind="ExternalInput").ap()
           for k, w in data.items()}
    aps["xn_hl"] = nc.dram_tensor("xn_hl", [N, 2 * D], F16).ap()
    aps["out"] = nc.dram_tensor("out_0", [N, D], F32, kind="ExternalOutput").ap()
    build(nc, aps)
    r = run_bass_kernel_spmd(nc, [{f"in_{k}": w for k, w in data.items()}], core_ids=[0])
    return r.results[0]["out_0"]
```
